# Optimizing a Trainium2 kernel written in Bass

```python
import numpy as np
import jax
import jax.numpy as jnp

def _softmax(x, axis=-1):
    return jax.nn.softmax(x, axis=axis)

def _gelu(x):
    return jax.nn.gelu(x, approximate=True)

def _silu(x):
    return jax.nn.silu(x)

def _sigmoid(x):
    return jax.nn.sigmoid(x)

def _layernorm(x, axis=-1, eps=1e-05):
    m = jnp.mean(x, axis=axis, keepdims=True)
    v = jnp.var(x, axis=axis, keepdims=True)
    return (x - m) / jnp.sqrt(v + eps)

def _scatter_add(tgt, idx, src, axis=0):
    return tgt.at[idx].add(src)

def _segment_sum(src, seg, n):
    return jax.ops.segment_sum(src, seg, n)
kernel_name = 'mk_adj_preln_d4_adj_r2_29eb0b'

def setup_inputs(seed: int=0):
    np.random.seed(seed)
    _w = jnp.asarray

    def _rec_inputs():
        import jax
        import jax.numpy as jnp
        _gk = jax.random.key(seed)
        x = -0.000125 + 0.9999 * jax.random.normal(jax.random.fold_in(_gk, 1), (16, 512, 128), jnp.float32)
        _w = (1.0 + jnp.arange(512, dtype=jnp.float32)) ** (-0.5)
        _w = _w / _w.mean()
        _pij = jnp.clip(0.015625 * _w[:, None] * _w[None, :], 0.0, 1.0)
        _a = jax.random.uniform(jax.random.fold_in(_gk, 2), (512, 512)) < _pij
        _a = jnp.logical_or(_a, jnp.swapaxes(_a, -1, -2))
        _a = jnp.logical_or(_a, jnp.eye(512, dtype=bool))
        _af = _a.astype(jnp.float32)
        _af = _af * jax.random.uniform(jax.random.fold_in(_gk, 3), (512, 512), jnp.float32, 0.05, 0.000488281)
        adj = _af
        return (x, adj)
    x, adj = _rec_inputs()

    def _L0_gnn_setup():
        import jax, jax.numpy as jnp
        import numpy as np
        B, T, D, H = (64, 1024, 128, 128)
        MAX_SKIP = 4

        def _lstm_last(Wih, Whh, bih, bhh, xs):
            N, _, Hd = xs.shape
            bias = bih + bhh

            def step(carry, x_t):
                h, c = carry
                g = x_t @ Wih.T + h @ Whh.T + bias
                i, f, gg, o = jnp.split(g, 4, axis=-1)
                c = jax.nn.sigmoid(f) * c + jax.nn.sigmoid(i) * jnp.tanh(gg)
                h = jax.nn.sigmoid(o) * jnp.tanh(c)
                return ((h, c), None)
            init = (jnp.zeros((N, Hd), xs.dtype), jnp.zeros((N, Hd), xs.dtype))
            (h_last, _), _ = jax.lax.scan(step, init, jnp.swapaxes(xs, 0, 1))
            return h_last
        key = jax.random.key(seed)
        ks = jax.random.split(key, 8)
        s = 0.05
        x = jax.random.normal(ks[0], (B, T, D), jnp.float32)
        adj = jax.random.uniform(ks[1], (T, T), jnp.float32) / T
        Wg0 = jax.random.normal(ks[2], (D, H), jnp.float32) * s
        bg0 = jnp.zeros((H,), jnp.float32)
        Wg1 = jax.random.normal(ks[3], (H, H), jnp.float32) * s
        bg1 = jnp.zeros((H,), jnp.float32)
        Wih = jax.random.normal(ks[4], (MAX_SKIP, 4 * H, H), jnp.float32) * s
        Whh = jax.random.normal(ks[5], (MAX_SKIP, 4 * H, H), jnp.float32) * s
        bih = jax.random.normal(ks[6], (MAX_SKIP, 4 * H), jnp.float32) * s
        bhh = jax.random.normal(ks[7], (MAX_SKIP, 4 * H), jnp.float32) * s
        return dict(x=x, adj=adj, Wg0=Wg0, bg0=bg0, Wg1=Wg1, bg1=bg1, Wih=Wih, Whh=Whh, bih=bih, bhh=bhh)
    _L0_gnn_all = _L0_gnn_setup()
    _L0_gnn_in = {k: v for k, v in _L0_gnn_all.items() if k in ('Wg0', 'bg0', 'Wg1', 'bg1', 'Wih', 'Whh', 'bih', 'bhh')}
    del _L0_gnn_all

    def _L1_gnn_setup():
        import jax, jax.numpy as jnp
        import numpy as np
        ALPHA = 0.2
        key = jax.random.key(seed)
        k1, k2, k3, k4 = jax.random.split(key, 4)
        B, N, Fin, Fout = (8, 1024, 128, 128)
        h = jax.random.normal(k1, (B, N, Fin), dtype=jnp.float32)
        adj = jax.random.randint(k2, (N, N), 0, 2).astype(jnp.float32)
        adj = jnp.maximum(adj, jnp.eye(N, dtype=jnp.float32))

        def xavier(k, shape, gain=1.414):
            fan_in, fan_out = (shape[0], shape[1])
            a = gain * np.sqrt(6.0 / (fan_in + fan_out))
            return jax.random.uniform(k, shape, dtype=jnp.float32, minval=-a, maxval=a)
        W = xavier(k3, (Fin, Fout))
        a = xavier(k4, (2 * Fout, 1))
        return {'h': h, 'adj_matrix': adj, 'W': W, 'a': a}
    _L1_gnn_all = _L1_gnn_setup()
    _L1_gnn_in = {k: v for k, v in _L1_gnn_all.items() if k in ('W', 'a')}
    del _L1_gnn_all

    def _L2_gnn_setup():
        import jax, jax.numpy as jnp
        import numpy as np
        EPS = 1e-05

        def _batchnorm(x, gamma, beta):
            mu = jnp.mean(x, axis=0)
            var = jnp.var(x, axis=0)
            return (x - mu) * jax.lax.rsqrt(var + EPS) * gamma + beta
        key = jax.random.key(seed)
        ks = jax.random.split(key, 4)
        b, n, d, h, o = (32, 1024, 128, 256, 128)
        features = jax.random.normal(ks[0], (b, n, d), dtype=jnp.float32)
        A = jax.random.uniform(ks[1], (n, n), dtype=jnp.float32)
        lim1 = float(np.sqrt(6.0 / (d + h)))
        W1 = jax.random.uniform(ks[2], (h, d), minval=-lim1, maxval=lim1, dtype=jnp.float32)
        b1 = jnp.zeros((h,), jnp.float32)
        lim2 = float(np.sqrt(6.0 / (h + o)))
        W2 = jax.random.uniform(ks[3], (o, h), minval=-lim2, maxval=lim2, dtype=jnp.float32)
        b2 = jnp.zeros((o,), jnp.float32)
        g1 = jnp.ones((h,), jnp.float32)
        be1 = jnp.zeros((h,), jnp.float32)
        g2 = jnp.ones((o,), jnp.float32)
        be2 = jnp.zeros((o,), jnp.float32)
        return {'features': features, 'A': A, 'W1': W1, 'b1': b1, 'g1': g1, 'be1': be1, 'W2': W2, 'b2': b2, 'g2': g2, 'be2': be2}
    _L2_gnn_all = _L2_gnn_setup()
    _L2_gnn_in = {k: v for k, v in _L2_gnn_all.items() if k in ('W1', 'b1', 'g1', 'be1', 'W2', 'b2', 'g2', 'be2')}
    del _L2_gnn_all

    def _L3_gnn_setup():
        import jax, jax.numpy as jnp
        import numpy as np
        NEG = -1e+30
        key = jax.random.key(seed)
        ks = jax.random.split(key, 4)
        B, T, C = (4, 2048, 128)
        x = jax.random.normal(ks[0], (B, T, C), dtype=jnp.float32)
        adj_mask = jax.random.normal(ks[1], (T, T), dtype=jnp.float32)
        Wqkv = jax.random.normal(ks[2], (C, 3 * C), dtype=jnp.float32) * (1.0 / np.sqrt(C))
        Wo = jax.random.normal(ks[3], (C, C), dtype=jnp.float32) * (1.0 / np.sqrt(C))
        return {'x': x, 'adj_mask': adj_mask, 'Wqkv': Wqkv, 'Wo': Wo}
    _L3_gnn_all = _L3_gnn_setup()
    _L3_gnn_in = {k: v for k, v in _L3_gnn_all.items() if k in ('Wqkv', 'Wo')}
    del _L3_gnn_all
    return {'x': x, 'adj': adj, 'L0_gnn_Wg0': _L0_gnn_in['Wg0'], 'L0_gnn_bg0': _L0_gnn_in['bg0'], 'L0_gnn_Wg1': _L0_gnn_in['Wg1'], 'L0_gnn_bg1': _L0_gnn_in['bg1'], 'L0_gnn_Wih': _L0_gnn_in['Wih'], 'L0_gnn_Whh': _L0_gnn_in['Whh'], 'L0_gnn_bih': _L0_gnn_in['bih'], 'L0_gnn_bhh': _L0_gnn_in['bhh'], 'L1_gnn_W': _L1_gnn_in['W'], 'L1_gnn_a': _L1_gnn_in['a'], 'L2_gnn_W1': _L2_gnn_in['W1'], 'L2_gnn_b1': _L2_gnn_in['b1'], 'L2_gnn_g1': _L2_gnn_in['g1'], 'L2_gnn_be1': _L2_gnn_in['be1'], 'L2_gnn_W2': _L2_gnn_in['W2'], 'L2_gnn_b2': _L2_gnn_in['b2'], 'L2_gnn_g2': _L2_gnn_in['g2'], 'L2_gnn_be2': _L2_gnn_in['be2'], 'L3_gnn_Wqkv': _L3_gnn_in['Wqkv'], 'L3_gnn_Wo': _L3_gnn_in['Wo']}

def reference(x, adj, L0_gnn_Wg0, L0_gnn_bg0, L0_gnn_Wg1, L0_gnn_bg1, L0_gnn_Wih, L0_gnn_Whh, L0_gnn_bih, L0_gnn_bhh, L1_gnn_W, L1_gnn_a, L2_gnn_W1, L2_gnn_b1, L2_gnn_g1, L2_gnn_be1, L2_gnn_W2, L2_gnn_b2, L2_gnn_g2, L2_gnn_be2, L3_gnn_Wqkv, L3_gnn_Wo):
    import jax
    import jax.numpy as jnp

    def _L0_gnn_ref(x, adj, Wg0, bg0, Wg1, bg1, Wih, Whh, bih, bhh):
        import jax, jax.numpy as jnp
        import numpy as np
        B, T, D, H = (64, 1024, 128, 128)
        MAX_SKIP = 4

        def _lstm_last(Wih, Whh, bih, bhh, xs):
            N, _, Hd = xs.shape
            bias = bih + bhh

            def step(carry, x_t):
                h, c = carry
                g = x_t @ Wih.T + h @ Whh.T + bias
                i, f, gg, o = jnp.split(g, 4, axis=-1)
                c = jax.nn.sigmoid(f) * c + jax.nn.sigmoid(i) * jnp.tanh(gg)
                h = jax.nn.sigmoid(o) * jnp.tanh(c)
                return ((h, c), None)
            init = (jnp.zeros((N, Hd), xs.dtype), jnp.zeros((N, Hd), xs.dtype))
            (h_last, _), _ = jax.lax.scan(step, init, jnp.swapaxes(xs, 0, 1))
            return h_last
        h = jax.nn.relu(jnp.einsum('ts,bsh->bth', adj, x @ Wg0 + bg0))
        h = jax.nn.relu(jnp.einsum('ts,bsh->bth', adj, h @ Wg1 + bg1))
        Bv, Tv, Hd = h.shape
        for p in range(1, MAX_SKIP + 1):
            nw = Tv // p
            wins = h[:, :nw * p, :].reshape(Bv * nw, p, Hd)
            last = _lstm_last(Wih[p - 1], Whh[p - 1], bih[p - 1], bhh[p - 1], wins)
            idx = jnp.arange(nw) * p + (p - 1)
            h = h.at[:, idx, :].set(last.reshape(Bv, nw, Hd))
        return h

    def _L1_gnn_ref(h, adj_matrix, W, a):
        import jax, jax.numpy as jnp
        import numpy as np
        ALPHA = 0.2
        Fout = W.shape[1]
        Wh = jnp.einsum('bnf,fo->bno', h, W)
        a1, a2 = (a[:Fout, 0], a[Fout:, 0])
        s1 = Wh @ a1
        s2 = Wh @ a2
        e = s1[:, :, None] + s2[:, None, :]
        e = jnp.where(e >= 0, e, ALPHA * e)
        e = jnp.where(adj_matrix[None] == 0, -jnp.inf, e)
        attention = jax.nn.softmax(e, axis=-1)
        h_prime = jnp.einsum('bij,bjo->bio', attention, Wh)
        return h_prime

    def _L2_gnn_ref(features, A, W1, b1, g1, be1, W2, b2, g2, be2):
        import jax, jax.numpy as jnp
        import numpy as np
        EPS = 1e-05

        def _batchnorm(x, gamma, beta):
            mu = jnp.mean(x, axis=0)
            var = jnp.var(x, axis=0)
            return (x - mu) * jax.lax.rsqrt(var + EPS) * gamma + beta
        b, n, d = features.shape
        A_norm = A + jnp.eye(n, dtype=A.dtype)
        deg = jnp.sum(A_norm, axis=0) + jnp.sum(A_norm, axis=1) - jnp.diagonal(A_norm)
        dinv = jax.lax.rsqrt(deg)
        A_hat = A_norm * dinv[:, None] * dinv[None, :]
        agg = jnp.einsum('nm,bmd->bnd', A_hat, features)
        x = agg.reshape(-1, d)
        h = jax.nn.relu(_batchnorm(x @ W1.T + b1, g1, be1))
        out = h @ W2.T + b2
        out = _batchnorm(out, g2, be2)
        return out.reshape(b, n, -1)

    def _L3_gnn_ref(x, adj_mask, Wqkv, Wo):
        import jax, jax.numpy as jnp
        import numpy as np
        NEG = -1e+30
        B, T, C = x.shape
        qkv = x @ Wqkv
        q, k, v = jnp.split(qkv, 3, axis=-1)
        scale = 1.0 / jnp.sqrt(jnp.asarray(C, dtype=x.dtype))
        scores = jnp.einsum('btd,bsd->bts', q, k) * scale + adj_mask
        causal = jnp.tril(jnp.ones((T, T), dtype=bool))
        scores = jnp.where(causal, scores, NEG)
        attn = jax.nn.softmax(scores, axis=-1)
        y = jnp.einsum('bts,bsd->btd', attn, v)
        return y @ Wo
    h = jnp.maximum(_layernorm(x, axis=-1), 0.0)
    x = x + _L0_gnn_ref(h, adj, L0_gnn_Wg0, L0_gnn_bg0, L0_gnn_Wg1, L0_gnn_bg1, L0_gnn_Wih, L0_gnn_Whh, L0_gnn_bih, L0_gnn_bhh)
    h = jnp.maximum(_layernorm(x, axis=-1), 0.0)
    x = x + _L1_gnn_ref(h, adj, L1_gnn_W, L1_gnn_a)
    h = jnp.maximum(_layernorm(x, axis=-1), 0.0)
    x = x + _L2_gnn_ref(h, adj, L2_gnn_W1, L2_gnn_b1, L2_gnn_g1, L2_gnn_be1, L2_gnn_W2, L2_gnn_b2, L2_gnn_g2, L2_gnn_be2)
    h = jnp.maximum(_layernorm(x, axis=-1), 0.0)
    x = x + _L3_gnn_ref(h, adj, L3_gnn_Wqkv, L3_gnn_Wo)
    return x

_drawn_inputs = setup_inputs


def setup_inputs(seed=0):
    import zlib

    import numpy as np

    out = dict(_drawn_inputs(seed))
    spreads = {'L0_gnn_bg0': (0.0, 0.8),
     'L0_gnn_bg1': (0.0, 0.8),
     'L2_gnn_b1': (0.0, 0.8),
     'L2_gnn_g1': (1.0, 0.2),
     'L2_gnn_be1': (0.0, 0.1),
     'L2_gnn_b2': (0.0, 0.8),
     'L2_gnn_g2': (1.0, 0.2),
     'L2_gnn_be2': (0.0, 0.1)}
    factors = {'L0_gnn_Wg0': 7.939, 'L0_gnn_Wg1': 5.536, 'L0_gnn_Wih': 3.55, 'L0_gnn_Whh': 8.0}
    for name, (base, spread) in spreads.items():
        noise = np.random.default_rng([zlib.crc32(name.encode()), seed]).standard_normal(out[name].shape)
        drawn = base * np.exp(spread * noise) if base else spread * noise
        out[name] = jnp.asarray(drawn.astype(out[name].dtype))
    for name, factor in factors.items():
        out[name] = (out[name] * factor).astype(out[name].dtype)
    return out
```

```python
from contextlib import ExitStack

import concourse.bass as bass
from concourse import mybir

F32 = mybir.dt.float32
F32R = mybir.dt.float32r
ALU = mybir.AluOpType
ACT = mybir.ActivationFunctionType

P = 128
NB, T, D = 16, 512, 128
CH = T // P
SKIP = 4
HALVES = 2
EPS = 1e-5
NEG = -1e30
SLOPE = 0.2

VECS = [("bih", 16), ("bg0", 1), ("b1", 2), ("g1", 2), ("be1", 2), ("b2", 1), ("g2", 1), ("be2", 1), ("a", 2)]
COL, _at = {}, 0
for _name, _n in VECS:
    COL[_name] = _at
    _at += _n
NVEC = _at
BHH_COL = 32


class Step:

    def __init__(self, j, slot):
        self.j, self.slot = j, slot

    def has(self, lag):
        return not isinstance(self.j, int) or 0 <= self.j - lag < NB

    def b(self, lag):
        return self.j - lag

    def ring(self, lag, n):
        return (self.slot - lag) % n

    def from_(self, lag, n):
        return not isinstance(self.j, int) or self.j - lag >= n


def pipeline(eng, start, unroll, lags, step):
    for j in range(start):
        step(Step(j, j))
    with eng.Fori(0, (NB - start) // unroll) as i:
        for k in range(unroll):
            step(Step(i * unroll + (start + k), start + k))
    for j in range(NB, NB + lags):
        step(Step(j, j))


def program(nc, x, adj, Wg0, bg0, Wg1, bg1, Wih, Whh, bih, bhh, gat_W, gat_a,
            W1, b1, g1, be1, W2, b2, g2, be2, Wqkv, Wo, out):
    ctx = ExitStack()
    with ctx:
        def sb(name, shape, dt=F32):
            return ctx.enter_context(nc.sbuf_tensor(name, shape, dt))

        def sem(name):
            return ctx.enter_context(nc.semaphore(name))

        bank = [ctx.enter_context(nc.psum_tensor(f"bank{i}", [P, 512], F32)) for i in range(8)]

        X = sb("x_stream", [P, NB, CH, D])
        A = sb("adj_rows", [P, CH, T])
        Ath = sb("adjT_hi", [P, CH, T], F32R)
        Atl = sb("adjT_lo", [P, CH, T], F32R)
        Ch = sb("col_hi", [P, NB, T], F32R)
        Cl = sb("col_lo", [P, NB, T], F32R)
        ident = sb("ident", [P, P])
        ones = sb("ones", [P, P])
        ones_r = sb("ones_r", [P, P], F32R)
        bg1_row = sb("bg1_row", [1, P])
        V = sb("vec_cols", [P, 48])
        lstm_bias = sb("lstm_bias", [P, SKIP, 4])
        gcn_wh = sb("gcn_wh", [P, 2, P], F32R)
        gcn_wl = sb("gcn_wl", [P, 2, P], F32R)
        gat_w = sb("gat_w", [P, P])
        bn_wh = sb("bn_wh", [P, 4, P], F32R)
        bn_wl = sb("bn_wl", [P, 4, P], F32R)
        wo32 = sb("wo32", [P, P])
        gat_v = sb("gat_v", [P, 2])
        gat_v2 = sb("gat_v2", [P, P])
        w_qk = sb("w_qk", [P, P])
        w_vo = sb("w_vo", [P, P])
        bg1_all = sb("bg1_all", [P, P])
        deg = sb("deg", [P, CH])
        dinv = sb("dinv", [P, CH])
        stats = sb("ln_stats", [P, 2, CH, 6])
        rstd = sb("ln_rstd", [P, 2, CH])
        nbias = sb("ln_bias", [P, 2, CH])
        pad = sb("pad", [1, 32])
        neg_half, d_eps = sb("neg_half", [P, CH]), sb("d_eps", [P, CH])
        quarter_d, sqrt_d = sb("quarter_d", [P, CH]), sb("sqrt_d", [P, CH])
        ln_d, ln_s, ln_q, ln_dd = (sb(f"ln_{k}", [P, CH]) for k in ("diff", "sum", "vars", "diff2"))
        ln_m, ln_qe, ln_dq, ln_v, ln_p = (sb(f"ln_{k}", [P, CH]) for k in ("mean", "vars_eps", "quarter", "dvar", "root"))
        s1 = sb("gat_s1", [P, CH])
        s1x = sb("gat_s1x", [P, CH])
        top = sb("row_top", [P, CH])
        e_top = sb("gat_e_top", [P, CH])
        l_top = sb("gat_l_top", [P, CH])
        soft_b = sb("soft_bias", [P, 2, CH])
        den = sb("soft_den", [P, 2, CH])
        rden = sb("soft_rden", [P, CH])
        bst1 = sb("bn1_stats", [P, HALVES, NB, 6])
        bst2 = sb("bn2_stats", [P, NB, 6])
        bmv = sb("bn_mean_var", [P, 3, 2])
        bve = sb("bn_var_eps", [P, 3])
        brs = sb("bn_rstd", [P, 3])
        bsc = sb("bn_scale", [P, 3])
        bmb = sb("bn_mean_b", [P, 3])
        bsh = sb("bn_shift", [P, 3])
        bms = sb("bn_shift_scaled", [P, 3])
        bbi = sb("bn_bias", [P, 3])

        SR = sb("scratch_r", [P, 8192], F32R)
        SF = sb("scratch_f", [P, 9728])

        def carve(t, at, *dims):
            n = 1
            for d in dims:
                n *= d
            v = t[:, at:at + n]
            names = "abcd"[:len(dims)]
            if len(dims) > 1:
                v = v.rearrange(f"p ({' '.join(names)}) -> p {' '.join(names)}",
                                **{c: d for c, d in zip(names, dims)})
            return v

        Hh, Hl = carve(SR, 0, 2, CH, D), carve(SR, 1024, 2, CH, D)
        Gh, Gl = carve(SR, 2048, 2, T), carve(SR, 3072, 2, T)
        Zh, Zl = carve(SR, 4096, 2, T), carve(SR, 5120, 2, T)
        Yh, Yl = carve(SR, 6144, 2, CH, D), carve(SR, 7168, 2, CH, D)
        WXh, WXl = carve(SR, 0, SKIP, T), carve(SR, 2048, SKIP, T)
        WHh, WHl = carve(SR, 4096, SKIP - 1, T), carve(SR, 5632, SKIP - 1, T)
        STh = carve(SR, 7168, 2, T)
        STl = sb("state_lo", [P, 2, T], F32R)
        Nh, Nl = carve(SR, 0, 2, CH, D), carve(SR, 1024, 2, CH, D)
        Rh, Rl = carve(SR, 2048, 2, HALVES, T), carve(SR, 4096, 2, HALVES, T)

        N = carve(SF, 0, 4, CH, D)
        T1 = carve(SF, 2048, 2, T)
        T2 = carve(SF, 3072, 2, T)
        wih_rows = carve(SF, 4096, 16, P)
        whh_rows = carve(SF, 6144, 12, P)
        diag_blocks = carve(SF, 7680, CH, P)
        deg_rows = carve(SF, 8192, T)
        deg_t = carve(SF, 3072, T)
        dinv_all = carve(SF, 8704, T)
        Th = carve(SF, 2048, 2, T)
        gcn_w32 = carve(SF, 2048, 2, P)
        vec_rows = carve(SF, 2304, P)
        bhh_rows = carve(SF, 2432, P)
        bias_deg = carve(SF, 9216, T)
        stage_w = carve(SF, 1024, 8, P)
        tw = stage_w[:, 0:4, :]
        TG = carve(SF, 0, 2, 4, T)
        CC = carve(SF, 4096, 2, T)
        TC = carve(SF, 5120, 2, T)
        HF = carve(SF, 6144, 2, T)
        TA = carve(SF, 7168, T)
        TB = carve(SF, 7680, T)
        HT = carve(SF, 2048, T)
        AG = carve(SF, 2560, T)
        U = carve(SF, 3072, CH, T)
        PT = carve(SF, 5120, CH, T)
        R = carve(SF, 7168, CH, T)
        NT = carve(SF, 9216, T)
        NT2 = carve(SF, 8704, 2, T)
        OS = carve(SF, 7168, T)
        TTS = carve(SF, 7680, 2, T)
        RZ = carve(SF, 2048, 2, HALVES, T)

        in_adj, in_vec, in_gcn_w, in_small = sem("in_adj"), sem("in_vec"), sem("in_gcn_w"), sem("in_small")
        in_lstm = sem("in_lstm")
        in_x = [sem(f"in_x{i}") for i in range(4)]
        in_adj2 = sem("in_adj2")
        consts = sem("consts")
        pool_chain = sem("pool_chain")
        dve_chain = sem("dve_chain")
        diag_ready = sem("diag_ready")
        prep_mm = sem("prep_mm")
        prep_hi = sem("prep_hi")
        prep_done = sem("prep_done")
        deg_ready, dinv_ready, dinv_col = sem("deg_ready"), sem("dinv_ready"), sem("dinv_col")

        ln_stats_done = sem("ln_stats_done")
        ln_sums, ln_square, ln_quarter = sem("ln_sums"), sem("ln_square"), sem("ln_quarter_done")
        ln_dvar, ln_root, ln_rstd = sem("ln_dvar_done"), sem("ln_root_done"), sem("ln_rstd_done")
        ln_scale_ready = sem("ln_scale_ready")
        ln_normed = sem("ln_normed")

        pads = []

        def apart(dve):
            pads.append(len(pads) % 32)
            dve.memset(pad[0:1, pads[-1]:pads[-1] + 1], 0.0)

        def ln_stats(dve, st, lag, nth):
            b, r = st.b(lag), st.ring(lag, 2)
            n = nth * NB + b
            if nth or st.from_(lag, 2):
                dve.wait_ge(ln_sums, n - 1)
            apart(dve)
            for c in range(CH):
                i = dve.bn_stats(stats[:, r, c, :], X[:, bass.ds(b, 1), c, :].rearrange("p o d -> p (o d)"))
            i.then_inc(ln_stats_done, 1)

        def ln_scale(pool, st, lag, nth):
            b, r = st.b(lag), st.ring(lag, 2)
            n = nth * NB + b
            me, vc_e, mo, vc_o = (stats[:, r, :, i] for i in (1, 2, 4, 5))
            pool.wait_ge(ln_stats_done, n + 1)
            pool.tensor_tensor(ln_d[:, :], me, mo, ALU.subtract)
            pool.tensor_tensor(ln_s[:, :], me, mo, ALU.add)
            pool.tensor_tensor(ln_q[:, :], vc_e, vc_o, ALU.add).then_inc(ln_sums, 1)
            pool.wait_ge(ln_sums, n + 1)
            pool.tensor_tensor(ln_dd[:, :], ln_d[:, :], ln_d[:, :], ALU.mult)
            pool.tensor_tensor(ln_m[:, :], ln_s[:, :], neg_half[:, :], ALU.mult)
            pool.tensor_tensor(ln_qe[:, :], ln_q[:, :], d_eps[:, :], ALU.add).then_inc(ln_square, 1)
            pool.wait_ge(ln_square, n + 1)
            pool.tensor_tensor(ln_dq[:, :], ln_dd[:, :], quarter_d[:, :], ALU.mult).then_inc(ln_quarter, 1)
            pool.wait_ge(ln_quarter, n + 1)
            pool.tensor_tensor(ln_v[:, :], ln_dq[:, :], ln_qe[:, :], ALU.add).then_inc(ln_dvar, 1)
            pool.wait_ge(ln_dvar, n + 1)
            pool.tensor_tensor(ln_p[:, :], ln_v[:, :], neg_half[:, :], ALU.pow).then_inc(ln_root, 1)
            pool.wait_ge(ln_root, n + 1)
            if nth or st.from_(lag, 2):
                pool.wait_ge(ln_normed, n - 1)
            pool.tensor_tensor(rstd[:, r, :], ln_p[:, :], sqrt_d[:, :], ALU.mult).then_inc(ln_rstd, 1)
            pool.wait_ge(ln_rstd, n + 1)
            pool.tensor_tensor(nbias[:, r, :], ln_m[:, :], rstd[:, r, :], ALU.mult).then_inc(ln_scale_ready, 1)

        def ln_apply(act, st, lag, nth, ring):
            b, r = st.b(lag), st.ring(lag, 2)
            n = nth * NB + b
            act.wait_ge(ln_scale_ready, n + 1)
            for c in range(CH):
                i = act.activation(N[:, st.ring(lag, ring), c, :],
                                   X[:, bass.ds(b, 1), c, :].rearrange("p o d -> p (o d)"),
                                   ACT.Relu, bias=nbias[:, r, c:c + 1], scale=rstd[:, r, c:c + 1])
            i.then_inc(ln_normed, 1)

        def product(pe, o, w, xv, first=True, last=True):
            pe.matmul(o, w[0], xv[0], start=first, stop=False)
            pe.matmul(o, w[0], xv[1], start=False, stop=False)
            return pe.matmul(o, w[1], xv[0], start=False, stop=last)

        def colb(t, b):
            return t[:, bass.ds(b, 1), :].rearrange("p o t -> p (o t)")

        gcn_h = sem("gcn_h_split")
        gcn_agg, gcn_agg_hi, gcn_agg_split = sem("gcn_agg"), sem("gcn_agg_hi"), sem("gcn_agg_split")
        gcn_z, gcn_z_sum, gcn_z_hi, gcn_z_split = sem("gcn_z"), sem("gcn_z_sum"), sem("gcn_z_hi"), sem("gcn_z_split")
        gcn_y, gcn_y_sum, gcn_y_hi, gcn_y_split = sem("gcn_y"), sem("gcn_y_sum"), sem("gcn_y_hi"), sem("gcn_y_split")
        gcn_o, gcn_o_hi, gcn_o_split = sem("gcn_o"), sem("gcn_o_hi"), sem("gcn_o_split")
        gcn_hh = sem("gcn_h_hi")
        ahat_tmp = sem("ahat_tmp")
        gate_mm = sem("gate_mm")
        cell_gates = sem("cell_gates")
        all_gates = sem("all_gates")
        cell_parts = sem("cell_parts")
        cell_new = sem("cell_new")
        cell_tanh = sem("cell_tanh")
        h_full, h_hi, h_split = sem("h_full"), sem("h_hi"), sem("h_split")

        def attention_events(name, events):
            return {k: sem(f"{name}_{k}") for k in events.split()}

        gat = attention_events("gat", "col t1 x_new t2 nt proj s1 s1_8 u e_top l_top bias relu v exp pt_mm pt_dve pt_act ag_mm ag "
                        "out_mm rden final")
        att = attention_events("att", "bn_in col t1 x_new t2 nt proj tt sc u bias exp pt_mm pt_dve pt_act ag_mm ag out_mm rden final")
        l2_hi, l2_split = sem("l2_h_hi"), sem("l2_h_split")
        l2_agg, l2_agg_hi, l2_agg_split = sem("l2_agg"), sem("l2_agg_hi"), sem("l2_agg_split")
        l2_z, l2_zstats = sem("l2_z"), sem("l2_z_stats")
        bn_chain, bn_var, bn_rs, bn_ready = sem("bn_chain"), sem("bn_var"), sem("bn_rs"), sem("bn_ready")
        l2_z2, l2_relu, l2_r_hi, l2_r_split = sem("l2_z2"), sem("l2_relu"), sem("l2_r_hi"), sem("l2_r_split")
        l2_o, l2_o_hi, l2_o_stats, l2_o_split = sem("l2_o"), sem("l2_o_hi"), sem("l2_o_stats"), sem("l2_o_split")
        causal_ready, mask_ready = sem("causal_ready"), sem("mask_ready")
        out_dma = sem("out_dma")

        block = ctx.enter_context(nc.Block())
        GATES = (0, 2, 1, 3)

        def lstm_units(p):
            nb = {1: 1, 2: 2, 3: 2, 4: 4}[p]
            return nb, T // p, NB // (2 * nb)

        SUB, GAT0 = {1: 0}, {1: 0}
        for _p in range(1, SKIP + 1):
            _r = lstm_units(_p)[2]
            SUB[_p + 1] = SUB[_p] + _r * _p * 2
            GAT0[_p + 1] = GAT0[_p] + _r * 2 * (4 * _p - 1)

        def lstm_walk(p, emit):
            R_ = lstm_units(p)[2]
            emit(0)
            return R_

        def col_view(t, p, r, k, s):
            nb, nw, _ = lstm_units(p)
            v = t[:, bass.ds((r * 2 + k) * nb, nb), 0:nw * p]
            return v.rearrange("q b (w s) -> q b w s", s=p)[:, :, :, s]

        def tile_view(v, p):
            nb, nw, _ = lstm_units(p)
            return v[:, 0:nb * nw].rearrange("q (b w) -> q b w", b=nb)

        def lstm_loop(eng, body):
            for p in range(1, SKIP + 1):
                R_ = lstm_units(p)[2]
                body(p, 0)
                if R_ == 2:
                    body(p, 1)
                else:
                    with eng.Fori(1, R_) as r:
                        body(p, r)

        SETUP = ["vec", "adj", "adj", "adj", "adj", "rowsum", "colsum", "diag", "bg1", "tw", "bnw", "fold"]
        G0 = len(SETUP)
        LATE = ["deg", "dinv"] + ["ahat"] * 4 + ["wih"] * 4 + ["whh"] * 3

        @block.sync
        def _(sp):
            sp.dma_start(A[:, :, :], adj.rearrange("(c p) s -> p c s", p=P)).then_inc(in_adj, 16)
            r = 0
            for ap, n in ((bih.rearrange("l (g d) -> (l g) d", d=P), 16), (bg0.rearrange("(o d) -> o d", o=1), 1),
                          (b1.rearrange("(o d) -> o d", o=2), 2), (g1.rearrange("(o d) -> o d", o=2), 2),
                          (be1.rearrange("(o d) -> o d", o=2), 2), (b2.rearrange("(o d) -> o d", o=1), 1),
                          (g2.rearrange("(o d) -> o d", o=1), 1), (be2.rearrange("(o d) -> o d", o=1), 1),
                          (gat_a.rearrange("(k o) u -> k (o u)", k=2), 2)):
                sp.dma_start(vec_rows[r:r + n, :], ap).then_inc(in_vec, 16)
                r += n
            sp.dma_start(bhh_rows[0:16, :], bhh.rearrange("l (g d) -> (l g) d", d=P)).then_inc(in_vec, 16)
            sp.dma_start(bg1_row[:, :], bg1.rearrange("(o d) -> o d", o=1)).then_inc(in_vec, 16)
            sp.dma_start(gcn_w32[:, 0, :], Wg0).then_inc(in_gcn_w, 16)
            sp.dma_start(gcn_w32[:, 1, :], Wg1).then_inc(in_gcn_w, 16)
            xv = x.rearrange("b (c p) d -> p b c d", p=P)
            for q in range(4):
                for b in range(4 * q, 4 * q + 4):
                    sp.dma_start(X[:, b, :, :], xv[:, b, :, :]).then_inc(in_x[q], 16)
                if q == 0:
                    sp.dma_start(gat_w[:, :], gat_W).then_inc(in_small, 16)
                    sp.dma_start(wo32[:, :], Wo).then_inc(in_small, 16)
                    sp.dma_start(stage_w[:, 0, :], gat_W).then_inc(in_small, 16)
                    sp.dma_start(stage_w[:, 4:6, :], W1.rearrange("(h p) d -> p h d", p=P)).then_inc(in_small, 16)
                    sp.dma_start(stage_w[:, 6:8, :], W2.rearrange("o (h d) -> o h d", h=2)).then_inc(in_small, 16)
                    sp.dma_start(stage_w[:, 1:4, :], Wqkv.rearrange("c (k d) -> c k d", k=3)).then_inc(in_small, 16)
            sp.dma_start(wih_rows[:, :, :], Wih.rearrange("l (g p) d -> p (l g) d", p=P)).then_inc(in_lstm, 16)
            sp.dma_start(whh_rows[:, :, :], Whh[1:SKIP].rearrange("l (g p) d -> p (l g) d", p=P)).then_inc(in_lstm, 16)
            sp.wait_ge(gat["final"], NB)
            sp.dma_start(A[:, :, :], adj.rearrange("(c p) s -> p c s", p=P)).then_inc(in_adj2, 16)
            ov = out.rearrange("b (c p) d -> p b c d", p=P)
            with sp.Fori(0, NB) as b:
                sp.wait_ge(att["final"], b + 1)
                sp.dma_start(ov[:, bass.ds(b, 1), :, :], X[:, bass.ds(b, 1), :, :]).then_inc(out_dma, 16)
            sp.wait_ge(out_dma, 16 * NB)

        @block.gpsimd
        def _(pool):
            pool.memset(ones[:, :], 1.0).then_inc(consts, 1)
            pool.memset(neg_half[:, :], -0.5).then_inc(consts, 1)
            pool.memset(d_eps[:, :], D * EPS).then_inc(consts, 1)
            pool.memset(quarter_d[:, :], D / 4).then_inc(consts, 1)
            pool.memset(sqrt_d[:, :], float(D) ** 0.5).then_inc(consts, 1)
            pool.wait_ge(consts, 1)
            pool.affine_select(out=ident[:, :], in_=ones[:, :], compare_op=ALU.is_equal, fill=0.0, base=0,
                               pattern=[[-1, P]], channel_multiplier=1).then_inc(consts, 1)
            pool.wait_ge(consts, 6)

            def gcn_step(st):
                if st.has(0):
                    ln_scale(pool, st, 0, 0)
            pipeline(pool, 2, 2, 0, gcn_step)
            pool.wait_ge(deg_ready, 1)
            pool.tensor_tensor(dinv[:, :], deg[:, :], neg_half[:, :], ALU.pow).then_inc(dinv_ready, 1)

            def gat_step(st):
                if st.has(0):
                    b = st.b(0)
                    if st.from_(0, 1):
                        pool.wait_ge(gat["t1"], b)
                    pool.tensor_tensor(HT, colb(Ch, b).bitcast(F32), colb(Cl, b).bitcast(F32),
                                       ALU.add).then_inc(gat["col"], 1)
                    ln_scale(pool, st, 0, 1)
            pool.wait_ge(h_split, SUB[SKIP + 1])
            pipeline(pool, 2, 2, 0, gat_step)

            pipeline(pool, 2, 2, 0, lambda st: ln_scale(pool, st, 0, 2))

            pool.wait_ge(bn_var, 1)
            pool.tensor_tensor(brs[:, 0:2], bve[:, 0:2], neg_half[:, 0:2], ALU.pow).then_inc(bn_rs, 1)
            pool.wait_ge(in_adj2, 16)
            for c in range(CH):
                blk = A[:, c, c * P:(c + 1) * P]
                pool.affine_select(out=blk, in_=blk, compare_op=ALU.is_ge, fill=NEG, base=0,
                                   pattern=[[-1, P]], channel_multiplier=1).then_inc(causal_ready, 1)
            pool.wait_ge(bn_var, 2)
            pool.tensor_tensor(brs[:, 2:3], bve[:, 2:3], neg_half[:, 0:1], ALU.pow).then_inc(bn_rs, 1)

            def att_step(st):
                if st.has(0):
                    b = st.b(0)
                    if st.from_(0, 1):
                        pool.wait_ge(att["col"], b)
                    pool.tensor_tensor(OS, colb(Ch, b).bitcast(F32), colb(Cl, b).bitcast(F32),
                                       ALU.add).then_inc(att["bn_in"], 1)
                    ln_scale(pool, st, 0, 3)
            pool.wait_ge(l2_o_split, NB)
            pipeline(pool, 2, 2, 0, att_step)

        @block.tensor
        def _(pe):
            pe.wait_ge(consts, 6)

            def transposes4(bk, srcs):
                for i, s in enumerate(srcs):
                    mm = pe.transpose(bank[bk][:, i * P:(i + 1) * P], s, ident[:, :])
                return mm

            for g, kind in enumerate(SETUP):
                bk = bank[g % 8]
                if g >= 8:
                    pe.wait_ge(prep_done, g - 7)
                if kind == "vec":
                    pe.wait_ge(in_vec, 16 * 11)
                    pe.transpose(bk[:, 0:NVEC], vec_rows[0:NVEC, :], ident[0:NVEC, 0:NVEC])
                    mm = pe.transpose(bk[:, BHH_COL:BHH_COL + 16], bhh_rows[0:16, :], ident[0:16, 0:16])
                elif kind == "adj":
                    c = g - 1
                    if c == 0:
                        pe.wait_ge(in_adj, 16)
                    mm = transposes4(g % 8, [A[:, t, c * P:(c + 1) * P] for t in range(CH)])
                elif kind == "rowsum":
                    pe.wait_ge(prep_done, 5)
                    for c in range(CH):
                        pe.matmul(bk[:, :], ones_r[:, :], Ath[:, c, :], start=(c == 0), stop=False)
                        mm = pe.matmul(bk[:, :], ones_r[:, :], Atl[:, c, :], start=False, stop=(c == CH - 1))
                elif kind == "colsum":
                    for c in range(CH):
                        mm = pe.matmul(bk[:, :], ones[:, :], A[:, c, :], start=(c == 0), stop=(c == CH - 1))
                elif kind == "diag":
                    pe.wait_ge(diag_ready, 1)
                    mm = pe.matmul(bk[:, :], ones[:, :], diag_blocks.rearrange("p a b -> p (a b)"),
                                   start=True, stop=True)
                elif kind == "bg1":
                    mm = pe.matmul(bk[:, 0:P], ones[0:1, :], bg1_row[:, :], start=True, stop=True)
                elif kind == "tw":
                    pe.wait_ge(in_small, 16 * 6)
                    mm = transposes4(g % 8, [stage_w[:, i, :] for i in range(4)])
                elif kind == "bnw":
                    mm = transposes4(g % 8, [stage_w[:, i, :] for i in range(4, 8)])
                else:
                    pe.wait_ge(prep_done, g)
                    pe.matmul(bk[:, 0:2], tw[:, 0, :], V[:, COL["a"]:COL["a"] + 2], start=True, stop=True)
                    pe.matmul(bk[:, P:2 * P], tw[:, 1, :], tw[:, 2, :], start=True, stop=True)
                    mm = pe.matmul(bk[:, 2 * P:3 * P], tw[:, 3, :], wo32[:, :], start=True, stop=True)
                mm.then_inc(prep_mm, 1)

            pe.wait_ge(prep_done, G0)

            def gcn_step(st):
                if st.has(2):
                    b, r = st.b(2), st.ring(2, 2)
                    pe.wait_ge(gcn_h, b + 1)
                    if st.from_(2, 2):
                        pe.wait_ge(gcn_agg_split, b - 1)
                    for c in range(CH):
                        mm = product(pe, bank[r][:, :], (Hh[:, r, c, :], Hl[:, r, c, :]), (Ath[:, c, :], Atl[:, c, :]),
                                     c == 0, c == CH - 1)
                    mm.then_inc(gcn_agg, 1)
                if st.has(3):
                    b, r = st.b(3), st.ring(3, 2)
                    pe.wait_ge(gcn_agg_split, b + 1)
                    if st.from_(3, 2):
                        pe.wait_ge(gcn_z_sum, b - 1)
                    product(pe, bank[2 + r][:, :], (gcn_wh[:, 0, :], gcn_wl[:, 0, :]),
                            (Gh[:, r, :], Gl[:, r, :])).then_inc(gcn_z, 1)
                if st.has(4):
                    b, r = st.b(4), st.ring(4, 2)
                    pe.wait_ge(gcn_z_split, b + 1)
                    if st.from_(4, 2):
                        pe.wait_ge(gcn_y_sum, b - 1)
                    for c in range(CH):
                        cs = slice(c * P, (c + 1) * P)
                        mm = product(pe, bank[4 + r][:, cs], (Zh[:, r, cs], Zl[:, r, cs]),
                                     (gcn_wh[:, 1, :], gcn_wl[:, 1, :]))
                    mm.then_inc(gcn_y, 1)
                if st.has(5):
                    b, r = st.b(5), st.ring(5, 2)
                    pe.wait_ge(gcn_y_split, b + 1)
                    if st.from_(5, 1):
                        pe.wait_ge(gcn_o_split, b)
                    for c in range(CH):
                        mm = product(pe, bank[6][:, :], (Yh[:, r, c, :], Yl[:, r, c, :]), (Ath[:, c, :], Atl[:, c, :]),
                                     c == 0, c == CH - 1)
                    mm.then_inc(gcn_o, 1)
            pipeline(pe, 6, 2, 5, gcn_step)

            pe.wait_ge(gcn_o_split, NB)
            pe.wait_ge(in_lstm, 32)
            for i, kind in enumerate(LATE):
                g = G0 + i
                if i >= 8:
                    pe.wait_ge(prep_done, g - 7)
                if kind == "deg":
                    mm = transposes4(i % 8, [deg_rows[:, c * P:(c + 1) * P] for c in range(CH)])
                elif kind == "dinv":
                    pe.wait_ge(dinv_col, 1)
                    mm = transposes4(i % 8, [Th[:, 0, c * P:(c + 1) * P] for c in range(CH)])
                elif kind == "ahat":
                    c = i - 2
                    pe.wait_ge(diag_ready, 2)
                    mm = transposes4(i % 8, [diag_blocks[:, c, :] if t == c else A[:, t, c * P:(c + 1) * P]
                                             for t in range(CH)])
                elif kind == "wih":
                    mm = transposes4(i % 8, [wih_rows[:, 4 * (i - 6) + k, :] for k in range(4)])
                else:
                    mm = transposes4(i % 8, [whh_rows[:, 4 * (i - 10) + k, :] for k in range(4)])
                mm.then_inc(prep_mm, 1)
            pe.wait_ge(prep_done, G0 + len(LATE))

            def lstm_pair(p, r):
                nb, nw, _ = lstm_units(p)
                if p > 1:
                    per = 2 * (p - 1) * nb // lstm_units(p - 1)[0]
                    pe.wait_ge(h_split, SUB[p - 1] + per * (r + 1))
                for s in range(p):
                    for k in range(2):
                        q = SUB[p] + (r * p + s) * 2 + k
                        if not (p == 1 and isinstance(r, int) and r == 0):
                            pe.wait_ge(all_gates, q - 1)
                        gates = [g for g in GATES if s > 0 or g != 1]
                        xs = (col_view(Ch, p, r, k, s), col_view(Cl, p, r, k, s))
                        for g in gates:
                            o = tile_view(bank[4 * k + g], p)
                            gs = slice(g * P, (g + 1) * P)
                            mm = product(pe, o, (WXh[:, p - 1, gs], WXl[:, p - 1, gs]), xs, True, s == 0)
                            if s == 0:
                                mm.then_inc(gate_mm, 1)
                        if s > 0:
                            pe.wait_ge(h_split, q - 1)
                            hs = (tile_view(STh[:, k, :], p), tile_view(STl[:, k, :], p))
                            for g in gates:
                                o = tile_view(bank[4 * k + g], p)
                                gs = slice(g * P, (g + 1) * P)
                                product(pe, o, (WHh[:, p - 2, gs], WHl[:, p - 2, gs]), hs, False,
                                        True).then_inc(gate_mm, 1)
            lstm_loop(pe, lstm_pair)

            def gat_step(st):
                if st.has(0):
                    b, r = st.b(0), st.ring(0, 2)
                    pe.wait_ge(gat["col"], b + 1)
                    if st.from_(0, 1):
                        pe.wait_ge(gat["x_new"], b)
                    transposes4(0, [HT[:, c * P:(c + 1) * P] for c in range(CH)]).then_inc(gat["t1"], 1)
                if st.has(1):
                    b, r = st.b(1), st.ring(1, 4)
                    pe.wait_ge(ln_normed, 1 * NB + b + 1)
                    if st.from_(1, 1):
                        pe.wait_ge(gat["nt"], b)
                    transposes4(1, [N[:, r, c, :] for c in range(CH)]).then_inc(gat["t2"], 1)
                if st.has(3):
                    b, r = st.b(3), st.ring(3, 4)
                    pe.wait_ge(gat["pt_act"], 2 * b + 2)
                    pe.wait_ge(gat["pt_dve"], 2 * b + 2)
                    for c in range(CH):
                        mm = pe.matmul(bank[6][:, :], N[:, r, c, :], PT[:, c, :], start=(c == 0), stop=(c == CH - 1))
                    mm.then_inc(gat["ag_mm"], 1)
                if st.has(1):
                    b, r = st.b(1), st.ring(1, 2)
                    pe.wait_ge(gat["nt"], b + 1)
                    if st.from_(1, 1):
                        pe.wait_ge(gat["u"], 4 * b)
                    pe.matmul(bank[2][:, :], gat_v2[:, :], NT, start=True, stop=True)
                    for c in range(CH):
                        mm = pe.matmul(bank[3][:, c:c + 1], NT[:, c * P:(c + 1) * P], gat_v[:, 0:1],
                                       start=True, stop=True)
                    mm.then_inc(gat["proj"], 1)
                if st.has(3):
                    b = st.b(3)
                    pe.wait_ge(gat["ag"], b + 1)
                    if st.from_(3, 1):
                        pe.wait_ge(gat["final"], b)
                    for c in range(CH):
                        mm = pe.matmul(bank[7][:, c * P:(c + 1) * P], AG[:, c * P:(c + 1) * P], gat_w[:, :],
                                       start=True, stop=True)
                    mm.then_inc(gat["out_mm"], 1)
                if st.has(2):
                    b = st.b(2)
                    for c in range(CH):
                        pe.wait_ge(gat["exp"], 4 * b + c + 1)
                        if c >= 2:
                            pe.wait_ge(gat["pt_act"] if c % 2 == 0 else gat["pt_dve"], 2 * b + 1)
                        elif st.from_(2, 1):
                            pe.wait_ge(gat["pt_act"] if c % 2 == 0 else gat["pt_dve"], 2 * b)
                        transposes4(4 + c % 2, [R[:, c, i * P:(i + 1) * P] for i in range(CH)]).then_inc(gat["pt_mm"], 1)
            pe.wait_ge(all_gates, SUB[SKIP + 1])
            pipeline(pe, 4, 4, 3, gat_step)

            def l2_step(st):
                if st.has(2):
                    b, r = st.b(2), st.ring(2, 2)
                    pe.wait_ge(l2_split, b + 1)
                    if st.from_(2, 2):
                        pe.wait_ge(l2_agg_split, b - 1)
                    for c in range(CH):
                        mm = product(pe, bank[r][:, :], (Nh[:, r, c, :], Nl[:, r, c, :]), (Ath[:, c, :], Atl[:, c, :]),
                                     c == 0, c == CH - 1)
                    mm.then_inc(l2_agg, 1)
                if st.has(3):
                    b, r = st.b(3), st.ring(3, 2)
                    pe.wait_ge(l2_agg_split, b + 1)
                    if st.from_(3, 2):
                        pe.wait_ge(l2_zstats, b - 1)
                    for h in range(HALVES):
                        mm = product(pe, bank[2 + 2 * r + h][:, :], (bn_wh[:, h, :], bn_wl[:, h, :]),
                                     (colb(Ch, b), colb(Cl, b)))
                    mm.then_inc(l2_z, 1)
            pe.wait_ge(gat["final"], NB)
            pipeline(pe, 6, 2, 3, l2_step)

            def l2b_step(st):
                if st.has(0):
                    b, r = st.b(0), st.ring(0, 2)
                    if st.from_(0, 2):
                        pe.wait_ge(l2_relu, b - 1)
                    for h in range(HALVES):
                        mm = product(pe, bank[2 * r + h][:, :], (bn_wh[:, h, :], bn_wl[:, h, :]),
                                     (colb(Ch, b), colb(Cl, b)))
                    mm.then_inc(l2_z2, 1)
                if st.has(1):
                    b, r = st.b(1), st.ring(1, 2)
                    pe.wait_ge(l2_r_split, b + 1)
                    if st.from_(1, 2):
                        pe.wait_ge(l2_o_split, b - 1)
                    for h in range(HALVES):
                        mm = product(pe, bank[4 + r][:, :], (bn_wh[:, 2 + h, :], bn_wl[:, 2 + h, :]),
                                     (Rh[:, r, h, :], Rl[:, r, h, :]), h == 0, h == HALVES - 1)
                    mm.then_inc(l2_o, 1)
            pe.wait_ge(l2_zstats, NB)
            pipeline(pe, 4, 2, 1, l2b_step)

            def att_step(st):
                if st.has(0):
                    b, r = st.b(0), st.ring(0, 2)
                    pe.wait_ge(att["col"], b + 1)
                    if st.from_(0, 1):
                        pe.wait_ge(att["x_new"], b)
                    transposes4(0, [HT[:, c * P:(c + 1) * P] for c in range(CH)]).then_inc(att["t1"], 1)
                if st.has(1):
                    b, r = st.b(1), st.ring(1, 4)
                    pe.wait_ge(ln_normed, 3 * NB + b + 1)
                    if st.from_(1, 1):
                        pe.wait_ge(att["nt"], b)
                    transposes4(1, [N[:, r, c, :] for c in range(CH)]).then_inc(att["t2"], 1)

                def scores(cs):
                    b, r = st.b(2), st.ring(2, 2)
                    for c in cs:
                        w = (c + 1) * P
                        if c >= 2:
                            pe.wait_ge(att["u"], 4 * b + c - 1)
                        elif st.from_(2, 1):
                            pe.wait_ge(att["u"], 4 * b + c - 1)
                        pe.matmul(bank[3 + c % 2][:, 0:w], TTS[:, r, c * P:w], NT2[:, r, 0:w],
                                  start=True, stop=True).then_inc(att["sc"], 1)
                if st.has(2):
                    pe.wait_ge(att["tt"], st.b(2) + 1)
                    scores((0, 1))
                if st.has(3):
                    b, r = st.b(3), st.ring(3, 4)
                    pe.wait_ge(att["pt_act"], 2 * b + 2)
                    pe.wait_ge(att["pt_dve"], 2 * b + 2)
                    if st.from_(3, 1):
                        pe.wait_ge(att["final"], b)
                    for c in range(CH):
                        mm = pe.matmul(bank[7][:, c * P:T], N[:, r, c, :], PT[:, c, c * P:T],
                                       start=(c == 0), stop=(c == CH - 1))
                    mm.then_inc(att["ag_mm"], 1)
                if st.has(2):
                    scores((2, 3))
                if st.has(1):
                    b, r = st.b(1), st.ring(1, 2)
                    pe.wait_ge(att["nt"], b + 1)
                    if st.from_(1, 1):
                        pe.wait_ge(att["tt"], b)
                    pe.matmul(bank[2][:, :], w_qk[:, :], NT2[:, r, :], start=True, stop=True).then_inc(att["proj"], 1)
                if st.has(3):
                    pe.wait_ge(att["ag"], st.b(3) + 1)
                    for c in range(CH):
                        mm = pe.matmul(bank[7][:, c * P:(c + 1) * P], AG[:, c * P:(c + 1) * P], w_vo[:, :],
                                       start=True, stop=True)
                    mm.then_inc(att["out_mm"], 1)
                if st.has(2):
                    b = st.b(2)
                    for c in range(CH):
                        pe.wait_ge(att["exp"], 4 * b + c + 1)
                        if c >= 2:
                            pe.wait_ge(att["pt_act"] if c % 2 == 0 else att["pt_dve"], 2 * b + 1)
                        elif st.from_(2, 1):
                            pe.wait_ge(att["pt_act"] if c % 2 == 0 else att["pt_dve"], 2 * b)
                        transposes4(5 + c % 2, [U[:, c, i * P:(i + 1) * P] for i in range(c + 1)]).then_inc(att["pt_mm"], 1)
            pe.wait_ge(l2_o_split, NB)
            pipeline(pe, 4, 4, 3, att_step)

        @block.scalar
        def _(act):
            act.wait_ge(consts, 6)
            act.activation(s1x[:, 0:1], ones[:, 0:1], ACT.Tanh)
            act.activation(ones_r[:, :], ones[:, :], ACT.Copy).then_inc(prep_hi, 1)
            act.wait_ge(in_gcn_w, 32)
            act.activation(gcn_wh[:, :, :], gcn_w32[:, :, :], ACT.Copy).then_inc(prep_hi, 1)

            def copy_hi(g, bk, dst, scale=1.0):
                act.wait_ge(prep_mm, g + 1)
                act.activation(dst, bank[bk][:, :], ACT.Copy, scale=scale).then_inc(prep_hi, 1)

            for g, kind in enumerate(SETUP):
                if kind == "adj":
                    copy_hi(g, g % 8, Ath[:, g - 1, :])
                elif kind == "bnw":
                    copy_hi(g, g % 8, bn_wh[:, :, :].rearrange("p a b -> p (a b)"))

            def gcn_step(st):
                if st.has(2):
                    b, r = st.b(2), st.ring(2, 2)
                    act.wait_ge(gcn_agg, b + 1)
                    if st.from_(2, 2):
                        act.wait_ge(gcn_z, b - 1)
                    act.activation(Gh[:, r, :], bank[r][:, :], ACT.Copy).then_inc(gcn_agg_hi, 1)
                if st.has(3):
                    b, r = st.b(3), st.ring(3, 2)
                    act.wait_ge(gcn_z_sum, b + 1)
                    if st.from_(3, 2):
                        act.wait_ge(gcn_y, b - 1)
                    act.activation(Zh[:, r, :], T1[:, r, :], ACT.Relu).then_inc(gcn_z_hi, 1)
                if st.has(4):
                    b, r = st.b(4), st.ring(4, 2)
                    act.wait_ge(gcn_y_sum, b + 1)
                    if st.from_(4, 2):
                        act.wait_ge(gcn_o, b - 1)
                    act.activation(Yh[:, r, :, :].rearrange("p a b -> p (a b)"), T2[:, r, :],
                                   ACT.Copy).then_inc(gcn_y_hi, 1)
                if st.has(1):
                    b = st.b(1)
                    if st.from_(1, 2):
                        act.wait_ge(gcn_h, b - 1)
                    ln_apply(act, st, 1, 0, 2)
                if st.has(5):
                    b = st.b(5)
                    act.wait_ge(gcn_o, b + 1)
                    act.activation(colb(Ch, b), bank[6][:, :], ACT.Relu).then_inc(gcn_o_hi, 1)
            pipeline(act, 6, 2, 5, gcn_step)

            act.wait_ge(gcn_o_split, NB)
            for i, kind in enumerate(LATE):
                g = G0 + i
                if kind == "ahat":
                    c = i - 2
                    act.wait_ge(ahat_tmp, c + 1)
                    act.activation(Ath[:, c, :], Th[:, (c + 1) % 2, :], ACT.Copy).then_inc(prep_hi, 1)
                elif kind == "wih":
                    copy_hi(g, i % 8, WXh[:, i - 6, :], 1.0 if i == 6 else 0.5)
                elif kind == "whh":
                    copy_hi(g, i % 8, WHh[:, i - 10, :], 0.5)

            def lstm_pair(p, r):
                def gates(s, k):
                    q = SUB[p] + (r * p + s) * 2 + k
                    order = [g for g in GATES if s > 0 or g != 1]
                    base = GAT0[p] + r * 2 * (4 * p - 1) + (k * 3 if s == 0 else 6 + (s - 1) * 8 + k * 4)
                    if not (p == 1 and isinstance(r, int) and r == 0):
                        act.wait_ge(h_full, q - 1)
                    for n, g in enumerate(order):
                        act.wait_ge(gate_mm, base + n + 1)
                        i = act.activation(tile_view(TG[:, k, g, :], p), tile_view(bank[4 * k + g], p), ACT.Tanh,
                                           bias=lstm_bias[:, p - 1, g:g + 1], scale=1.0 if g == 2 else 0.5)
                        if n == len(order) - 2:
                            i.then_inc(cell_gates, 1)
                    i.then_inc(all_gates, 1)

                def tanh_c(s, k):
                    q = SUB[p] + (r * p + s) * 2 + k
                    act.wait_ge(cell_new, q + 1)
                    act.activation(tile_view(TC[:, k, :], p), tile_view(CC[:, k, :], p), ACT.Tanh,
                                   scale=0.5).then_inc(cell_tanh, 1)
                for s in range(p):
                    for k in range(2):
                        gates(s, k)
                        if p > 1:
                            tanh_c(s, k)
                        elif k == 1:
                            tanh_c(0, 0)
                            tanh_c(0, 1)
            lstm_loop(act, lstm_pair)

            def gat_step(st):
                if st.has(2):
                    b = st.b(2)
                    act.wait_ge(gat["s1_8"], b + 1)
                    for c in range(CH):
                        act.wait_ge(gat["u"], 4 * b + c + 1)
                        if st.from_(2, 1):
                            act.wait_ge(gat["pt_mm"], 4 * b - 3 + c)
                        act.activation(R[:, c, :], U[:, c, :], ACT.Relu, bias=s1x[:, c:c + 1],
                                       scale=1.0 - SLOPE).then_inc(gat["relu"], 1)
                if st.has(1):
                    b, r = st.b(1), st.ring(1, 2)
                    act.wait_ge(gat["t2"], b + 1)
                    if st.from_(1, 1):
                        act.wait_ge(gat["proj"], b)
                    act.activation(NT, bank[1][:, :], ACT.Copy).then_inc(gat["nt"], 1)
                if st.has(3):
                    b = st.b(3)
                    act.wait_ge(gat["ag_mm"], b + 1)
                    if st.from_(3, 1):
                        act.wait_ge(gat["out_mm"], b)
                    act.activation(AG, bank[6][:, :], ACT.Copy).then_inc(gat["ag"], 1)
                if st.has(2):
                    b, r = st.b(2), st.ring(2, 2)
                    act.wait_ge(gat["bias"], b + 1)
                    if st.from_(2, 2):
                        act.wait_ge(gat["rden"], b - 1)
                    for c in range(CH):
                        act.wait_ge(gat["v"], 4 * b + c + 1)
                        act.activation(R[:, c, :], U[:, c, :], ACT.Exp, bias=soft_b[:, r, c:c + 1],
                                       accum_out=den[:, r, c:c + 1]).then_inc(gat["exp"], 1)
                        if c >= 1 and (c - 1) % 2 == 0:
                            pt_copy(st, c - 1, gat, 4)
                if st.has(0):
                    if st.from_(0, 4):
                        act.wait_ge(gat["ag_mm"], st.b(0) - 3)
                    ln_apply(act, st, 0, 1, 4)

            def pt_copy(st, c, s, bk):
                b = st.b(2)
                act.wait_ge(s["pt_mm"], 4 * b + c + 1)
                if c == 0 and st.from_(2, 1):
                    act.wait_ge(s["ag_mm"], b)
                n = CH if s is gat else c + 1
                act.activation(PT[:, 0:n, c * P:(c + 1) * P],
                               bank[bk][:, 0:n * P].rearrange("p (a b) -> p a b", b=P), ACT.Copy).then_inc(s["pt_act"], 1)
            act.wait_ge(h_split, SUB[SKIP + 1])
            pipeline(act, 4, 4, 3, gat_step)

            def l2_step(st):
                if st.has(1):
                    if st.from_(1, 2):
                        act.wait_ge(l2_split, st.b(1) - 1)
                    ln_apply(act, st, 1, 2, 2)
                if st.has(2):
                    b, r = st.b(2), st.ring(2, 2)
                    act.wait_ge(l2_agg, b + 1)
                    act.activation(colb(Ch, b), bank[r][:, :], ACT.Copy).then_inc(l2_agg_hi, 1)
            act.wait_ge(gat["final"], NB)
            pipeline(act, 6, 2, 3, l2_step)

            def l2b_step(st):
                if st.has(0):
                    b, r = st.b(0), st.ring(0, 2)
                    act.wait_ge(l2_z2, b + 1)
                    if st.from_(0, 2):
                        act.wait_ge(l2_r_split, b - 1)
                    for h in range(HALVES):
                        i = act.activation(RZ[:, r, h, :], bank[2 * r + h][:, :], ACT.Relu, bias=bbi[:, h:h + 1],
                                           scale=bsc[:, h:h + 1])
                    i.then_inc(l2_relu, 1)
                if st.has(1):
                    b, r = st.b(1), st.ring(1, 2)
                    act.wait_ge(l2_o, b + 1)
                    act.activation(colb(Ch, b), bank[4 + r][:, :], ACT.Copy).then_inc(l2_o_hi, 1)
            act.wait_ge(bn_ready, 1)
            pipeline(act, 4, 2, 1, l2b_step)

            def att_step(st):
                if st.has(0):
                    b = st.b(0)
                    act.wait_ge(att["bn_in"], b + 1)
                    if st.from_(0, 1):
                        act.wait_ge(att["t1"], b)
                    act.activation(HT, OS, ACT.Identity, bias=bbi[:, 2:3], scale=bsc[:, 2:3]).then_inc(att["col"], 1)
                if st.has(1):
                    b, r = st.b(1), st.ring(1, 2)
                    act.wait_ge(att["t2"], b + 1)
                    if st.from_(1, 2):
                        act.wait_ge(att["sc"], 4 * b - 4)
                    act.activation(NT2[:, r, :], bank[1][:, :], ACT.Copy).then_inc(att["nt"], 1)
                if st.has(2):
                    b, r = st.b(2), st.ring(2, 2)
                    if st.from_(2, 2):
                        act.wait_ge(att["rden"], b - 1)
                    act.wait_ge(att["bias"], b + 1)
                    for c in range(CH):
                        w = (c + 1) * P
                        act.activation(U[:, c, 0:w], U[:, c, 0:w], ACT.Exp, bias=soft_b[:, r, c:c + 1],
                                       accum_out=den[:, r, c:c + 1]).then_inc(att["exp"], 1)
                if st.has(3):
                    b = st.b(3)
                    act.wait_ge(att["ag_mm"], b + 1)
                    if st.from_(3, 1):
                        act.wait_ge(att["out_mm"], b)
                    act.activation(AG, bank[7][:, :], ACT.Copy).then_inc(att["ag"], 1)
                if st.has(1):
                    b, r = st.b(1), st.ring(1, 2)
                    act.wait_ge(att["proj"], b + 1)
                    act.activation(TTS[:, r, :], bank[2][:, :], ACT.Copy).then_inc(att["tt"], 1)
                if st.has(2):
                    pt_copy(st, 0, att, 5)
                    pt_copy(st, 2, att, 5)
                if st.has(0):
                    if st.from_(0, 4):
                        act.wait_ge(att["ag_mm"], st.b(0) - 3)
                    ln_apply(act, st, 0, 3, 4)
            act.wait_ge(l2_o_split, NB)
            act.wait_ge(bn_ready, 2)
            pipeline(act, 4, 4, 3, att_step)

        @block.vector
        def _(dve):
            n = [0]

            def then(i):
                n[0] += 1
                i.then_inc(dve_chain, 1)
                dve.wait_ge(dve_chain, n[0])

            hi = [2]

            def split_lo(dst, src, hi_ap, scale=None):
                hi[0] += 1
                dve.wait_ge(prep_hi, hi[0])
                h = hi_ap.bitcast(F32)
                if scale is None:
                    i = dve.tensor_tensor(dst, src, h, ALU.subtract)
                else:
                    i = dve.scalar_tensor_tensor(out=dst, in0=src, scalar=scale, in1=h, op0=ALU.mult, op1=ALU.subtract)
                return i

            dve.wait_ge(prep_hi, 2)
            then(dve.tensor_tensor(gcn_wl[:, :, :], gcn_w32[:, :, :], gcn_wh[:, :, :].bitcast(F32), ALU.subtract))
            dve.wait_ge(in_adj, 16)
            for c in range(CH):
                i = dve.tensor_tensor(diag_blocks[:, c, :], A[:, c, c * P:(c + 1) * P], ident[:, :], ALU.mult)
            i.then_inc(diag_ready, 1)
            for g, kind in enumerate(SETUP):
                bk = bank[g % 8][:, :]
                if kind not in ("adj", "bnw"):
                    dve.wait_ge(prep_mm, g + 1)
                if kind == "vec":
                    then(dve.tensor_copy(V[:, 0:NVEC], bk[:, 0:NVEC]))
                    then(dve.tensor_copy(V[:, BHH_COL:BHH_COL + 16], bk[:, BHH_COL:BHH_COL + 16]))
                    lb = lstm_bias[:, :, :].rearrange("p a b -> p (a b)")
                    then(dve.tensor_tensor(lb, V[:, 0:16], V[:, BHH_COL:BHH_COL + 16], ALU.add))
                    for s in (slice(0, 2), slice(3, 4)):
                        then(dve.tensor_scalar(lstm_bias[:, :, s], lstm_bias[:, :, s], 0.5, None, ALU.mult))
                    i = dve.tensor_copy(s1[:, 0:1], V[:, 0:1])
                elif kind == "adj":
                    i = split_lo(Atl[:, g - 1, :], bk, Ath[:, g - 1, :])
                elif kind == "rowsum":
                    then(dve.tensor_copy(deg_rows, bk))
                    i = dve.tensor_scalar(bias_deg, deg_rows, V[:, COL["bg0"]:COL["bg0"] + 1], None, ALU.mult)
                elif kind == "colsum":
                    dve.wait_ge(prep_done, g)
                    i = dve.tensor_tensor(deg_t, bk, deg_rows, ALU.add)
                elif kind == "diag":
                    dve.wait_ge(prep_done, g)
                    i = dve.scalar_tensor_tensor(out=deg_rows, in0=deg_t, scalar=1.0, in1=bk, op0=ALU.add,
                                                 op1=ALU.subtract)
                elif kind == "bg1":
                    i = dve.tensor_copy(bg1_all[:, :], bk[:, 0:P])
                elif kind == "tw":
                    i = dve.tensor_copy(tw.rearrange("p a b -> p (a b)"), bk)
                elif kind == "bnw":
                    i = split_lo(bn_wl[:, :, :].rearrange("p a b -> p (a b)"), bk,
                                 bn_wh[:, :, :].rearrange("p a b -> p (a b)"))
                else:
                    then(dve.tensor_copy(gat_v[:, :], bk[:, 0:2]))
                    then(dve.tensor_scalar(gat_v2[:, :], ones[:, :], gat_v[:, 1:2], None, ALU.mult))
                    then(dve.tensor_scalar(w_qk[:, :], bk[:, P:2 * P], float(D) ** -0.5, None, ALU.mult))
                    i = dve.tensor_copy(w_vo[:, :], bk[:, 2 * P:3 * P])
                i.then_inc(prep_done, 1)

            def gcn_step(st):
                if st.has(2):
                    b, r = st.b(2), st.ring(2, 2)
                    dve.wait_ge(gcn_agg_hi, b + 1)
                    dve.tensor_tensor(Gl[:, r, :], bank[r][:, :], Gh[:, r, :].bitcast(F32),
                                      ALU.subtract).then_inc(gcn_agg_split, 1)
                if st.has(0):
                    b, r = st.b(0), st.ring(0, 2)
                    if isinstance(st.j, int):
                        dve.wait_ge(in_x[st.j // 4], 64)
                    else:
                        for q in range(4):
                            dve.wait_ge(in_x[q], 64)
                    ln_stats(dve, st, 0, 0)
                if st.has(3):
                    b, r = st.b(3), st.ring(3, 2)
                    dve.wait_ge(gcn_z, b + 1)
                    dve.tensor_tensor(T1[:, r, :], bank[2 + r][:, :], bias_deg, ALU.add).then_inc(gcn_z_sum, 1)
                if st.has(4):
                    b, r = st.b(4), st.ring(4, 2)
                    dve.wait_ge(gcn_y, b + 1)
                    dve.tensor_tensor(T2[:, r, :].rearrange("p (a b) -> p a b", b=P),
                                      bank[4 + r][:, :].rearrange("p (a b) -> p a b", b=P),
                                      bg1_all[:, None, :].to_broadcast([P, CH, P]), ALU.add).then_inc(gcn_y_sum, 1)
                if st.has(1):
                    b, r = st.b(1), st.ring(1, 2)
                    dve.wait_ge(ln_normed, b + 1)
                    if st.from_(1, 2):
                        dve.wait_ge(gcn_agg, b - 1)
                    dve.tensor_copy(Hh[:, r, :, :], N[:, r, :, :]).then_inc(gcn_hh, 1)
                    dve.wait_ge(gcn_hh, b + 1)
                    dve.tensor_tensor(Hl[:, r, :, :], N[:, r, :, :], Hh[:, r, :, :].bitcast(F32),
                                      ALU.subtract).then_inc(gcn_h, 1)
                if st.has(3):
                    b, r = st.b(3), st.ring(3, 2)
                    dve.wait_ge(gcn_z_hi, b + 1)
                    dve.scalar_tensor_tensor(out=Zl[:, r, :], in0=T1[:, r, :], scalar=0.0,
                                             in1=Zh[:, r, :].bitcast(F32), op0=ALU.max,
                                             op1=ALU.subtract).then_inc(gcn_z_split, 1)
                if st.has(4):
                    b, r = st.b(4), st.ring(4, 2)
                    dve.wait_ge(gcn_y_hi, b + 1)
                    dve.tensor_tensor(Yl[:, r, :, :].rearrange("p a b -> p (a b)"), T2[:, r, :],
                                      Yh[:, r, :, :].rearrange("p a b -> p (a b)").bitcast(F32),
                                      ALU.subtract).then_inc(gcn_y_split, 1)
                if st.has(5):
                    b = st.b(5)
                    dve.wait_ge(gcn_o_hi, b + 1)
                    dve.scalar_tensor_tensor(out=colb(Cl, b), in0=bank[6][:, :], scalar=0.0,
                                             in1=colb(Ch, b).bitcast(F32), op0=ALU.max,
                                             op1=ALU.subtract).then_inc(gcn_o_split, 1)
            pipeline(dve, 6, 2, 5, gcn_step)

            for c in range(CH):
                i = dve.tensor_tensor(diag_blocks[:, c, :], A[:, c, c * P:(c + 1) * P], ident[:, :], ALU.add)
            i.then_inc(diag_ready, 1)
            for i_, kind in enumerate(LATE):
                g = G0 + i_
                bk = bank[i_ % 8][:, :]
                if kind == "deg":
                    dve.wait_ge(prep_mm, g + 1)
                    dve.tensor_copy(deg[:, :], bk.rearrange("p (c q) -> p c q", q=P)[:, :, 0]).then_inc(deg_ready, 1)
                    dve.wait_ge(dinv_ready, 1)
                    for c in range(CH):
                        i = dve.tensor_scalar(Th[:, 0, c * P:(c + 1) * P], ones[:, :], dinv[:, c:c + 1], None, ALU.mult)
                    i.then_inc(dinv_col, 1)
                    i = dve.tensor_copy(s1[:, 0:1], dinv[:, 0:1])
                elif kind == "dinv":
                    dve.wait_ge(prep_mm, g + 1)
                    i = dve.tensor_copy(dinv_all, bk)
                elif kind == "ahat":
                    c = i_ - 2
                    dve.wait_ge(prep_mm, g + 1)
                    dve.wait_ge(prep_done, g)
                    th = Th[:, (c + 1) % 2, :]
                    dve.scalar_tensor_tensor(out=th, in0=bk, scalar=dinv[:, c:c + 1], in1=dinv_all,
                                             op0=ALU.mult, op1=ALU.mult).then_inc(ahat_tmp, 1)
                    i = split_lo(Atl[:, c, :], th, Ath[:, c, :])
                elif kind == "wih":
                    i = split_lo(WXl[:, i_ - 6, :], bk, WXh[:, i_ - 6, :], 1.0 if i_ == 6 else 0.5)
                else:
                    i = split_lo(WHl[:, i_ - 10, :], bk, WHh[:, i_ - 10, :], 0.5)
                i.then_inc(prep_done, 1)
            dve.tensor_scalar(A[:, :, :], A[:, :, :], 0.0, NEG, ALU.is_equal, ALU.mult).then_inc(mask_ready, 1)

            def lstm_pair(p, r):
                def cell(s, k):
                    q = SUB[p] + (r * p + s) * 2 + k
                    ti, tg, tf = (tile_view(TG[:, k, g, :], p) for g in (0, 2, 1))
                    cc = tile_view(CC[:, k, :], p)
                    dve.wait_ge(cell_gates, q + 1)
                    if s == 0:
                        dve.scalar_tensor_tensor(out=cc, in0=ti, scalar=1.0, in1=tg, op0=ALU.add,
                                                 op1=ALU.mult).then_inc(cell_new, 1)
                        return
                    ta, tb = tile_view(TA, p), tile_view(TB, p)
                    dve.scalar_tensor_tensor(out=ta, in0=ti, scalar=1.0, in1=tg, op0=ALU.add, op1=ALU.mult)
                    dve.scalar_tensor_tensor(out=tb, in0=tf, scalar=1.0, in1=cc, op0=ALU.add,
                                             op1=ALU.mult).then_inc(cell_parts, 1)
                    dve.wait_ge(cell_parts, PARTS[p] + (r * (p - 1) + s - 1) * 2 + k + 1)
                    dve.scalar_tensor_tensor(out=cc, in0=tb, scalar=0.5, in1=ta, op0=ALU.mult,
                                             op1=ALU.add).then_inc(cell_new, 1)

                def h_out(s, k):
                    q = SUB[p] + (r * p + s) * 2 + k
                    dve.wait_ge(all_gates, q + 1)
                    dve.wait_ge(cell_tanh, q + 1)
                    hf = tile_view(HF[:, k, :], p)
                    dve.scalar_tensor_tensor(out=hf, in0=tile_view(TG[:, k, 3, :], p), scalar=1.0,
                                             in1=tile_view(TC[:, k, :], p), op0=ALU.add,
                                             op1=ALU.mult).then_inc(h_full, 1)
                    if s < p - 1:
                        dh, dl = tile_view(STh[:, k, :], p), tile_view(STl[:, k, :], p)
                    else:
                        dh, dl = col_view(Ch, p, r, k, s), col_view(Cl, p, r, k, s)
                    dve.wait_ge(h_full, q + 1)
                    dve.tensor_copy(dh, hf).then_inc(h_hi, 1)
                    dve.wait_ge(h_hi, q + 1)
                    dve.tensor_tensor(dl, hf, dh.bitcast(F32), ALU.subtract).then_inc(h_split, 1)
                for s in range(p):
                    for k in range(2):
                        cell(s, k)
                        if p > 1:
                            h_out(s, k)
                        elif k == 1:
                            h_out(0, 0)
                            h_out(0, 1)
            PARTS = {1: 0}
            for p in range(1, SKIP + 1):
                PARTS[p + 1] = PARTS[p] + lstm_units(p)[2] * 2 * (p - 1)
            lstm_loop(dve, lstm_pair)

            def xb(b):
                return X[:, bass.ds(b, 1), :, :].rearrange("p o c d -> p (o c d)")

            def pt_copy(st, c, s, bk):
                b = st.b(2)
                dve.wait_ge(s["pt_mm"], 4 * b + c + 1)
                if c == 1 and st.from_(2, 1):
                    dve.wait_ge(s["ag_mm"], b)
                m = CH if s is gat else c + 1
                dve.tensor_copy(PT[:, 0:m, c * P:(c + 1) * P],
                                bank[bk + 1][:, 0:m * P].rearrange("p (a b) -> p a b", b=P)).then_inc(s["pt_dve"], 1)

            def add_out(st, s):
                b, r = st.b(3), st.ring(3, 2)
                dve.reciprocal(rden[:, :], den[:, r, :]).then_inc(s["rden"], 1)
                dve.wait_ge(s["rden"], b + 1)
                dve.wait_ge(s["out_mm"], b + 1)
                for c in range(CH):
                    xc = X[:, bass.ds(b, 1), c, :].rearrange("p o d -> p (o d)")
                    i = dve.scalar_tensor_tensor(out=xc, in0=bank[7][:, c * P:(c + 1) * P], scalar=rden[:, c:c + 1],
                                                 in1=xc, op0=ALU.mult, op1=ALU.add)
                i.then_inc(s["final"], 1)

            def gat_step(st):
                if st.has(2):
                    b, r = st.b(2), st.ring(2, 2)
                    dve.wait_ge(gat["proj"], b + 1)
                    if st.from_(2, 1):
                        dve.wait_ge(gat["exp"], 4 * b)
                    dve.tensor_copy(s1[:, :], bank[3][:, 0:CH]).then_inc(gat["s1"], 1)
                    dve.wait_ge(gat["s1"], b + 1)
                    dve.tensor_scalar(s1x[:, :], s1[:, :], 1.0 - SLOPE, None, ALU.mult).then_inc(gat["s1_8"], 1)
                    apart(dve)
                    for c in range(CH):
                        dve.tensor_tensor_reduce(U[:, c, :], bank[2][:, :], A[:, c, :], 1.0, NEG, ALU.add,
                                                 ALU.max, top[:, c:c + 1]).then_inc(gat["u"], 1)
                    dve.wait_ge(gat["u"], 4 * b + 4)
                    dve.tensor_tensor(e_top[:, :], top[:, :], s1[:, :], ALU.add).then_inc(gat["e_top"], 1)
                    dve.wait_ge(gat["e_top"], b + 1)
                    dve.scalar_tensor_tensor(out=l_top[:, :], in0=e_top[:, :], scalar=SLOPE, in1=e_top[:, :],
                                             op0=ALU.mult, op1=ALU.max).then_inc(gat["l_top"], 1)
                    dve.wait_ge(gat["l_top"], b + 1)
                    dve.scalar_tensor_tensor(out=soft_b[:, r, :], in0=s1[:, :], scalar=SLOPE, in1=l_top[:, :],
                                             op0=ALU.mult, op1=ALU.subtract).then_inc(gat["bias"], 1)
                if st.has(0):
                    b = st.b(0)
                    dve.wait_ge(gat["t1"], b + 1)
                    dve.scalar_tensor_tensor(out=xb(b), in0=bank[0][:, :], scalar=0.5, in1=xb(b), op0=ALU.mult,
                                             op1=ALU.add).then_inc(gat["x_new"], 1)
                    dve.wait_ge(gat["x_new"], b + 1)
                    ln_stats(dve, st, 0, 1)
                if st.has(2):
                    b = st.b(2)
                    for c in range(CH):
                        dve.wait_ge(gat["relu"], 4 * b + c + 1)
                        dve.scalar_tensor_tensor(out=U[:, c, :], in0=U[:, c, :], scalar=SLOPE, in1=R[:, c, :],
                                                 op0=ALU.mult, op1=ALU.add).then_inc(gat["v"], 1)
                if st.has(3):
                    add_out(st, gat)
                if st.has(2):
                    pt_copy(st, 1, gat, 4)
                    pt_copy(st, 3, gat, 4)
            dve.wait_ge(h_split, SUB[SKIP + 1])
            pipeline(dve, 4, 4, 3, gat_step)

            def l2_step(st):
                if st.has(0):
                    ln_stats(dve, st, 0, 2)
                if st.has(2):
                    b, r = st.b(2), st.ring(2, 2)
                    dve.wait_ge(l2_agg_hi, b + 1)
                    dve.tensor_tensor(colb(Cl, b), bank[r][:, :], colb(Ch, b).bitcast(F32),
                                      ALU.subtract).then_inc(l2_agg_split, 1)
                if st.has(1):
                    b, r = st.b(1), st.ring(1, 2)
                    dve.wait_ge(ln_normed, 2 * NB + b + 1)
                    if st.from_(1, 2):
                        dve.wait_ge(l2_agg, b - 1)
                    dve.tensor_copy(Nh[:, r, :, :], N[:, r, :, :]).then_inc(l2_hi, 1)
                    dve.wait_ge(l2_hi, b + 1)
                    dve.tensor_tensor(Nl[:, r, :, :], N[:, r, :, :], Nh[:, r, :, :].bitcast(F32),
                                      ALU.subtract).then_inc(l2_split, 1)
                if st.has(3):
                    b, r = st.b(3), st.ring(3, 2)
                    dve.wait_ge(l2_z, b + 1)
                    apart(dve)
                    for h in range(HALVES):
                        i = dve.bn_stats(bst1[:, h, bass.ds(b, 1), :].rearrange("p o s -> p (o s)"),
                                         bank[2 + 2 * r + h][:, :])
                    i.then_inc(l2_zstats, 1)
            dve.wait_ge(gat["final"], NB)
            pipeline(dve, 6, 2, 3, l2_step)

            def bn_params(lo, hi_, gain, beta, bias, k):
                w = slice(lo, hi_)
                then(dve.tensor_scalar(bve[:, w], bmv[:, w, 1], 1.0, EPS, ALU.mult, ALU.add))
                then(dve.tensor_tensor(bmb[:, w], bmv[:, w, 0], bias, ALU.add))
                dve.tensor_tensor(bsh[:, w], bias, bmb[:, w], ALU.subtract).then_inc(bn_var, 1)
                dve.wait_ge(bn_var, k)
                dve.wait_ge(bn_rs, k)
                then(dve.tensor_tensor(bsc[:, w], brs[:, w], gain, ALU.mult))
                then(dve.tensor_tensor(bms[:, w], bsh[:, w], bsc[:, w], ALU.mult))
                dve.tensor_tensor(bbi[:, w], bms[:, w], beta, ALU.add).then_inc(bn_ready, 1)

            dve.wait_ge(l2_zstats, NB)
            for h in range(HALVES):
                then(dve.bn_aggr(bmv[:, h, :], bst1[:, h, :, :].rearrange("p b s -> p (b s)")))
            bn_params(0, 2, V[:, COL["g1"]:COL["g1"] + 2], V[:, COL["be1"]:COL["be1"] + 2],
                      V[:, COL["b1"]:COL["b1"] + 2], 1)

            def l2b_step(st):
                if st.has(0):
                    b, r = st.b(0), st.ring(0, 2)
                    dve.wait_ge(l2_relu, b + 1)
                    if st.from_(0, 2):
                        dve.wait_ge(l2_o, b - 1)
                    dve.tensor_copy(Rh[:, r, :, :], RZ[:, r, :, :]).then_inc(l2_r_hi, 1)
                    dve.wait_ge(l2_r_hi, b + 1)
                    dve.tensor_tensor(Rl[:, r, :, :], RZ[:, r, :, :], Rh[:, r, :, :].bitcast(F32),
                                      ALU.subtract).then_inc(l2_r_split, 1)
                if st.has(1):
                    b, r = st.b(1), st.ring(1, 2)
                    dve.wait_ge(l2_o_hi, b + 1)
                    apart(dve)
                    dve.bn_stats(bst2[:, bass.ds(b, 1), :].rearrange("p o s -> p (o s)"),
                                 bank[4 + r][:, :]).then_inc(l2_o_stats, 1)
                    dve.tensor_tensor(colb(Cl, b), bank[4 + r][:, :], colb(Ch, b).bitcast(F32),
                                      ALU.subtract).then_inc(l2_o_split, 1)
            pipeline(dve, 4, 2, 1, l2b_step)
            dve.wait_ge(l2_o_stats, NB)
            then(dve.bn_aggr(bmv[:, 2, :], bst2[:, :, :].rearrange("p b s -> p (b s)")))
            bn_params(2, 3, V[:, COL["g2"]:COL["g2"] + 1], V[:, COL["be2"]:COL["be2"] + 1],
                      V[:, COL["b2"]:COL["b2"] + 1], 2)

            def att_step(st):
                if st.has(2):
                    b, r = st.b(2), st.ring(2, 2)
                    for c in range(CH):
                        w = (c + 1) * P
                        dve.wait_ge(att["sc"], 4 * b + c + 1)
                        if st.from_(2, 1):
                            dve.wait_ge(att["pt_mm"], 4 * b - 3 + c)
                        apart(dve)
                        dve.tensor_tensor_reduce(U[:, c, 0:w], bank[3 + c % 2][:, 0:w], A[:, c, 0:w], 1.0, NEG,
                                                 ALU.add, ALU.max, top[:, c:c + 1]).then_inc(att["u"], 1)
                    dve.wait_ge(att["u"], 4 * b + 4)
                    if st.from_(2, 2):
                        dve.wait_ge(att["exp"], 4 * b - 4)
                    dve.tensor_scalar(soft_b[:, r, :], top[:, :], -1.0, None, ALU.mult).then_inc(att["bias"], 1)
                if st.has(0):
                    b = st.b(0)
                    dve.wait_ge(att["t1"], b + 1)
                    dve.tensor_tensor(xb(b), bank[0][:, :], xb(b), ALU.add).then_inc(att["x_new"], 1)
                    dve.wait_ge(att["x_new"], b + 1)
                    ln_stats(dve, st, 0, 3)
                if st.has(3):
                    add_out(st, att)
                if st.has(2):
                    pt_copy(st, 1, att, 5)
                    pt_copy(st, 3, att, 5)
            dve.wait_ge(causal_ready, CH)
            pipeline(dve, 4, 4, 3, att_step)


INPUTS = ["x", "adj", "L0_gnn_Wg0", "L0_gnn_bg0", "L0_gnn_Wg1", "L0_gnn_bg1", "L0_gnn_Wih", "L0_gnn_Whh",
          "L0_gnn_bih", "L0_gnn_bhh", "L1_gnn_W", "L1_gnn_a", "L2_gnn_W1", "L2_gnn_b1", "L2_gnn_g1", "L2_gnn_be1",
          "L2_gnn_W2", "L2_gnn_b2", "L2_gnn_g2", "L2_gnn_be2", "L3_gnn_Wqkv", "L3_gnn_Wo"]


def kernel(**inputs):
    import numpy as np
    import concourse.bacc as bacc
    from concourse.bass_utils import run_bass_kernel_spmd

    nc = bacc.Bacc("TRN2", target_bir_lowering=False, num_devices=1)
    arrays, args = {}, []
    for name in INPUTS:
        a = np.ascontiguousarray(inputs[name])
        arrays[f"in_{name}"] = a
        args.append(nc.dram_tensor(f"in_{name}", a.shape, mybir.dt.from_np(a.dtype), kind="ExternalInput").ap())
    args.append(nc.dram_tensor("out_x", (NB, T, D), F32, kind="ExternalOutput").ap())
    program(nc, *args)
    r = run_bass_kernel_spmd(nc, [arrays], core_ids=[0])
    return r.results[0]["out_x"]
```

```python
from contextlib import ExitStack

import concourse.bass as bass
from concourse import mybir

F32 = mybir.dt.float32
F32R = mybir.dt.float32r
ALU = mybir.AluOpType
ACT = mybir.ActivationFunctionType

P = 128
NB, T, D = 16, 512, 128
CH = T // P
SKIP = 4
HALVES = 2
EPS = 1e-5
NEG = -1e30
SLOPE = 0.2

VECS = [("bih", 16), ("bg0", 1), ("b1", 2), ("g1", 2), ("be1", 2), ("b2", 1), ("g2", 1), ("be2", 1), ("a", 2)]
COL, _at = {}, 0
for _name, _n in VECS:
    COL[_name] = _at
    _at += _n
NVEC = _at
BHH_COL = 32


class Step:

    def __init__(self, j, slot):
        self.j, self.slot = j, slot

    def has(self, lag):
        return not isinstance(self.j, int) or 0 <= self.j - lag < NB

    def b(self, lag):
        return self.j - lag

    def ring(self, lag, n):
        return (self.slot - lag) % n

    def from_(self, lag, n):
        return not isinstance(self.j, int) or self.j - lag >= n


def pipeline(eng, start, unroll, lags, step):
    for j in range(start):
        step(Step(j, j))
    with eng.Fori(0, (NB - start) // unroll) as i:
        for k in range(unroll):
            step(Step(i * unroll + (start + k), start + k))
    for j in range(NB, NB + lags):
        step(Step(j, j))


def program(nc, x, adj, Wg0, bg0, Wg1, bg1, Wih, Whh, bih, bhh, gat_W, gat_a,
            W1, b1, g1, be1, W2, b2, g2, be2, Wqkv, Wo, out):
    ctx = ExitStack()
    with ctx:
        def sb(name, shape, dt=F32):
            return ctx.enter_context(nc.sbuf_tensor(name, shape, dt))

        def sem(name):
            return ctx.enter_context(nc.semaphore(name))

        bank = [ctx.enter_context(nc.psum_tensor(f"bank{i}", [P, 512], F32)) for i in range(8)]

        X = sb("x_stream", [P, NB, CH, D])
        A = sb("adj_rows", [P, CH, T])
        Ath = sb("adjT_hi", [P, CH, T], F32R)
        Atl = sb("adjT_lo", [P, CH, T], F32R)
        Ch = sb("col_hi", [P, NB, T], F32R)
        Cl = sb("col_lo", [P, NB, T], F32R)
        ident = sb("ident", [P, P])
        ones = sb("ones", [P, P])
        ones_r = sb("ones_r", [P, P], F32R)
        bg1_row = sb("bg1_row", [1, P])
        V = sb("vec_cols", [P, 48])
        lstm_bias = sb("lstm_bias", [P, SKIP, 4])
        gcn_wh = sb("gcn_wh", [P, 2, P], F32R)
        gcn_wl = sb("gcn_wl", [P, 2, P], F32R)
        gat_w = sb("gat_w", [P, P])
        bn_wh = sb("bn_wh", [P, 4, P], F32R)
        bn_wl = sb("bn_wl", [P, 4, P], F32R)
        wo32 = sb("wo32", [P, P])
        gat_v = sb("gat_v", [P, 2])
        gat_v2 = sb("gat_v2", [P, P])
        w_qk = sb("w_qk", [P, P])
        w_vo = sb("w_vo", [P, P])
        bg1_all = sb("bg1_all", [P, P])
        deg = sb("deg", [P, CH])
        dinv = sb("dinv", [P, CH])
        stats = sb("ln_stats", [P, 2, CH, 6])
        rstd = sb("ln_rstd", [P, 2, CH])
        nbias = sb("ln_bias", [P, 2, CH])
        pad = sb("pad", [1, 32])
        neg_half, d_eps = sb("neg_half", [P, CH]), sb("d_eps", [P, CH])
        quarter_d, sqrt_d = sb("quarter_d", [P, CH]), sb("sqrt_d", [P, CH])
        ln_d, ln_s, ln_q, ln_dd = (sb(f"ln_{k}", [P, CH]) for k in ("diff", "sum", "vars", "diff2"))
        ln_m, ln_qe, ln_dq, ln_v, ln_p = (sb(f"ln_{k}", [P, CH]) for k in ("mean", "vars_eps", "quarter", "dvar", "root"))
        s1 = sb("gat_s1", [P, CH])
        s1x = sb("gat_s1x", [P, CH])
        top = sb("row_top", [P, CH])
        e_top = sb("gat_e_top", [P, CH])
        l_top = sb("gat_l_top", [P, CH])
        soft_b = sb("soft_bias", [P, 2, CH])
        den = sb("soft_den", [P, 2, CH])
        rden = sb("soft_rden", [P, CH])
        bst1 = sb("bn1_stats", [P, HALVES, NB, 6])
        bst2 = sb("bn2_stats", [P, NB, 6])
        bmv = sb("bn_mean_var", [P, 3, 2])
        bve = sb("bn_var_eps", [P, 3])
        brs = sb("bn_rstd", [P, 3])
        bsc = sb("bn_scale", [P, 3])
        bmb = sb("bn_mean_b", [P, 3])
        bsh = sb("bn_shift", [P, 3])
        bms = sb("bn_shift_scaled", [P, 3])
        bbi = sb("bn_bias", [P, 3])

        SR = sb("scratch_r", [P, 8192], F32R)
        SF = sb("scratch_f", [P, 9728])

        def carve(t, at, *dims):
            n = 1
            for d in dims:
                n *= d
            v = t[:, at:at + n]
            names = "abcd"[:len(dims)]
            if len(dims) > 1:
                v = v.rearrange(f"p ({' '.join(names)}) -> p {' '.join(names)}",
                                **{c: d for c, d in zip(names, dims)})
            return v

        Hh, Hl = carve(SR, 0, 2, CH, D), carve(SR, 1024, 2, CH, D)
        Gh, Gl = carve(SR, 2048, 2, T), carve(SR, 3072, 2, T)
        Zh, Zl = carve(SR, 4096, 2, T), carve(SR, 5120, 2, T)
        Yh, Yl = carve(SR, 6144, 2, CH, D), carve(SR, 7168, 2, CH, D)
        WXh, WXl = carve(SR, 0, SKIP, T), carve(SR, 2048, SKIP, T)
        WHh, WHl = carve(SR, 4096, SKIP - 1, T), carve(SR, 5632, SKIP - 1, T)
        STh = carve(SR, 7168, 2, T)
        STl = sb("state_lo", [P, 2, T], F32R)
        Nh, Nl = carve(SR, 0, 2, CH, D), carve(SR, 1024, 2, CH, D)
        Rh, Rl = carve(SR, 2048, 2, HALVES, T), carve(SR, 4096, 2, HALVES, T)

        N = carve(SF, 0, 4, CH, D)
        T1 = carve(SF, 2048, 2, T)
        T2 = carve(SF, 3072, 2, T)
        wih_rows = carve(SF, 4096, 16, P)
        whh_rows = carve(SF, 6144, 12, P)
        diag_blocks = carve(SF, 7680, CH, P)
        deg_rows = carve(SF, 8192, T)
        deg_t = carve(SF, 3072, T)
        dinv_all = carve(SF, 8704, T)
        Th = carve(SF, 2048, 2, T)
        gcn_w32 = carve(SF, 2048, 2, P)
        vec_rows = carve(SF, 2304, P)
        bhh_rows = carve(SF, 2432, P)
        bias_deg = carve(SF, 9216, T)
        stage_w = carve(SF, 1024, 8, P)
        tw = stage_w[:, 0:4, :]
        TG = carve(SF, 0, 2, 4, T)
        CC = carve(SF, 4096, 2, T)
        TC = carve(SF, 5120, 2, T)
        HF = carve(SF, 6144, 2, T)
        TA = carve(SF, 7168, T)
        TB = carve(SF, 7680, T)
        HT = carve(SF, 2048, T)
        AG = carve(SF, 2560, T)
        U = carve(SF, 3072, 2, CH, T)
        PT = carve(SF, 7168, CH, T)
        NT = carve(SF, 9216, T)
        OS = carve(SF, 9216, T)
        NTh, NTl = carve(SR, 0, 2, T), carve(SR, 1024, 2, T)
        QTh, QTl = carve(SR, 2048, 2, T), carve(SR, 3072, 2, T)
        w_qkh, w_qkl = carve(SR, 4096, P), carve(SR, 4224, P)
        RZ = carve(SF, 2048, 2, HALVES, T)

        in_adj, in_vec, in_gcn_w, in_small = sem("in_adj"), sem("in_vec"), sem("in_gcn_w"), sem("in_small")
        in_lstm = sem("in_lstm")
        in_x = [sem(f"in_x{i}") for i in range(4)]
        in_adj2 = sem("in_adj2")
        consts = sem("consts")
        pool_chain = sem("pool_chain")
        dve_chain = sem("dve_chain")
        diag_ready = sem("diag_ready")
        prep_mm = sem("prep_mm")
        prep_hi = sem("prep_hi")
        prep_done = sem("prep_done")
        deg_ready, dinv_ready, dinv_col = sem("deg_ready"), sem("dinv_ready"), sem("dinv_col")

        ln_stats_done = sem("ln_stats_done")
        ln_sums, ln_square, ln_quarter = sem("ln_sums"), sem("ln_square"), sem("ln_quarter_done")
        ln_dvar, ln_root, ln_rstd = sem("ln_dvar_done"), sem("ln_root_done"), sem("ln_rstd_done")
        ln_scale_ready = sem("ln_scale_ready")
        ln_normed = sem("ln_normed")

        pads = []

        def apart(dve):
            pads.append(len(pads) % 32)
            dve.memset(pad[0:1, pads[-1]:pads[-1] + 1], 0.0)

        def ln_stats(dve, st, lag, nth):
            b, r = st.b(lag), st.ring(lag, 2)
            n = nth * NB + b
            if nth or st.from_(lag, 2):
                dve.wait_ge(ln_sums, n - 1)
            apart(dve)
            for c in range(CH):
                i = dve.bn_stats(stats[:, r, c, :], X[:, bass.ds(b, 1), c, :].rearrange("p o d -> p (o d)"))
            i.then_inc(ln_stats_done, 1)

        def ln_scale(pool, st, lag, nth):
            b, r = st.b(lag), st.ring(lag, 2)
            n = nth * NB + b
            me, vc_e, mo, vc_o = (stats[:, r, :, i] for i in (1, 2, 4, 5))
            pool.wait_ge(ln_stats_done, n + 1)
            pool.tensor_tensor(ln_d[:, :], me, mo, ALU.subtract)
            pool.tensor_tensor(ln_s[:, :], me, mo, ALU.add)
            pool.tensor_tensor(ln_q[:, :], vc_e, vc_o, ALU.add).then_inc(ln_sums, 1)
            pool.wait_ge(ln_sums, n + 1)
            pool.tensor_tensor(ln_dd[:, :], ln_d[:, :], ln_d[:, :], ALU.mult)
            pool.tensor_tensor(ln_m[:, :], ln_s[:, :], neg_half[:, :], ALU.mult)
            pool.tensor_tensor(ln_qe[:, :], ln_q[:, :], d_eps[:, :], ALU.add).then_inc(ln_square, 1)
            pool.wait_ge(ln_square, n + 1)
            pool.tensor_tensor(ln_dq[:, :], ln_dd[:, :], quarter_d[:, :], ALU.mult).then_inc(ln_quarter, 1)
            pool.wait_ge(ln_quarter, n + 1)
            pool.tensor_tensor(ln_v[:, :], ln_dq[:, :], ln_qe[:, :], ALU.add).then_inc(ln_dvar, 1)
            pool.wait_ge(ln_dvar, n + 1)
            pool.tensor_tensor(ln_p[:, :], ln_v[:, :], neg_half[:, :], ALU.pow).then_inc(ln_root, 1)
            pool.wait_ge(ln_root, n + 1)
            if nth or st.from_(lag, 2):
                pool.wait_ge(ln_normed, n - 1)
            pool.tensor_tensor(rstd[:, r, :], ln_p[:, :], sqrt_d[:, :], ALU.mult).then_inc(ln_rstd, 1)
            pool.wait_ge(ln_rstd, n + 1)
            pool.tensor_tensor(nbias[:, r, :], ln_m[:, :], rstd[:, r, :], ALU.mult).then_inc(ln_scale_ready, 1)

        def ln_apply(act, st, lag, nth, ring):
            b, r = st.b(lag), st.ring(lag, 2)
            n = nth * NB + b
            act.wait_ge(ln_scale_ready, n + 1)
            for c in range(CH):
                i = act.activation(N[:, st.ring(lag, ring), c, :],
                                   X[:, bass.ds(b, 1), c, :].rearrange("p o d -> p (o d)"),
                                   ACT.Relu, bias=nbias[:, r, c:c + 1], scale=rstd[:, r, c:c + 1])
            i.then_inc(ln_normed, 1)

        def product(pe, o, w, xv, first=True, last=True):
            pe.matmul(o, w[0], xv[0], start=first, stop=False)
            pe.matmul(o, w[0], xv[1], start=False, stop=False)
            return pe.matmul(o, w[1], xv[0], start=False, stop=last)

        def colb(t, b):
            return t[:, bass.ds(b, 1), :].rearrange("p o t -> p (o t)")

        gcn_h = sem("gcn_h_split")
        gcn_agg, gcn_agg_hi, gcn_agg_split = sem("gcn_agg"), sem("gcn_agg_hi"), sem("gcn_agg_split")
        gcn_z, gcn_z_sum, gcn_z_hi, gcn_z_split = sem("gcn_z"), sem("gcn_z_sum"), sem("gcn_z_hi"), sem("gcn_z_split")
        gcn_y, gcn_y_sum, gcn_y_hi, gcn_y_split = sem("gcn_y"), sem("gcn_y_sum"), sem("gcn_y_hi"), sem("gcn_y_split")
        gcn_o, gcn_o_hi, gcn_o_split = sem("gcn_o"), sem("gcn_o_hi"), sem("gcn_o_split")
        gcn_hh = sem("gcn_h_hi")
        ahat_tmp = sem("ahat_tmp")
        gate_mm = sem("gate_mm")
        cell_gates = sem("cell_gates")
        all_gates = sem("all_gates")
        cell_parts = sem("cell_parts")
        cell_new = sem("cell_new")
        cell_tanh = sem("cell_tanh")
        h_full, h_hi, h_split = sem("h_full"), sem("h_hi"), sem("h_split")

        def attention_events(name, events):
            return {k: sem(f"{name}_{k}") for k in events.split()}

        gat = attention_events("gat", "col t1 x_new t2 nt proj s1 s1_8 u e_top l_top bias relu v exp pt_mm pt_dve pt_act ag_mm ag "
                        "out_mm rden final")
        att = attention_events("att", "bn_in col t1 x_new t2 nt_hi nt w_hi w_split proj qt_hi qt sc u bias exp pt_mm pt_dve pt_act ag_mm ag out_mm rden final")
        l2_hi, l2_split = sem("l2_h_hi"), sem("l2_h_split")
        l2_agg, l2_agg_hi, l2_agg_split = sem("l2_agg"), sem("l2_agg_hi"), sem("l2_agg_split")
        l2_z, l2_zstats = sem("l2_z"), sem("l2_z_stats")
        bn_chain, bn_var, bn_rs, bn_ready = sem("bn_chain"), sem("bn_var"), sem("bn_rs"), sem("bn_ready")
        l2_z2, l2_relu, l2_r_hi, l2_r_split = sem("l2_z2"), sem("l2_relu"), sem("l2_r_hi"), sem("l2_r_split")
        l2_o, l2_o_hi, l2_o_stats, l2_o_split = sem("l2_o"), sem("l2_o_hi"), sem("l2_o_stats"), sem("l2_o_split")
        causal_ready, mask_ready = sem("causal_ready"), sem("mask_ready")
        out_dma = sem("out_dma")

        block = ctx.enter_context(nc.Block())
        GATES = (0, 2, 1, 3)

        def lstm_units(p):
            nb = {1: 1, 2: 2, 3: 2, 4: 4}[p]
            return nb, T // p, NB // (2 * nb)

        SUB, GAT0 = {1: 0}, {1: 0}
        for _p in range(1, SKIP + 1):
            _r = lstm_units(_p)[2]
            SUB[_p + 1] = SUB[_p] + _r * _p * 2
            GAT0[_p + 1] = GAT0[_p] + _r * 2 * (4 * _p - 1)

        def lstm_walk(p, emit):
            R_ = lstm_units(p)[2]
            emit(0)
            return R_

        def col_view(t, p, r, k, s):
            nb, nw, _ = lstm_units(p)
            v = t[:, bass.ds((r * 2 + k) * nb, nb), 0:nw * p]
            return v.rearrange("q b (w s) -> q b w s", s=p)[:, :, :, s]

        def tile_view(v, p):
            nb, nw, _ = lstm_units(p)
            return v[:, 0:nb * nw].rearrange("q (b w) -> q b w", b=nb)

        def lstm_loop(eng, body):
            for p in range(1, SKIP + 1):
                R_ = lstm_units(p)[2]
                body(p, 0)
                if R_ == 2:
                    body(p, 1)
                else:
                    with eng.Fori(1, R_) as r:
                        body(p, r)

        SETUP = ["vec", "adj", "adj", "adj", "adj", "rowsum", "colsum", "diag", "bg1", "tw", "bnw", "fold"]
        G0 = len(SETUP)
        LATE = ["deg", "dinv"] + ["ahat"] * 4 + ["wih"] * 4 + ["whh"] * 3

        @block.sync
        def _(sp):
            sp.dma_start(A[:, :, :], adj.rearrange("(c p) s -> p c s", p=P)).then_inc(in_adj, 16)
            r = 0
            for ap, n in ((bih.rearrange("l (g d) -> (l g) d", d=P), 16), (bg0.rearrange("(o d) -> o d", o=1), 1),
                          (b1.rearrange("(o d) -> o d", o=2), 2), (g1.rearrange("(o d) -> o d", o=2), 2),
                          (be1.rearrange("(o d) -> o d", o=2), 2), (b2.rearrange("(o d) -> o d", o=1), 1),
                          (g2.rearrange("(o d) -> o d", o=1), 1), (be2.rearrange("(o d) -> o d", o=1), 1),
                          (gat_a.rearrange("(k o) u -> k (o u)", k=2), 2)):
                sp.dma_start(vec_rows[r:r + n, :], ap).then_inc(in_vec, 16)
                r += n
            sp.dma_start(bhh_rows[0:16, :], bhh.rearrange("l (g d) -> (l g) d", d=P)).then_inc(in_vec, 16)
            sp.dma_start(bg1_row[:, :], bg1.rearrange("(o d) -> o d", o=1)).then_inc(in_vec, 16)
            sp.dma_start(gcn_w32[:, 0, :], Wg0).then_inc(in_gcn_w, 16)
            sp.dma_start(gcn_w32[:, 1, :], Wg1).then_inc(in_gcn_w, 16)
            xv = x.rearrange("b (c p) d -> p b c d", p=P)
            for q in range(4):
                for b in range(4 * q, 4 * q + 4):
                    sp.dma_start(X[:, b, :, :], xv[:, b, :, :]).then_inc(in_x[q], 16)
                if q == 0:
                    sp.dma_start(gat_w[:, :], gat_W).then_inc(in_small, 16)
                    sp.dma_start(wo32[:, :], Wo).then_inc(in_small, 16)
                    sp.dma_start(stage_w[:, 0, :], gat_W).then_inc(in_small, 16)
                    sp.dma_start(stage_w[:, 4:6, :], W1.rearrange("(h p) d -> p h d", p=P)).then_inc(in_small, 16)
                    sp.dma_start(stage_w[:, 6:8, :], W2.rearrange("o (h d) -> o h d", h=2)).then_inc(in_small, 16)
                    sp.dma_start(stage_w[:, 1:4, :], Wqkv.rearrange("c (k d) -> c k d", k=3)).then_inc(in_small, 16)
            sp.dma_start(wih_rows[:, :, :], Wih.rearrange("l (g p) d -> p (l g) d", p=P)).then_inc(in_lstm, 16)
            sp.dma_start(whh_rows[:, :, :], Whh[1:SKIP].rearrange("l (g p) d -> p (l g) d", p=P)).then_inc(in_lstm, 16)
            sp.wait_ge(gat["final"], NB)
            sp.dma_start(A[:, :, :], adj.rearrange("(c p) s -> p c s", p=P)).then_inc(in_adj2, 16)
            ov = out.rearrange("b (c p) d -> p b c d", p=P)
            with sp.Fori(0, NB) as b:
                sp.wait_ge(att["final"], b + 1)
                sp.dma_start(ov[:, bass.ds(b, 1), :, :], X[:, bass.ds(b, 1), :, :]).then_inc(out_dma, 16)
            sp.wait_ge(out_dma, 16 * NB)

        @block.gpsimd
        def _(pool):
            pool.memset(ones[:, :], 1.0).then_inc(consts, 1)
            pool.memset(neg_half[:, :], -0.5).then_inc(consts, 1)
            pool.memset(d_eps[:, :], D * EPS).then_inc(consts, 1)
            pool.memset(quarter_d[:, :], D / 4).then_inc(consts, 1)
            pool.memset(sqrt_d[:, :], float(D) ** 0.5).then_inc(consts, 1)
            pool.wait_ge(consts, 1)
            pool.affine_select(out=ident[:, :], in_=ones[:, :], compare_op=ALU.is_equal, fill=0.0, base=0,
                               pattern=[[-1, P]], channel_multiplier=1).then_inc(consts, 1)
            pool.wait_ge(consts, 6)

            def gcn_step(st):
                if st.has(0):
                    ln_scale(pool, st, 0, 0)
            pipeline(pool, 2, 2, 0, gcn_step)
            pool.wait_ge(deg_ready, 1)
            pool.tensor_tensor(dinv[:, :], deg[:, :], neg_half[:, :], ALU.pow).then_inc(dinv_ready, 1)

            def gat_step(st):
                if st.has(0):
                    b = st.b(0)
                    if st.from_(0, 1):
                        pool.wait_ge(gat["t1"], b)
                    pool.tensor_tensor(HT, colb(Ch, b).bitcast(F32), colb(Cl, b).bitcast(F32),
                                       ALU.add).then_inc(gat["col"], 1)
                if st.has(1):
                    ln_scale(pool, st, 1, 1)
            pool.wait_ge(h_split, SUB[SKIP + 1])
            pipeline(pool, 4, 2, 1, gat_step)

            pipeline(pool, 2, 2, 0, lambda st: ln_scale(pool, st, 0, 2))

            pool.wait_ge(bn_var, 1)
            pool.tensor_tensor(brs[:, 0:2], bve[:, 0:2], neg_half[:, 0:2], ALU.pow).then_inc(bn_rs, 1)
            pool.wait_ge(in_adj2, 16)
            for c in range(CH):
                blk = A[:, c, c * P:(c + 1) * P]
                pool.affine_select(out=blk, in_=blk, compare_op=ALU.is_ge, fill=NEG, base=0,
                                   pattern=[[-1, P]], channel_multiplier=1).then_inc(causal_ready, 1)
            pool.wait_ge(bn_var, 2)
            pool.tensor_tensor(brs[:, 2:3], bve[:, 2:3], neg_half[:, 0:1], ALU.pow).then_inc(bn_rs, 1)

            def att_step(st):
                if st.has(0):
                    b = st.b(0)
                    if st.from_(0, 1):
                        pool.wait_ge(att["col"], b)
                    pool.tensor_tensor(OS, colb(Ch, b).bitcast(F32), colb(Cl, b).bitcast(F32),
                                       ALU.add).then_inc(att["bn_in"], 1)
                if st.has(1):
                    ln_scale(pool, st, 1, 3)
            pool.wait_ge(l2_o_split, NB)
            pipeline(pool, 4, 2, 1, att_step)

        @block.tensor
        def _(pe):
            pe.wait_ge(consts, 6)

            def transposes4(bk, srcs):
                for i, s in enumerate(srcs):
                    mm = pe.transpose(bank[bk][:, i * P:(i + 1) * P], s, ident[:, :])
                return mm

            for g, kind in enumerate(SETUP):
                bk = bank[g % 8]
                if g >= 8:
                    pe.wait_ge(prep_done, g - 7)
                if kind == "vec":
                    pe.wait_ge(in_vec, 16 * 11)
                    pe.transpose(bk[:, 0:NVEC], vec_rows[0:NVEC, :], ident[0:NVEC, 0:NVEC])
                    mm = pe.transpose(bk[:, BHH_COL:BHH_COL + 16], bhh_rows[0:16, :], ident[0:16, 0:16])
                elif kind == "adj":
                    c = g - 1
                    if c == 0:
                        pe.wait_ge(in_adj, 16)
                    mm = transposes4(g % 8, [A[:, t, c * P:(c + 1) * P] for t in range(CH)])
                elif kind == "rowsum":
                    pe.wait_ge(prep_done, 5)
                    for c in range(CH):
                        pe.matmul(bk[:, :], ones_r[:, :], Ath[:, c, :], start=(c == 0), stop=False)
                        mm = pe.matmul(bk[:, :], ones_r[:, :], Atl[:, c, :], start=False, stop=(c == CH - 1))
                elif kind == "colsum":
                    for c in range(CH):
                        mm = pe.matmul(bk[:, :], ones[:, :], A[:, c, :], start=(c == 0), stop=(c == CH - 1))
                elif kind == "diag":
                    pe.wait_ge(diag_ready, 1)
                    mm = pe.matmul(bk[:, :], ones[:, :], diag_blocks.rearrange("p a b -> p (a b)"),
                                   start=True, stop=True)
                elif kind == "bg1":
                    mm = pe.matmul(bk[:, 0:P], ones[0:1, :], bg1_row[:, :], start=True, stop=True)
                elif kind == "tw":
                    pe.wait_ge(in_small, 16 * 6)
                    mm = transposes4(g % 8, [stage_w[:, i, :] for i in range(4)])
                elif kind == "bnw":
                    mm = transposes4(g % 8, [stage_w[:, i, :] for i in range(4, 8)])
                else:
                    pe.wait_ge(prep_done, g)
                    pe.matmul(bk[:, 0:2], tw[:, 0, :], V[:, COL["a"]:COL["a"] + 2], start=True, stop=True)
                    pe.matmul(bk[:, P:2 * P], tw[:, 1, :], tw[:, 2, :], start=True, stop=True)
                    mm = pe.matmul(bk[:, 2 * P:3 * P], tw[:, 3, :], wo32[:, :], start=True, stop=True)
                mm.then_inc(prep_mm, 1)

            pe.wait_ge(prep_done, G0)

            def gcn_step(st):
                if st.has(2):
                    b, r = st.b(2), st.ring(2, 2)
                    pe.wait_ge(gcn_h, b + 1)
                    if st.from_(2, 2):
                        pe.wait_ge(gcn_agg_split, b - 1)
                    for c in range(CH):
                        mm = product(pe, bank[r][:, :], (Hh[:, r, c, :], Hl[:, r, c, :]), (Ath[:, c, :], Atl[:, c, :]),
                                     c == 0, c == CH - 1)
                    mm.then_inc(gcn_agg, 1)
                if st.has(3):
                    b, r = st.b(3), st.ring(3, 2)
                    pe.wait_ge(gcn_agg_split, b + 1)
                    if st.from_(3, 2):
                        pe.wait_ge(gcn_z_sum, b - 1)
                    product(pe, bank[2 + r][:, :], (gcn_wh[:, 0, :], gcn_wl[:, 0, :]),
                            (Gh[:, r, :], Gl[:, r, :])).then_inc(gcn_z, 1)
                if st.has(4):
                    b, r = st.b(4), st.ring(4, 2)
                    pe.wait_ge(gcn_z_split, b + 1)
                    if st.from_(4, 2):
                        pe.wait_ge(gcn_y_sum, b - 1)
                    for c in range(CH):
                        cs = slice(c * P, (c + 1) * P)
                        mm = product(pe, bank[4 + r][:, cs], (Zh[:, r, cs], Zl[:, r, cs]),
                                     (gcn_wh[:, 1, :], gcn_wl[:, 1, :]))
                    mm.then_inc(gcn_y, 1)
                if st.has(5):
                    b, r = st.b(5), st.ring(5, 2)
                    pe.wait_ge(gcn_y_split, b + 1)
                    if st.from_(5, 1):
                        pe.wait_ge(gcn_o_split, b)
                    for c in range(CH):
                        mm = product(pe, bank[6][:, :], (Yh[:, r, c, :], Yl[:, r, c, :]), (Ath[:, c, :], Atl[:, c, :]),
                                     c == 0, c == CH - 1)
                    mm.then_inc(gcn_o, 1)
            pipeline(pe, 6, 2, 5, gcn_step)

            pe.wait_ge(gcn_o_split, NB)
            pe.wait_ge(in_lstm, 32)
            for i, kind in enumerate(LATE):
                g = G0 + i
                if i >= 8:
                    pe.wait_ge(prep_done, g - 7)
                if kind == "deg":
                    mm = transposes4(i % 8, [deg_rows[:, c * P:(c + 1) * P] for c in range(CH)])
                elif kind == "dinv":
                    pe.wait_ge(dinv_col, 1)
                    mm = transposes4(i % 8, [Th[:, 0, c * P:(c + 1) * P] for c in range(CH)])
                elif kind == "ahat":
                    c = i - 2
                    pe.wait_ge(diag_ready, 2)
                    mm = transposes4(i % 8, [diag_blocks[:, c, :] if t == c else A[:, t, c * P:(c + 1) * P]
                                             for t in range(CH)])
                elif kind == "wih":
                    mm = transposes4(i % 8, [wih_rows[:, 4 * (i - 6) + k, :] for k in range(4)])
                else:
                    mm = transposes4(i % 8, [whh_rows[:, 4 * (i - 10) + k, :] for k in range(4)])
                mm.then_inc(prep_mm, 1)
            pe.wait_ge(prep_done, G0 + len(LATE))

            def lstm_pair(p, r):
                nb, nw, _ = lstm_units(p)
                if p > 1:
                    per = 2 * (p - 1) * nb // lstm_units(p - 1)[0]
                    pe.wait_ge(h_split, SUB[p - 1] + per * (r + 1))
                for s in range(p):
                    for k in range(2):
                        q = SUB[p] + (r * p + s) * 2 + k
                        if not (p == 1 and isinstance(r, int) and r == 0):
                            pe.wait_ge(all_gates, q - 1)
                        gates = [g for g in GATES if s > 0 or g != 1]
                        xs = (col_view(Ch, p, r, k, s), col_view(Cl, p, r, k, s))
                        for g in gates:
                            o = tile_view(bank[4 * k + g], p)
                            gs = slice(g * P, (g + 1) * P)
                            mm = product(pe, o, (WXh[:, p - 1, gs], WXl[:, p - 1, gs]), xs, True, s == 0)
                            if s == 0:
                                mm.then_inc(gate_mm, 1)
                        if s > 0:
                            pe.wait_ge(h_split, q - 1)
                            hs = (tile_view(STh[:, k, :], p), tile_view(STl[:, k, :], p))
                            for g in gates:
                                o = tile_view(bank[4 * k + g], p)
                                gs = slice(g * P, (g + 1) * P)
                                product(pe, o, (WHh[:, p - 2, gs], WHl[:, p - 2, gs]), hs, False,
                                        True).then_inc(gate_mm, 1)
            lstm_loop(pe, lstm_pair)

            def back_to_rows(st, s):
                b = st.b(0)
                pe.wait_ge(s["col"], b + 1)
                if st.from_(0, 1):
                    pe.wait_ge(s["x_new"], b)
                transposes4(0, [HT[:, c * P:(c + 1) * P] for c in range(CH)]).then_inc(s["t1"], 1)

            def rows_to_col(st, s, nth):
                b, r = st.b(1), st.ring(1, 4)
                pe.wait_ge(ln_normed, nth * NB + b + 1)
                if st.from_(1, 1):
                    pe.wait_ge(s["nt"], b)
                transposes4(1, [N[:, r, c, :] for c in range(CH)]).then_inc(s["t2"], 1)

            def attend(st, s):
                b, r = st.b(4), st.ring(4, 4)
                pe.wait_ge(s["pt_act"], 2 * b + 2)
                pe.wait_ge(s["pt_dve"], 2 * b + 2)
                if st.from_(4, 1):
                    pe.wait_ge(s["final"], b)
                for c in range(CH):
                    t0 = 0 if s is gat else c * P
                    mm = pe.matmul(bank[7][:, t0:T], N[:, r, c, :], PT[:, c, t0:T], start=(c == 0), stop=(c == CH - 1))
                mm.then_inc(s["ag_mm"], 1)

            def project_out(st, s, w):
                pe.wait_ge(s["ag"], st.b(4) + 1)
                for c in range(CH):
                    mm = pe.matmul(bank[7][:, c * P:(c + 1) * P], AG[:, c * P:(c + 1) * P], w, start=True, stop=True)
                mm.then_inc(s["out_mm"], 1)

            def probs_t(st, s, c, bk):
                b = st.b(3)
                pe.wait_ge(s["exp"], 4 * b + c + 1)
                if c >= 2:
                    pe.wait_ge(s["pt_act"] if c % 2 == 0 else s["pt_dve"], 2 * b + 1)
                elif st.from_(3, 1):
                    pe.wait_ge(s["pt_act"] if c % 2 == 0 else s["pt_dve"], 2 * b)
                n = CH if s is gat else c + 1
                transposes4(bk + c % 2, [U[:, st.ring(3, 2), c, i * P:(i + 1) * P] for i in range(n)]
                            ).then_inc(s["pt_mm"], 1)

            def gat_step(st):
                if st.has(0):
                    if st.from_(0, 2):
                        pe.wait_ge(gat["s1"], st.b(0) - 1)
                    back_to_rows(st, gat)
                if st.has(1):
                    rows_to_col(st, gat, 1)
                if st.has(4):
                    attend(st, gat)
                if st.has(3):
                    probs_t(st, gat, 0, 4)
                if st.has(4):
                    project_out(st, gat, gat_w[:, :])
                if st.has(3):
                    probs_t(st, gat, 1, 4)
                if st.has(1):
                    b, r = st.b(1), st.ring(1, 2)
                    pe.wait_ge(gat["nt"], b + 1)
                    if st.from_(1, 2):
                        pe.wait_ge(gat["u"], 4 * b - 4)
                    pe.matmul(bank[2 + r][:, :], gat_v2[:, :], NT, start=True, stop=True)
                    if st.has(0):
                        pe.wait_ge(gat["x_new"], b + 2)
                    for c in range(CH):
                        mm = pe.matmul(bank[0][:, c:c + 1], NT[:, c * P:(c + 1) * P], gat_v[:, 0:1],
                                       start=True, stop=True)
                    mm.then_inc(gat["proj"], 1)
                if st.has(3):
                    probs_t(st, gat, 2, 4)
                    probs_t(st, gat, 3, 4)
            pe.wait_ge(all_gates, SUB[SKIP + 1])
            pipeline(pe, 8, 4, 4, gat_step)

            def l2_step(st):
                if st.has(2):
                    b, r = st.b(2), st.ring(2, 2)
                    pe.wait_ge(l2_split, b + 1)
                    if st.from_(2, 2):
                        pe.wait_ge(l2_agg_split, b - 1)
                    for c in range(CH):
                        mm = product(pe, bank[r][:, :], (Nh[:, r, c, :], Nl[:, r, c, :]), (Ath[:, c, :], Atl[:, c, :]),
                                     c == 0, c == CH - 1)
                    mm.then_inc(l2_agg, 1)
                if st.has(3):
                    b, r = st.b(3), st.ring(3, 2)
                    pe.wait_ge(l2_agg_split, b + 1)
                    if st.from_(3, 2):
                        pe.wait_ge(l2_zstats, b - 1)
                    for h in range(HALVES):
                        mm = product(pe, bank[2 + 2 * r + h][:, :], (bn_wh[:, h, :], bn_wl[:, h, :]),
                                     (colb(Ch, b), colb(Cl, b)))
                    mm.then_inc(l2_z, 1)
            pe.wait_ge(gat["final"], NB)
            pipeline(pe, 6, 2, 3, l2_step)

            def l2b_step(st):
                if st.has(0):
                    b, r = st.b(0), st.ring(0, 2)
                    if st.from_(0, 2):
                        pe.wait_ge(l2_relu, b - 1)
                    for h in range(HALVES):
                        mm = product(pe, bank[2 * r + h][:, :], (bn_wh[:, h, :], bn_wl[:, h, :]),
                                     (colb(Ch, b), colb(Cl, b)))
                    mm.then_inc(l2_z2, 1)
                if st.has(1):
                    b, r = st.b(1), st.ring(1, 2)
                    pe.wait_ge(l2_r_split, b + 1)
                    if st.from_(1, 2):
                        pe.wait_ge(l2_o_split, b - 1)
                    for h in range(HALVES):
                        mm = product(pe, bank[4 + r][:, :], (bn_wh[:, 2 + h, :], bn_wl[:, 2 + h, :]),
                                     (Rh[:, r, h, :], Rl[:, r, h, :]), h == 0, h == HALVES - 1)
                    mm.then_inc(l2_o, 1)
            pe.wait_ge(l2_zstats, NB)
            pipeline(pe, 4, 2, 1, l2b_step)

            def att_step(st):
                def scores(c):
                    b, r = st.b(2), st.ring(2, 2)
                    w = (c + 1) * P
                    if c >= 2 or st.from_(2, 1):
                        pe.wait_ge(att["u"], 4 * b + c - 1)
                    q = slice(c * P, w)
                    product(pe, bank[3 + c % 2][:, 0:w], (QTh[:, r, q], QTl[:, r, q]),
                            (NTh[:, r, 0:w], NTl[:, r, 0:w])).then_inc(att["sc"], 1)

                if st.has(4):
                    attend(st, att)
                if st.has(0):
                    back_to_rows(st, att)
                if st.has(1):
                    rows_to_col(st, att, 3)
                if st.has(4):
                    project_out(st, att, w_vo[:, :])
                if st.has(2):
                    pe.wait_ge(att["qt"], st.b(2) + 1)
                    scores(0)
                    scores(1)
                if st.has(3):
                    probs_t(st, att, 0, 5)
                if st.has(1):
                    b, r = st.b(1), st.ring(1, 2)
                    pe.wait_ge(att["nt"], b + 1)
                    if st.from_(1, 1):
                        pe.wait_ge(att["qt"], b)
                    product(pe, bank[2][:, :], (w_qkh, w_qkl), (NTh[:, r, :], NTl[:, r, :])).then_inc(att["proj"], 1)
                if st.has(2):
                    scores(2)
                if st.has(3):
                    probs_t(st, att, 1, 5)
                if st.has(2):
                    scores(3)
                if st.has(3):
                    probs_t(st, att, 2, 5)
                    probs_t(st, att, 3, 5)
            pe.wait_ge(att["w_split"], 1)
            pe.wait_ge(l2_o_split, NB)
            pipeline(pe, 8, 4, 4, att_step)

        @block.scalar
        def _(act):
            act.wait_ge(consts, 6)
            act.activation(s1x[:, 0:1], ones[:, 0:1], ACT.Tanh)
            act.activation(ones_r[:, :], ones[:, :], ACT.Copy).then_inc(prep_hi, 1)
            act.wait_ge(in_gcn_w, 32)
            act.activation(gcn_wh[:, :, :], gcn_w32[:, :, :], ACT.Copy).then_inc(prep_hi, 1)

            def copy_hi(g, bk, dst, scale=1.0):
                act.wait_ge(prep_mm, g + 1)
                act.activation(dst, bank[bk][:, :], ACT.Copy, scale=scale).then_inc(prep_hi, 1)

            for g, kind in enumerate(SETUP):
                if kind == "adj":
                    copy_hi(g, g % 8, Ath[:, g - 1, :])
                elif kind == "bnw":
                    copy_hi(g, g % 8, bn_wh[:, :, :].rearrange("p a b -> p (a b)"))

            def gcn_step(st):
                if st.has(1):
                    b = st.b(1)
                    if st.from_(1, 2):
                        act.wait_ge(gcn_h, b - 1)
                    ln_apply(act, st, 1, 0, 2)
                if st.has(2):
                    b, r = st.b(2), st.ring(2, 2)
                    act.wait_ge(gcn_agg, b + 1)
                    if st.from_(2, 2):
                        act.wait_ge(gcn_z, b - 1)
                    act.activation(Gh[:, r, :], bank[r][:, :], ACT.Copy).then_inc(gcn_agg_hi, 1)
                if st.has(3):
                    b, r = st.b(3), st.ring(3, 2)
                    act.wait_ge(gcn_z_sum, b + 1)
                    if st.from_(3, 2):
                        act.wait_ge(gcn_y, b - 1)
                    act.activation(Zh[:, r, :], T1[:, r, :], ACT.Relu).then_inc(gcn_z_hi, 1)
                if st.has(4):
                    b, r = st.b(4), st.ring(4, 2)
                    act.wait_ge(gcn_y_sum, b + 1)
                    if st.from_(4, 2):
                        act.wait_ge(gcn_o, b - 1)
                    act.activation(Yh[:, r, :, :].rearrange("p a b -> p (a b)"), T2[:, r, :],
                                   ACT.Copy).then_inc(gcn_y_hi, 1)
                if st.has(5):
                    b = st.b(5)
                    act.wait_ge(gcn_o, b + 1)
                    act.activation(colb(Ch, b), bank[6][:, :], ACT.Relu).then_inc(gcn_o_hi, 1)
            pipeline(act, 6, 2, 5, gcn_step)

            act.wait_ge(gcn_o_split, NB)
            for i, kind in enumerate(LATE):
                g = G0 + i
                if kind == "ahat":
                    c = i - 2
                    act.wait_ge(ahat_tmp, c + 1)
                    act.activation(Ath[:, c, :], Th[:, (c + 1) % 2, :], ACT.Copy).then_inc(prep_hi, 1)
                elif kind == "wih":
                    copy_hi(g, i % 8, WXh[:, i - 6, :], 1.0 if i == 6 else 0.5)
                elif kind == "whh":
                    copy_hi(g, i % 8, WHh[:, i - 10, :], 0.5)

            def lstm_pair(p, r):
                def gates(s, k):
                    q = SUB[p] + (r * p + s) * 2 + k
                    order = [g for g in GATES if s > 0 or g != 1]
                    base = GAT0[p] + r * 2 * (4 * p - 1) + (k * 3 if s == 0 else 6 + (s - 1) * 8 + k * 4)
                    if not (p == 1 and isinstance(r, int) and r == 0):
                        act.wait_ge(h_full, q - 1)
                    for n, g in enumerate(order):
                        act.wait_ge(gate_mm, base + n + 1)
                        i = act.activation(tile_view(TG[:, k, g, :], p), tile_view(bank[4 * k + g], p), ACT.Tanh,
                                           bias=lstm_bias[:, p - 1, g:g + 1], scale=1.0 if g == 2 else 0.5)
                        if n == len(order) - 2:
                            i.then_inc(cell_gates, 1)
                    i.then_inc(all_gates, 1)

                def tanh_c(s, k):
                    q = SUB[p] + (r * p + s) * 2 + k
                    act.wait_ge(cell_new, q + 1)
                    act.activation(tile_view(TC[:, k, :], p), tile_view(CC[:, k, :], p), ACT.Tanh,
                                   scale=0.5).then_inc(cell_tanh, 1)
                for s in range(p):
                    for k in range(2):
                        gates(s, k)
                        if p > 1:
                            tanh_c(s, k)
                        elif k == 1:
                            tanh_c(0, 0)
                            tanh_c(0, 1)
            lstm_loop(act, lstm_pair)

            def pt_copy(st, c, s, bk):
                b = st.b(3)
                act.wait_ge(s["pt_mm"], 4 * b + c + 1)
                if c == 0 and st.from_(3, 1):
                    act.wait_ge(s["ag_mm"], b)
                n = CH if s is gat else c + 1
                act.activation(PT[:, 0:n, c * P:(c + 1) * P],
                               bank[bk][:, 0:n * P].rearrange("p (a b) -> p a b", b=P), ACT.Copy).then_inc(s["pt_act"], 1)

            def exp_row(st, c, s):
                b, r = st.b(3), st.ring(3, 2)
                w = T if s is gat else (c + 1) * P
                if c == 0:
                    act.wait_ge(s["bias"], b + 1)
                    if s is gat:
                        act.wait_ge(s["v"], 4 * b + 4)
                    if st.from_(3, 2):
                        act.wait_ge(s["rden"], b - 1)
                act.activation(U[:, r, c, 0:w], U[:, r, c, 0:w], ACT.Exp, bias=soft_b[:, r, c:c + 1],
                               accum_out=den[:, r, c:c + 1]).then_inc(s["exp"], 1)

            def attended(st, s):
                b = st.b(4)
                act.wait_ge(s["ag_mm"], b + 1)
                if st.from_(4, 1):
                    act.wait_ge(s["out_mm"], b)
                act.activation(AG, bank[7][:, :], ACT.Copy).then_inc(s["ag"], 1)

            def gat_step(st):
                def relu_part(c):
                    b = st.b(2)
                    if c == 0:
                        act.wait_ge(gat["s1_8"], b + 1)
                    act.wait_ge(gat["u"], 4 * b + c + 1)
                    if c >= 1 or st.from_(2, 1):
                        act.wait_ge(gat["v"], 4 * b + c)
                    act.activation(bank[6][:, :], U[:, st.ring(2, 2), c, :], ACT.Relu, bias=s1x[:, c:c + 1],
                                   scale=1.0 - SLOPE).then_inc(gat["relu"], 1)

                for c in range(CH):
                    if st.has(3):
                        exp_row(st, c, gat)
                    if st.has(2):
                        relu_part(c)
                    if st.has(4) and c == 2:
                        attended(st, gat)
                    if st.has(1) and c == 0:
                        b = st.b(1)
                        act.wait_ge(gat["t2"], b + 1)
                        if st.from_(1, 1):
                            act.wait_ge(gat["proj"], b)
                        act.activation(NT, bank[1][:, :], ACT.Copy).then_inc(gat["nt"], 1)
                if st.has(3):
                    pt_copy(st, 0, gat, 4)
                    pt_copy(st, 2, gat, 4)
                if st.has(0):
                    if st.from_(0, 4):
                        act.wait_ge(gat["ag_mm"], st.b(0) - 3)
                    ln_apply(act, st, 0, 1, 4)
            act.wait_ge(h_split, SUB[SKIP + 1])
            pipeline(act, 8, 4, 4, gat_step)

            def l2_step(st):
                if st.has(1):
                    if st.from_(1, 2):
                        act.wait_ge(l2_split, st.b(1) - 1)
                    ln_apply(act, st, 1, 2, 2)
                if st.has(2):
                    b, r = st.b(2), st.ring(2, 2)
                    act.wait_ge(l2_agg, b + 1)
                    act.activation(colb(Ch, b), bank[r][:, :], ACT.Copy).then_inc(l2_agg_hi, 1)
            act.wait_ge(gat["final"], NB)
            pipeline(act, 6, 2, 3, l2_step)

            def l2b_step(st):
                if st.has(0):
                    b, r = st.b(0), st.ring(0, 2)
                    act.wait_ge(l2_z2, b + 1)
                    if st.from_(0, 2):
                        act.wait_ge(l2_r_split, b - 1)
                    for h in range(HALVES):
                        i = act.activation(RZ[:, r, h, :], bank[2 * r + h][:, :], ACT.Relu, bias=bbi[:, h:h + 1],
                                           scale=bsc[:, h:h + 1])
                    i.then_inc(l2_relu, 1)
                if st.has(1):
                    b, r = st.b(1), st.ring(1, 2)
                    act.wait_ge(l2_o, b + 1)
                    act.activation(colb(Ch, b), bank[4 + r][:, :], ACT.Copy).then_inc(l2_o_hi, 1)
            act.wait_ge(bn_ready, 1)
            pipeline(act, 4, 2, 1, l2b_step)

            def att_step(st):
                if st.has(0):
                    b = st.b(0)
                    act.wait_ge(att["bn_in"], b + 1)
                    if st.from_(0, 1):
                        act.wait_ge(att["t1"], b)
                    act.activation(HT, OS, ACT.Identity, bias=bbi[:, 2:3], scale=bsc[:, 2:3]).then_inc(att["col"], 1)
                if st.has(3):
                    exp_row(st, 0, att)
                    exp_row(st, 1, att)
                if st.has(4):
                    attended(st, att)
                if st.has(3):
                    exp_row(st, 2, att)
                if st.has(1):
                    b, r = st.b(1), st.ring(1, 2)
                    act.wait_ge(att["t2"], b + 1)
                    if st.from_(1, 2):
                        act.wait_ge(att["sc"], 4 * b - 4)
                    act.activation(NTh[:, r, :], bank[1][:, :], ACT.Copy).then_inc(att["nt_hi"], 1)
                if st.has(3):
                    exp_row(st, 3, att)
                    pt_copy(st, 0, att, 5)
                if st.has(1):
                    b, r = st.b(1), st.ring(1, 2)
                    act.wait_ge(att["proj"], b + 1)
                    act.activation(QTh[:, r, :], bank[2][:, :], ACT.Copy).then_inc(att["qt_hi"], 1)
                if st.has(3):
                    pt_copy(st, 2, att, 5)
                if st.has(0):
                    if st.from_(0, 4):
                        act.wait_ge(att["ag_mm"], st.b(0) - 3)
                    ln_apply(act, st, 0, 3, 4)
            act.wait_ge(l2_o_split, NB)
            act.activation(w_qkh, w_qk[:, :], ACT.Copy).then_inc(att["w_hi"], 1)
            act.wait_ge(bn_ready, 2)
            pipeline(act, 8, 4, 4, att_step)

        @block.vector
        def _(dve):
            n = [0]

            def then(i):
                n[0] += 1
                i.then_inc(dve_chain, 1)
                dve.wait_ge(dve_chain, n[0])

            hi = [2]

            def split_lo(dst, src, hi_ap, scale=None):
                hi[0] += 1
                dve.wait_ge(prep_hi, hi[0])
                h = hi_ap.bitcast(F32)
                if scale is None:
                    i = dve.tensor_tensor(dst, src, h, ALU.subtract)
                else:
                    i = dve.scalar_tensor_tensor(out=dst, in0=src, scalar=scale, in1=h, op0=ALU.mult, op1=ALU.subtract)
                return i

            dve.wait_ge(prep_hi, 2)
            then(dve.tensor_tensor(gcn_wl[:, :, :], gcn_w32[:, :, :], gcn_wh[:, :, :].bitcast(F32), ALU.subtract))
            dve.wait_ge(in_adj, 16)
            for c in range(CH):
                i = dve.tensor_tensor(diag_blocks[:, c, :], A[:, c, c * P:(c + 1) * P], ident[:, :], ALU.mult)
            i.then_inc(diag_ready, 1)
            for g, kind in enumerate(SETUP):
                bk = bank[g % 8][:, :]
                if kind not in ("adj", "bnw"):
                    dve.wait_ge(prep_mm, g + 1)
                if kind == "vec":
                    then(dve.tensor_copy(V[:, 0:NVEC], bk[:, 0:NVEC]))
                    then(dve.tensor_copy(V[:, BHH_COL:BHH_COL + 16], bk[:, BHH_COL:BHH_COL + 16]))
                    lb = lstm_bias[:, :, :].rearrange("p a b -> p (a b)")
                    then(dve.tensor_tensor(lb, V[:, 0:16], V[:, BHH_COL:BHH_COL + 16], ALU.add))
                    for s in (slice(0, 2), slice(3, 4)):
                        then(dve.tensor_scalar(lstm_bias[:, :, s], lstm_bias[:, :, s], 0.5, None, ALU.mult))
                    i = dve.tensor_copy(s1[:, 0:1], V[:, 0:1])
                elif kind == "adj":
                    i = split_lo(Atl[:, g - 1, :], bk, Ath[:, g - 1, :])
                elif kind == "rowsum":
                    then(dve.tensor_copy(deg_rows, bk))
                    i = dve.tensor_scalar(bias_deg, deg_rows, V[:, COL["bg0"]:COL["bg0"] + 1], None, ALU.mult)
                elif kind == "colsum":
                    dve.wait_ge(prep_done, g)
                    i = dve.tensor_tensor(deg_t, bk, deg_rows, ALU.add)
                elif kind == "diag":
                    dve.wait_ge(prep_done, g)
                    i = dve.scalar_tensor_tensor(out=deg_rows, in0=deg_t, scalar=1.0, in1=bk, op0=ALU.add,
                                                 op1=ALU.subtract)
                elif kind == "bg1":
                    i = dve.tensor_copy(bg1_all[:, :], bk[:, 0:P])
                elif kind == "tw":
                    i = dve.tensor_copy(tw.rearrange("p a b -> p (a b)"), bk)
                elif kind == "bnw":
                    i = split_lo(bn_wl[:, :, :].rearrange("p a b -> p (a b)"), bk,
                                 bn_wh[:, :, :].rearrange("p a b -> p (a b)"))
                else:
                    then(dve.tensor_copy(gat_v[:, :], bk[:, 0:2]))
                    then(dve.tensor_scalar(gat_v2[:, :], ones[:, :], gat_v[:, 1:2], None, ALU.mult))
                    then(dve.tensor_scalar(w_qk[:, :], bk[:, P:2 * P], float(D) ** -0.5, None, ALU.mult))
                    i = dve.tensor_copy(w_vo[:, :], bk[:, 2 * P:3 * P])
                i.then_inc(prep_done, 1)

            def gcn_step(st):
                if st.has(1):
                    b, r = st.b(1), st.ring(1, 2)
                    dve.wait_ge(ln_normed, b + 1)
                    if st.from_(1, 2):
                        dve.wait_ge(gcn_agg, b - 1)
                    dve.tensor_copy(Hh[:, r, :, :], N[:, r, :, :]).then_inc(gcn_hh, 1)
                    dve.wait_ge(gcn_hh, b + 1)
                    dve.tensor_tensor(Hl[:, r, :, :], N[:, r, :, :], Hh[:, r, :, :].bitcast(F32),
                                      ALU.subtract).then_inc(gcn_h, 1)
                if st.has(2):
                    b, r = st.b(2), st.ring(2, 2)
                    dve.wait_ge(gcn_agg_hi, b + 1)
                    dve.tensor_tensor(Gl[:, r, :], bank[r][:, :], Gh[:, r, :].bitcast(F32),
                                      ALU.subtract).then_inc(gcn_agg_split, 1)
                if st.has(0):
                    b, r = st.b(0), st.ring(0, 2)
                    if isinstance(st.j, int):
                        dve.wait_ge(in_x[st.j // 4], 64)
                    else:
                        for q in range(4):
                            dve.wait_ge(in_x[q], 64)
                    ln_stats(dve, st, 0, 0)
                if st.has(3):
                    b, r = st.b(3), st.ring(3, 2)
                    dve.wait_ge(gcn_z, b + 1)
                    dve.tensor_tensor(T1[:, r, :], bank[2 + r][:, :], bias_deg, ALU.add).then_inc(gcn_z_sum, 1)
                if st.has(4):
                    b, r = st.b(4), st.ring(4, 2)
                    dve.wait_ge(gcn_y, b + 1)
                    dve.tensor_tensor(T2[:, r, :].rearrange("p (a b) -> p a b", b=P),
                                      bank[4 + r][:, :].rearrange("p (a b) -> p a b", b=P),
                                      bg1_all[:, None, :].to_broadcast([P, CH, P]), ALU.add).then_inc(gcn_y_sum, 1)
                if st.has(3):
                    b, r = st.b(3), st.ring(3, 2)
                    dve.wait_ge(gcn_z_hi, b + 1)
                    dve.scalar_tensor_tensor(out=Zl[:, r, :], in0=T1[:, r, :], scalar=0.0,
                                             in1=Zh[:, r, :].bitcast(F32), op0=ALU.max,
                                             op1=ALU.subtract).then_inc(gcn_z_split, 1)
                if st.has(4):
                    b, r = st.b(4), st.ring(4, 2)
                    dve.wait_ge(gcn_y_hi, b + 1)
                    dve.tensor_tensor(Yl[:, r, :, :].rearrange("p a b -> p (a b)"), T2[:, r, :],
                                      Yh[:, r, :, :].rearrange("p a b -> p (a b)").bitcast(F32),
                                      ALU.subtract).then_inc(gcn_y_split, 1)
                if st.has(5):
                    b = st.b(5)
                    dve.wait_ge(gcn_o_hi, b + 1)
                    dve.scalar_tensor_tensor(out=colb(Cl, b), in0=bank[6][:, :], scalar=0.0,
                                             in1=colb(Ch, b).bitcast(F32), op0=ALU.max,
                                             op1=ALU.subtract).then_inc(gcn_o_split, 1)
            pipeline(dve, 6, 2, 5, gcn_step)

            for c in range(CH):
                i = dve.tensor_tensor(diag_blocks[:, c, :], A[:, c, c * P:(c + 1) * P], ident[:, :], ALU.add)
            i.then_inc(diag_ready, 1)
            for i_, kind in enumerate(LATE):
                g = G0 + i_
                bk = bank[i_ % 8][:, :]
                if kind == "deg":
                    dve.wait_ge(prep_mm, g + 1)
                    dve.tensor_copy(deg[:, :], bk.rearrange("p (c q) -> p c q", q=P)[:, :, 0]).then_inc(deg_ready, 1)
                    dve.wait_ge(dinv_ready, 1)
                    for c in range(CH):
                        i = dve.tensor_scalar(Th[:, 0, c * P:(c + 1) * P], ones[:, :], dinv[:, c:c + 1], None, ALU.mult)
                    i.then_inc(dinv_col, 1)
                    i = dve.tensor_copy(s1[:, 0:1], dinv[:, 0:1])
                elif kind == "dinv":
                    dve.wait_ge(prep_mm, g + 1)
                    i = dve.tensor_copy(dinv_all, bk)
                elif kind == "ahat":
                    c = i_ - 2
                    dve.wait_ge(prep_mm, g + 1)
                    dve.wait_ge(prep_done, g)
                    th = Th[:, (c + 1) % 2, :]
                    dve.scalar_tensor_tensor(out=th, in0=bk, scalar=dinv[:, c:c + 1], in1=dinv_all,
                                             op0=ALU.mult, op1=ALU.mult).then_inc(ahat_tmp, 1)
                    i = split_lo(Atl[:, c, :], th, Ath[:, c, :])
                elif kind == "wih":
                    i = split_lo(WXl[:, i_ - 6, :], bk, WXh[:, i_ - 6, :], 1.0 if i_ == 6 else 0.5)
                else:
                    i = split_lo(WHl[:, i_ - 10, :], bk, WHh[:, i_ - 10, :], 0.5)
                i.then_inc(prep_done, 1)
            dve.tensor_scalar(A[:, :, :], A[:, :, :], 0.0, NEG, ALU.is_equal, ALU.mult).then_inc(mask_ready, 1)

            def lstm_pair(p, r):
                def cell(s, k):
                    q = SUB[p] + (r * p + s) * 2 + k
                    ti, tg, tf = (tile_view(TG[:, k, g, :], p) for g in (0, 2, 1))
                    cc = tile_view(CC[:, k, :], p)
                    dve.wait_ge(cell_gates, q + 1)
                    if s == 0:
                        dve.scalar_tensor_tensor(out=cc, in0=ti, scalar=1.0, in1=tg, op0=ALU.add,
                                                 op1=ALU.mult).then_inc(cell_new, 1)
                        return
                    ta, tb = tile_view(TA, p), tile_view(TB, p)
                    dve.scalar_tensor_tensor(out=ta, in0=ti, scalar=1.0, in1=tg, op0=ALU.add, op1=ALU.mult)
                    dve.scalar_tensor_tensor(out=tb, in0=tf, scalar=1.0, in1=cc, op0=ALU.add,
                                             op1=ALU.mult).then_inc(cell_parts, 1)
                    dve.wait_ge(cell_parts, PARTS[p] + (r * (p - 1) + s - 1) * 2 + k + 1)
                    dve.scalar_tensor_tensor(out=cc, in0=tb, scalar=0.5, in1=ta, op0=ALU.mult,
                                             op1=ALU.add).then_inc(cell_new, 1)

                def h_out(s, k):
                    q = SUB[p] + (r * p + s) * 2 + k
                    dve.wait_ge(all_gates, q + 1)
                    dve.wait_ge(cell_tanh, q + 1)
                    hf = tile_view(HF[:, k, :], p)
                    dve.scalar_tensor_tensor(out=hf, in0=tile_view(TG[:, k, 3, :], p), scalar=1.0,
                                             in1=tile_view(TC[:, k, :], p), op0=ALU.add,
                                             op1=ALU.mult).then_inc(h_full, 1)
                    if s < p - 1:
                        dh, dl = tile_view(STh[:, k, :], p), tile_view(STl[:, k, :], p)
                    else:
                        dh, dl = col_view(Ch, p, r, k, s), col_view(Cl, p, r, k, s)
                    dve.wait_ge(h_full, q + 1)
                    dve.tensor_copy(dh, hf).then_inc(h_hi, 1)
                    dve.wait_ge(h_hi, q + 1)
                    dve.tensor_tensor(dl, hf, dh.bitcast(F32), ALU.subtract).then_inc(h_split, 1)
                for s in range(p):
                    for k in range(2):
                        cell(s, k)
                        if p > 1:
                            h_out(s, k)
                        elif k == 1:
                            h_out(0, 0)
                            h_out(0, 1)
            PARTS = {1: 0}
            for p in range(1, SKIP + 1):
                PARTS[p + 1] = PARTS[p] + lstm_units(p)[2] * 2 * (p - 1)
            lstm_loop(dve, lstm_pair)

            def xb(b):
                return X[:, bass.ds(b, 1), :, :].rearrange("p o c d -> p (o c d)")

            def pt_copy(st, c, s, bk):
                b = st.b(3)
                dve.wait_ge(s["pt_mm"], 4 * b + c + 1)
                if c == 1 and st.from_(3, 1):
                    dve.wait_ge(s["ag_mm"], b)
                m = CH if s is gat else c + 1
                dve.tensor_copy(PT[:, 0:m, c * P:(c + 1) * P],
                                bank[bk + 1][:, 0:m * P].rearrange("p (a b) -> p a b", b=P)).then_inc(s["pt_dve"], 1)

            def add_out(st, s):
                b, r = st.b(4), st.ring(4, 2)
                dve.reciprocal(rden[:, :], den[:, r, :]).then_inc(s["rden"], 1)
                dve.wait_ge(s["rden"], b + 1)
                dve.wait_ge(s["out_mm"], b + 1)
                for c in range(CH):
                    xc = X[:, bass.ds(b, 1), c, :].rearrange("p o d -> p (o d)")
                    i = dve.scalar_tensor_tensor(out=xc, in0=bank[7][:, c * P:(c + 1) * P], scalar=rden[:, c:c + 1],
                                                 in1=xc, op0=ALU.mult, op1=ALU.add)
                i.then_inc(s["final"], 1)

            def gat_step(st):
                def u_row(c):
                    b, r = st.b(2), st.ring(2, 2)
                    dve.tensor_tensor_reduce(U[:, r, c, :], bank[2 + r][:, :], A[:, c, :], 1.0, NEG, ALU.add,
                                             ALU.max, top[:, c:c + 1]).then_inc(gat["u"], 1)

                def v_row(c):
                    b, r = st.b(2), st.ring(2, 2)
                    dve.wait_ge(gat["relu"], 4 * b + c + 1)
                    dve.scalar_tensor_tensor(out=U[:, r, c, :], in0=U[:, r, c, :], scalar=SLOPE, in1=bank[6][:, :],
                                             op0=ALU.mult, op1=ALU.add).then_inc(gat["v"], 1)

                if st.has(2):
                    b, r = st.b(2), st.ring(2, 2)
                    dve.wait_ge(gat["proj"], b + 1)
                    if st.from_(2, 2):
                        dve.wait_ge(gat["pt_mm"], 4 * b - 4)
                    if st.from_(2, 1):
                        dve.wait_ge(gat["bias"], b)
                    dve.tensor_copy(s1[:, :], bank[0][:, 0:CH]).then_inc(gat["s1"], 1)
                    dve.wait_ge(gat["s1"], b + 1)
                    dve.tensor_scalar(s1x[:, :], s1[:, :], 1.0 - SLOPE, None, ALU.mult).then_inc(gat["s1_8"], 1)
                    u_row(0)
                    u_row(1)
                    v_row(0)
                if st.has(0):
                    b = st.b(0)
                    dve.wait_ge(gat["t1"], b + 1)
                    dve.scalar_tensor_tensor(out=xb(b), in0=bank[0][:, :], scalar=0.5, in1=xb(b), op0=ALU.mult,
                                             op1=ALU.add).then_inc(gat["x_new"], 1)
                if st.has(2):
                    apart(dve)
                    u_row(2)
                    v_row(1)
                if st.has(0):
                    dve.wait_ge(gat["x_new"], st.b(0) + 1)
                    ln_stats(dve, st, 0, 1)
                if st.has(2):
                    apart(dve)
                    u_row(3)
                    v_row(2)
                if st.has(4):
                    add_out(st, gat)
                if st.has(3):
                    pt_copy(st, 1, gat, 4)
                if st.has(2):
                    v_row(3)
                    b, r = st.b(2), st.ring(2, 2)
                    dve.wait_ge(gat["u"], 4 * b + 4)
                    dve.tensor_tensor(e_top[:, :], top[:, :], s1[:, :], ALU.add).then_inc(gat["e_top"], 1)
                    dve.wait_ge(gat["e_top"], b + 1)
                    dve.scalar_tensor_tensor(out=l_top[:, :], in0=e_top[:, :], scalar=SLOPE, in1=e_top[:, :],
                                             op0=ALU.mult, op1=ALU.max).then_inc(gat["l_top"], 1)
                    dve.wait_ge(gat["l_top"], b + 1)
                    dve.scalar_tensor_tensor(out=soft_b[:, r, :], in0=s1[:, :], scalar=SLOPE, in1=l_top[:, :],
                                             op0=ALU.mult, op1=ALU.subtract).then_inc(gat["bias"], 1)
                if st.has(3):
                    pt_copy(st, 3, gat, 4)
            dve.wait_ge(h_split, SUB[SKIP + 1])
            pipeline(dve, 8, 4, 4, gat_step)

            def l2_step(st):
                if st.has(1):
                    b, r = st.b(1), st.ring(1, 2)
                    dve.wait_ge(ln_normed, 2 * NB + b + 1)
                    if st.from_(1, 2):
                        dve.wait_ge(l2_agg, b - 1)
                    dve.tensor_copy(Nh[:, r, :, :], N[:, r, :, :]).then_inc(l2_hi, 1)
                    dve.wait_ge(l2_hi, b + 1)
                    dve.tensor_tensor(Nl[:, r, :, :], N[:, r, :, :], Nh[:, r, :, :].bitcast(F32),
                                      ALU.subtract).then_inc(l2_split, 1)
                if st.has(0):
                    ln_stats(dve, st, 0, 2)
                if st.has(2):
                    b, r = st.b(2), st.ring(2, 2)
                    dve.wait_ge(l2_agg_hi, b + 1)
                    dve.tensor_tensor(colb(Cl, b), bank[r][:, :], colb(Ch, b).bitcast(F32),
                                      ALU.subtract).then_inc(l2_agg_split, 1)
                if st.has(3):
                    b, r = st.b(3), st.ring(3, 2)
                    dve.wait_ge(l2_z, b + 1)
                    apart(dve)
                    for h in range(HALVES):
                        i = dve.bn_stats(bst1[:, h, bass.ds(b, 1), :].rearrange("p o s -> p (o s)"),
                                         bank[2 + 2 * r + h][:, :])
                    i.then_inc(l2_zstats, 1)
            dve.wait_ge(gat["final"], NB)
            pipeline(dve, 6, 2, 3, l2_step)

            def bn_params(lo, hi_, gain, beta, bias, k):
                w = slice(lo, hi_)
                then(dve.tensor_scalar(bve[:, w], bmv[:, w, 1], 1.0, EPS, ALU.mult, ALU.add))
                then(dve.tensor_tensor(bmb[:, w], bmv[:, w, 0], bias, ALU.add))
                dve.tensor_tensor(bsh[:, w], bias, bmb[:, w], ALU.subtract).then_inc(bn_var, 1)
                dve.wait_ge(bn_var, k)
                dve.wait_ge(bn_rs, k)
                then(dve.tensor_tensor(bsc[:, w], brs[:, w], gain, ALU.mult))
                then(dve.tensor_tensor(bms[:, w], bsh[:, w], bsc[:, w], ALU.mult))
                dve.tensor_tensor(bbi[:, w], bms[:, w], beta, ALU.add).then_inc(bn_ready, 1)

            dve.wait_ge(l2_zstats, NB)
            for h in range(HALVES):
                then(dve.bn_aggr(bmv[:, h, :], bst1[:, h, :, :].rearrange("p b s -> p (b s)")))
            bn_params(0, 2, V[:, COL["g1"]:COL["g1"] + 2], V[:, COL["be1"]:COL["be1"] + 2],
                      V[:, COL["b1"]:COL["b1"] + 2], 1)

            def l2b_step(st):
                if st.has(0):
                    b, r = st.b(0), st.ring(0, 2)
                    dve.wait_ge(l2_relu, b + 1)
                    if st.from_(0, 2):
                        dve.wait_ge(l2_o, b - 1)
                    dve.tensor_copy(Rh[:, r, :, :], RZ[:, r, :, :]).then_inc(l2_r_hi, 1)
                    dve.wait_ge(l2_r_hi, b + 1)
                    dve.tensor_tensor(Rl[:, r, :, :], RZ[:, r, :, :], Rh[:, r, :, :].bitcast(F32),
                                      ALU.subtract).then_inc(l2_r_split, 1)
                if st.has(1):
                    b, r = st.b(1), st.ring(1, 2)
                    dve.wait_ge(l2_o_hi, b + 1)
                    apart(dve)
                    dve.bn_stats(bst2[:, bass.ds(b, 1), :].rearrange("p o s -> p (o s)"),
                                 bank[4 + r][:, :]).then_inc(l2_o_stats, 1)
                    dve.tensor_tensor(colb(Cl, b), bank[4 + r][:, :], colb(Ch, b).bitcast(F32),
                                      ALU.subtract).then_inc(l2_o_split, 1)
            pipeline(dve, 4, 2, 1, l2b_step)
            dve.wait_ge(l2_o_stats, NB)
            then(dve.bn_aggr(bmv[:, 2, :], bst2[:, :, :].rearrange("p b s -> p (b s)")))
            bn_params(2, 3, V[:, COL["g2"]:COL["g2"] + 1], V[:, COL["be2"]:COL["be2"] + 1],
                      V[:, COL["b2"]:COL["b2"] + 1], 2)

            def att_step(st):
                def u_row(c):
                    b, r = st.b(2), st.ring(2, 2)
                    w = (c + 1) * P
                    dve.wait_ge(att["sc"], 4 * b + c + 1)
                    if c == 0 and st.from_(2, 2):
                        dve.wait_ge(att["pt_mm"], 4 * b - 4)
                    apart(dve)
                    dve.tensor_tensor_reduce(U[:, r, c, 0:w], bank[3 + c % 2][:, 0:w], A[:, c, 0:w], 1.0, NEG,
                                             ALU.add, ALU.max, top[:, c:c + 1]).then_inc(att["u"], 1)

                def low(dst, bk, high):
                    return dve.tensor_tensor(dst, bank[bk][:, :], high.bitcast(F32), ALU.subtract)

                if st.has(0):
                    b = st.b(0)
                    dve.wait_ge(att["t1"], b + 1)
                    dve.tensor_tensor(xb(b), bank[0][:, :], xb(b), ALU.add).then_inc(att["x_new"], 1)
                    dve.wait_ge(att["x_new"], b + 1)
                    ln_stats(dve, st, 0, 3)
                if st.has(1):
                    b, r = st.b(1), st.ring(1, 2)
                    dve.wait_ge(att["nt_hi"], b + 1)
                    low(NTl[:, r, :], 1, NTh[:, r, :]).then_inc(att["nt"], 1)
                if st.has(2):
                    u_row(0)
                    u_row(1)
                if st.has(4):
                    add_out(st, att)
                if st.has(1):
                    b, r = st.b(1), st.ring(1, 2)
                    dve.wait_ge(att["qt_hi"], b + 1)
                    low(QTl[:, r, :], 2, QTh[:, r, :]).then_inc(att["qt"], 1)
                if st.has(2):
                    u_row(2)
                if st.has(3):
                    pt_copy(st, 1, att, 5)
                if st.has(2):
                    u_row(3)
                    b, r = st.b(2), st.ring(2, 2)
                    dve.wait_ge(att["u"], 4 * b + 4)
                    if st.from_(2, 2):
                        dve.wait_ge(att["exp"], 4 * b - 4)
                    dve.tensor_scalar(soft_b[:, r, :], top[:, :], -1.0, None, ALU.mult).then_inc(att["bias"], 1)
                if st.has(3):
                    pt_copy(st, 3, att, 5)
            dve.wait_ge(att["w_hi"], 1)
            dve.tensor_tensor(w_qkl, w_qk[:, :], w_qkh.bitcast(F32), ALU.subtract).then_inc(att["w_split"], 1)
            dve.wait_ge(causal_ready, CH)
            pipeline(dve, 8, 4, 4, att_step)


INPUTS = ["x", "adj", "L0_gnn_Wg0", "L0_gnn_bg0", "L0_gnn_Wg1", "L0_gnn_bg1", "L0_gnn_Wih", "L0_gnn_Whh",
          "L0_gnn_bih", "L0_gnn_bhh", "L1_gnn_W", "L1_gnn_a", "L2_gnn_W1", "L2_gnn_b1", "L2_gnn_g1", "L2_gnn_be1",
          "L2_gnn_W2", "L2_gnn_b2", "L2_gnn_g2", "L2_gnn_be2", "L3_gnn_Wqkv", "L3_gnn_Wo"]


def kernel(**inputs):
    import numpy as np
    import concourse.bacc as bacc
    from concourse.bass_utils import run_bass_kernel_spmd

    nc = bacc.Bacc("TRN2", target_bir_lowering=False, num_devices=1)
    arrays, args = {}, []
    for name in INPUTS:
        a = np.ascontiguousarray(inputs[name])
        arrays[f"in_{name}"] = a
        args.append(nc.dram_tensor(f"in_{name}", a.shape, mybir.dt.from_np(a.dtype), kind="ExternalInput").ap())
    args.append(nc.dram_tensor("out_x", (NB, T, D), F32, kind="ExternalOutput").ap())
    program(nc, *args)
    r = run_bass_kernel_spmd(nc, [arrays], core_ids=[0])
    return r.results[0]["out_x"]
```

```python
from contextlib import ExitStack

import concourse.bass as bass
from concourse import mybir

F32 = mybir.dt.float32
F32R = mybir.dt.float32r
ALU = mybir.AluOpType
ACT = mybir.ActivationFunctionType

P = 128
NB, T, D = 16, 512, 128
CH = T // P
SKIP = 4
HALVES = 2
EPS = 1e-5
NEG = -1e30
SLOPE = 0.2

VECS = [("bih", 16), ("bg0", 1), ("b1", 2), ("g1", 2), ("be1", 2), ("b2", 1), ("g2", 1), ("be2", 1), ("a", 2)]
COL, _at = {}, 0
for _name, _n in VECS:
    COL[_name] = _at
    _at += _n
NVEC = _at
BHH_COL = 32


class Step:

    def __init__(self, j, slot):
        self.j, self.slot = j, slot

    def has(self, lag):
        return not isinstance(self.j, int) or 0 <= self.j - lag < NB

    def b(self, lag):
        return self.j - lag

    def ring(self, lag, n):
        return (self.slot - lag) % n

    def from_(self, lag, n):
        return not isinstance(self.j, int) or self.j - lag >= n


def pipeline(eng, start, unroll, lags, step, between=lambda j: None, first=0):
    for j in range(first, start):
        step(Step(j, j))
        between(j)
    with eng.Fori(0, (NB - start) // unroll) as i:
        for k in range(unroll):
            step(Step(i * unroll + (start + k), start + k))
    for j in range(NB, NB + lags):
        step(Step(j, j))
        between(j)


def program(nc, x, adj, Wg0, bg0, Wg1, bg1, Wih, Whh, bih, bhh, gat_W, gat_a,
            W1, b1, g1, be1, W2, b2, g2, be2, Wqkv, Wo, out):
    ctx = ExitStack()
    with ctx:
        def sb(name, shape, dt=F32):
            return ctx.enter_context(nc.sbuf_tensor(name, shape, dt))

        def sem(name):
            return ctx.enter_context(nc.semaphore(name))

        bank = [ctx.enter_context(nc.psum_tensor(f"bank{i}", [P, 512], F32)) for i in range(8)]

        X = sb("x_stream", [P, NB, CH, D])
        A = sb("adj_rows", [P, CH, T])
        Ath = sb("adjT_hi", [P, CH, T], F32R)
        Atl = sb("adjT_lo", [P, CH, T], F32R)
        Ch = sb("col_hi", [P, NB, T], F32R)
        Cl = sb("col_lo", [P, NB, T], F32R)
        ident = sb("ident", [P, P])
        ones = sb("ones", [P, P])
        ones_r = sb("ones_r", [P, P], F32R)
        bg1_row = sb("bg1_row", [1, P])
        V = sb("vec_cols", [P, 48])
        lstm_bias = sb("lstm_bias", [P, SKIP, 4])
        gcn_wh = sb("gcn_wh", [P, 2, P], F32R)
        gcn_wl = sb("gcn_wl", [P, 2, P], F32R)
        gat_w = sb("gat_w", [P, P])
        bn_wh = sb("bn_wh", [P, 4, P], F32R)
        bn_wl = sb("bn_wl", [P, 4, P], F32R)
        wo32 = sb("wo32", [P, P])
        gat_v = sb("gat_v", [P, 2])
        gat_v2 = sb("gat_v2", [P, P])
        w_qk = sb("w_qk", [P, P])
        w_vo = sb("w_vo", [P, P])
        bg1_all = sb("bg1_all", [P, P])
        deg = sb("deg", [P, CH])
        dinv = sb("dinv", [P, CH])
        stats = sb("ln_stats", [P, 2, CH, 6])
        rstd = sb("ln_rstd", [P, 2, CH])
        nbias = sb("ln_bias", [P, 2, CH])
        pad = sb("pad", [1, 32])
        neg_half, d_eps = sb("neg_half", [P, CH]), sb("d_eps", [P, CH])
        quarter_d, sqrt_d = sb("quarter_d", [P, CH]), sb("sqrt_d", [P, CH])
        ln_d, ln_s, ln_q, ln_dd = (sb(f"ln_{k}", [P, CH]) for k in ("diff", "sum", "vars", "diff2"))
        ln_m, ln_qe, ln_dq, ln_v, ln_p = (sb(f"ln_{k}", [P, CH]) for k in ("mean", "vars_eps", "quarter", "dvar", "root"))
        s1 = sb("gat_s1", [P, CH])
        s1x = sb("gat_s1x", [P, CH])
        top = sb("row_top", [P, CH])
        e_top = sb("gat_e_top", [P, CH])
        l_top = sb("gat_l_top", [P, CH])
        soft_b = sb("soft_bias", [P, 2, CH])
        den = sb("soft_den", [P, 2, CH])
        rden = sb("soft_rden", [P, CH])
        bst1 = sb("bn1_stats", [P, HALVES, NB, 6])
        bst2 = sb("bn2_stats", [P, NB, 6])
        bmv = sb("bn_mean_var", [P, 3, 2])
        bve = sb("bn_var_eps", [P, 3])
        brs = sb("bn_rstd", [P, 3])
        bsc = sb("bn_scale", [P, 3])
        bmb = sb("bn_mean_b", [P, 3])
        bsh = sb("bn_shift", [P, 3])
        bms = sb("bn_shift_scaled", [P, 3])
        bbi = sb("bn_bias", [P, 3])

        SR = sb("scratch_r", [P, 8192], F32R)
        SF = sb("scratch_f", [P, 9728])

        def carve(t, at, *dims):
            n = 1
            for d in dims:
                n *= d
            v = t[:, at:at + n]
            names = "abcd"[:len(dims)]
            if len(dims) > 1:
                v = v.rearrange(f"p ({' '.join(names)}) -> p {' '.join(names)}",
                                **{c: d for c, d in zip(names, dims)})
            return v

        Hh, Hl = carve(SR, 0, 2, CH, D), carve(SR, 1024, 2, CH, D)
        Gh, Gl = carve(SR, 2048, 2, T), carve(SR, 3072, 2, T)
        Zh, Zl = carve(SR, 4096, 2, T), carve(SR, 5120, 2, T)
        Yh, Yl = carve(SR, 6144, 2, CH, D), carve(SR, 7168, 2, CH, D)
        WXh, WXl = carve(SR, 0, SKIP, T), carve(SR, 2048, SKIP, T)
        WHh, WHl = carve(SR, 4096, SKIP - 1, T), carve(SR, 5632, SKIP - 1, T)
        STh = carve(SR, 7168, 2, T)
        STl = sb("state_lo", [P, 2, T], F32R)
        Nh, Nl = carve(SR, 0, 2, CH, D), carve(SR, 1024, 2, CH, D)
        Rh, Rl = carve(SR, 2048, 2, HALVES, T), carve(SR, 4096, 2, HALVES, T)

        N = carve(SF, 0, 4, CH, D)
        T1 = carve(SF, 2048, 2, T)
        T2 = carve(SF, 3072, 2, T)
        wih_rows = carve(SF, 4096, 16, P)
        whh_rows = carve(SF, 6144, 12, P)
        diag_blocks = carve(SF, 7680, CH, P)
        deg_rows = carve(SF, 8192, T)
        dinv_cols = deg_rows
        deg_t = carve(SF, 8704, T)
        dinv_all = deg_t
        loops = carve(SF, 5120, CH, P)
        Th = carve(SF, 3072, CH, T)
        gcn_w32 = carve(SF, 2048, 2, P)
        vec_rows = carve(SF, 2304, P)
        bhh_rows = carve(SF, 2432, P)
        bias_deg = carve(SF, 9216, T)
        stage_w = carve(SF, 1024, 8, P)
        tw = stage_w[:, 0:4, :]
        TG = carve(SF, 0, 2, 4, T)
        CC = carve(SF, 4096, 2, T)
        TC = carve(SF, 5120, 2, T)
        HF = carve(SF, 6144, 2, T)
        TA = carve(SF, 7168, T)
        TB = carve(SF, 7680, T)
        HT = carve(SF, 9216, T)
        AG = carve(SF, 2560, T)
        U = carve(SF, 3072, 2, CH, T)
        PT = carve(SF, 7168, CH, T)
        NT = carve(SF, 2048, T)
        OS = carve(SF, 2048, T)
        NTh, NTl = carve(SR, 0, 2, T), carve(SR, 1024, 2, T)
        QTh, QTl = carve(SR, 2048, 2, T), carve(SR, 3072, 2, T)
        w_qkh, w_qkl = carve(SR, 4096, P), carve(SR, 4224, P)
        RZ = carve(SF, 2048, 2, HALVES, T)

        in_adj, in_vec, in_gcn_w, in_small = sem("in_adj"), sem("in_vec"), sem("in_gcn_w"), sem("in_small")
        in_lstm = sem("in_lstm")
        in_x0 = sem("in_x0")
        in_x = [sem(f"in_x_quarter{i}") for i in range(4)]
        in_adj2 = sem("in_adj2")
        consts = sem("consts")
        dve_chain = sem("dve_chain")
        diag_ready = sem("diag_ready")
        prep_mm = sem("prep_mm")
        prep_hi = sem("prep_hi")
        prep_done = sem("prep_done")
        deg_ready, dinv_ready, dinv_col = sem("deg_ready"), sem("dinv_ready"), sem("dinv_col")

        ln_stats_done = sem("ln_stats_done")
        ln_sums, ln_square, ln_quarter = sem("ln_sums"), sem("ln_square"), sem("ln_quarter_done")
        ln_dvar, ln_root, ln_rstd = sem("ln_dvar_done"), sem("ln_root_done"), sem("ln_rstd_done")
        ln_scale_ready = sem("ln_scale_ready")
        ln_normed = sem("ln_normed")

        pads = []

        def apart(dve):
            pads.append(len(pads) % 32)
            dve.memset(pad[0:1, pads[-1]:pads[-1] + 1], 0.0)

        def ln_stats(dve, st, lag, nth):
            b, r = st.b(lag), st.ring(lag, 2)
            n = nth * NB + b
            if nth or st.from_(lag, 2):
                dve.wait_ge(ln_sums, n - 1)
            apart(dve)
            for c in range(CH):
                i = dve.bn_stats(stats[:, r, c, :], X[:, bass.ds(b, 1), c, :].rearrange("p o d -> p (o d)"))
            i.then_inc(ln_stats_done, 1)

        def ln_scale(pool, st, lag, nth):
            b, r = st.b(lag), st.ring(lag, 2)
            n = nth * NB + b
            me, vc_e, mo, vc_o = (stats[:, r, :, i] for i in (1, 2, 4, 5))
            pool.wait_ge(ln_stats_done, n + 1)
            pool.tensor_tensor(ln_d[:, :], me, mo, ALU.subtract)
            pool.tensor_tensor(ln_s[:, :], me, mo, ALU.add)
            pool.tensor_tensor(ln_q[:, :], vc_e, vc_o, ALU.add).then_inc(ln_sums, 1)
            pool.wait_ge(ln_sums, n + 1)
            pool.tensor_tensor(ln_dd[:, :], ln_d[:, :], ln_d[:, :], ALU.mult)
            pool.tensor_tensor(ln_m[:, :], ln_s[:, :], neg_half[:, :], ALU.mult)
            pool.tensor_tensor(ln_qe[:, :], ln_q[:, :], d_eps[:, :], ALU.add).then_inc(ln_square, 1)
            pool.wait_ge(ln_square, n + 1)
            pool.tensor_tensor(ln_dq[:, :], ln_dd[:, :], quarter_d[:, :], ALU.mult).then_inc(ln_quarter, 1)
            pool.wait_ge(ln_quarter, n + 1)
            pool.tensor_tensor(ln_v[:, :], ln_dq[:, :], ln_qe[:, :], ALU.add).then_inc(ln_dvar, 1)
            pool.wait_ge(ln_dvar, n + 1)
            pool.tensor_tensor(ln_p[:, :], ln_v[:, :], neg_half[:, :], ALU.pow).then_inc(ln_root, 1)
            pool.wait_ge(ln_root, n + 1)
            if nth or st.from_(lag, 2):
                pool.wait_ge(ln_normed, n - 1)
            pool.tensor_tensor(rstd[:, r, :], ln_p[:, :], sqrt_d[:, :], ALU.mult).then_inc(ln_rstd, 1)
            pool.wait_ge(ln_rstd, n + 1)
            pool.tensor_tensor(nbias[:, r, :], ln_m[:, :], rstd[:, r, :], ALU.mult).then_inc(ln_scale_ready, 1)

        def ln_apply(act, st, lag, nth, ring):
            b, r = st.b(lag), st.ring(lag, 2)
            n = nth * NB + b
            act.wait_ge(ln_scale_ready, n + 1)
            for c in range(CH):
                i = act.activation(N[:, st.ring(lag, ring), c, :],
                                   X[:, bass.ds(b, 1), c, :].rearrange("p o d -> p (o d)"),
                                   ACT.Relu, bias=nbias[:, r, c:c + 1], scale=rstd[:, r, c:c + 1])
            i.then_inc(ln_normed, 1)

        def product(pe, o, w, xv, first=True, last=True):
            pe.matmul(o, w[0], xv[0], start=first, stop=False)
            pe.matmul(o, w[0], xv[1], start=False, stop=False)
            return pe.matmul(o, w[1], xv[0], start=False, stop=last)

        def colb(t, b):
            return t[:, bass.ds(b, 1), :].rearrange("p o t -> p (o t)")

        gcn_h = sem("gcn_h_split")
        gcn_agg, gcn_agg_hi, gcn_agg_split = sem("gcn_agg"), sem("gcn_agg_hi"), sem("gcn_agg_split")
        gcn_z, gcn_z_sum, gcn_z_hi, gcn_z_split = sem("gcn_z"), sem("gcn_z_sum"), sem("gcn_z_hi"), sem("gcn_z_split")
        gcn_y, gcn_y_sum, gcn_y_hi, gcn_y_split = sem("gcn_y"), sem("gcn_y_sum"), sem("gcn_y_hi"), sem("gcn_y_split")
        gcn_o, gcn_o_hi, gcn_o_split = sem("gcn_o"), sem("gcn_o_hi"), sem("gcn_o_split")
        gcn_hh = sem("gcn_h_hi")
        ahat_tmp = sem("ahat_tmp")
        gate_mm = sem("gate_mm")
        cell_gates = sem("cell_gates")
        all_gates = sem("all_gates")
        cell_parts = sem("cell_parts")
        cell_new = sem("cell_new")
        cell_tanh = sem("cell_tanh")
        h_full, h_hi, h_split = sem("h_full"), sem("h_hi"), sem("h_split")

        def attention_events(name, events):
            return {k: sem(f"{name}_{k}") for k in events.split()}

        gat = attention_events("gat", "col t1 x_new t2 nt proj s1 s1_8 u e_top l_top bias relu v exp pt_mm pt_dve "
                               "pt_act ag_mm ag out_mm rden final")
        att = attention_events("att", "bn_in col t1 x_new t2 nt_hi nt w_hi w_split proj qt_hi qt sc u bias exp pt_mm "
                               "pt_dve pt_act ag_mm ag out_mm rden final")
        l2_hi, l2_split = sem("l2_h_hi"), sem("l2_h_split")
        l2_agg, l2_agg_hi, l2_agg_split = sem("l2_agg"), sem("l2_agg_hi"), sem("l2_agg_split")
        l2_z, l2_zstats = sem("l2_z"), sem("l2_z_stats")
        bn_var, bn_rs, bn_ready = sem("bn_var"), sem("bn_rs"), sem("bn_ready")
        l2_z2, l2_relu, l2_r_hi, l2_r_split = sem("l2_z2"), sem("l2_relu"), sem("l2_r_hi"), sem("l2_r_split")
        l2_o, l2_o_hi, l2_o_stats, l2_o_split = sem("l2_o"), sem("l2_o_hi"), sem("l2_o_stats"), sem("l2_o_split")
        causal_ready, mask_ready = sem("causal_ready"), sem("mask_ready")
        out_dma = sem("out_dma")

        block = ctx.enter_context(nc.Block())
        GATES = (0, 2, 1, 3)

        def lstm_units(p):
            nb = {1: 1, 2: 2, 3: 2, 4: 4}[p]
            return nb, T // p, NB // (2 * nb)

        SUB, GAT0 = {1: 0}, {1: 0}
        for _p in range(1, SKIP + 1):
            _r = lstm_units(_p)[2]
            SUB[_p + 1] = SUB[_p] + _r * _p * 2
            GAT0[_p + 1] = GAT0[_p] + _r * 2 * (4 * _p - 1)

        def col_view(t, p, r, k, s):
            nb, nw, _ = lstm_units(p)
            v = t[:, bass.ds((r * 2 + k) * nb, nb), 0:nw * p]
            return v.rearrange("q b (w s) -> q b w s", s=p)[:, :, :, s]

        def tile_view(v, p):
            nb, nw, _ = lstm_units(p)
            return v[:, 0:nb * nw].rearrange("q (b w) -> q b w", b=nb)

        def lstm_loop(eng, body):
            for p in range(1, SKIP + 1):
                R_ = lstm_units(p)[2]
                after = (p + 1, 0) if 1 < p < SKIP else None
                body(p, 0, (p, 1) if p > 1 else None)
                if R_ > 2:
                    with eng.Fori(1, R_ - 1) as r:
                        body(p, r, (p, r + 1) if p > 1 else None)
                body(p, R_ - 1, after)

        def begun(p, r):
            return p > 2 or (p == 2 and not (isinstance(r, int) and r == 0))

        GROUPS = [("adj", 0), ("adj", 1), ("adj", 2), ("adj", 3), ("vec", 0), ("bg1", 0), ("rowsum", 0),
                  ("colsum", 0), ("diag", 0), ("deg", 0), ("tw", 0), ("dinv", 0), ("bnw", 0), ("fold", 0),
                  ("wih", 0), ("wih", 1), ("wih", 2), ("wih", 3), ("whh", 0), ("whh", 1), ("whh", 2),
                  ("ahat", 0), ("ahat", 1), ("ahat", 2), ("ahat", 3)]
        BANKS = [3, 4, 5, 6, 7, 7, 7] + [7] * 7 + [0, 1, 2, 3, 4, 5, 6] + [4, 5, 6, 7]
        BEFORE_GCN, LSTM_WEIGHTS, A_HAT = range(0, 4), range(14, 21), range(21, 25)
        WITH_GCN = {2: range(4, 7), NB: range(7, 8), NB + 1: range(8, 9), NB + 2: range(9, 11),
                    NB + 3: range(11, 13), NB + 4: range(13, 14)}
        L2_EARLY = {NB: range(0, 1), NB + 1: range(1, 2), NB + 2: range(2, 4), NB + 3: range(4, 6)}

        @block.sync
        def _(sp):
            xv = x.rearrange("b (c p) d -> p b c d", p=P)
            sp.dma_start(X[:, 0, :, :], xv[:, 0, :, :]).then_inc(in_x0, 16)
            sp.dma_start(A[:, :, :], adj.rearrange("(c p) s -> p c s", p=P)).then_inc(in_adj, 16)
            sp.dma_start(gcn_w32[:, 0, :], Wg0).then_inc(in_gcn_w, 16)
            sp.dma_start(gcn_w32[:, 1, :], Wg1).then_inc(in_gcn_w, 16)
            for q in range(4):
                for b in range(max(4 * q, 1), 4 * q + 4):
                    sp.dma_start(X[:, b, :, :], xv[:, b, :, :]).then_inc(in_x[q], 16)
                if q == 0:
                    r = 0
                    for ap, n in ((bih.rearrange("l (g d) -> (l g) d", d=P), 16), (bg0.rearrange("(o d) -> o d", o=1), 1),
                                  (b1.rearrange("(o d) -> o d", o=2), 2), (g1.rearrange("(o d) -> o d", o=2), 2),
                                  (be1.rearrange("(o d) -> o d", o=2), 2), (b2.rearrange("(o d) -> o d", o=1), 1),
                                  (g2.rearrange("(o d) -> o d", o=1), 1), (be2.rearrange("(o d) -> o d", o=1), 1),
                                  (gat_a.rearrange("(k o) u -> k (o u)", k=2), 2)):
                        sp.dma_start(vec_rows[r:r + n, :], ap).then_inc(in_vec, 16)
                        r += n
                    sp.dma_start(bhh_rows[0:16, :], bhh.rearrange("l (g d) -> (l g) d", d=P)).then_inc(in_vec, 16)
                    sp.dma_start(bg1_row[:, :], bg1.rearrange("(o d) -> o d", o=1)).then_inc(in_vec, 16)
                if q == 0:
                    sp.dma_start(gat_w[:, :], gat_W).then_inc(in_small, 16)
                    sp.dma_start(wo32[:, :], Wo).then_inc(in_small, 16)
                    sp.dma_start(stage_w[:, 0, :], gat_W).then_inc(in_small, 16)
                    sp.dma_start(stage_w[:, 4:6, :], W1.rearrange("(h p) d -> p h d", p=P)).then_inc(in_small, 16)
                    sp.dma_start(stage_w[:, 6:8, :], W2.rearrange("o (h d) -> o h d", h=2)).then_inc(in_small, 16)
                    sp.dma_start(stage_w[:, 1:4, :], Wqkv.rearrange("c (k d) -> c k d", k=3)).then_inc(in_small, 16)
            sp.dma_start(wih_rows[:, :, :], Wih.rearrange("l (g p) d -> p (l g) d", p=P)).then_inc(in_lstm, 16)
            sp.dma_start(whh_rows[:, :, :], Whh[1:SKIP].rearrange("l (g p) d -> p (l g) d", p=P)).then_inc(in_lstm, 16)
            sp.wait_ge(gat["final"], NB)
            sp.dma_start(A[:, :, :], adj.rearrange("(c p) s -> p c s", p=P)).then_inc(in_adj2, 16)
            ov = out.rearrange("b (c p) d -> p b c d", p=P)
            with sp.Fori(0, NB) as b:
                sp.wait_ge(att["final"], b + 1)
                sp.dma_start(ov[:, bass.ds(b, 1), :, :], X[:, bass.ds(b, 1), :, :]).then_inc(out_dma, 16)
            sp.wait_ge(out_dma, 16 * NB)

        @block.gpsimd
        def _(pool):
            pool.memset(ones[:, :], 1.0).then_inc(consts, 1)
            pool.memset(neg_half[:, :], -0.5).then_inc(consts, 1)
            pool.memset(d_eps[:, :], D * EPS).then_inc(consts, 1)
            pool.memset(quarter_d[:, :], D / 4).then_inc(consts, 1)
            pool.memset(sqrt_d[:, :], float(D) ** 0.5).then_inc(consts, 1)
            pool.wait_ge(consts, 1)
            pool.affine_select(out=ident[:, :], in_=ones[:, :], compare_op=ALU.is_equal, fill=0.0, base=0,
                               pattern=[[-1, P]], channel_multiplier=1).then_inc(consts, 1)
            pool.wait_ge(consts, 6)

            def gcn_step(st):
                if st.has(0):
                    ln_scale(pool, st, 0, 0)
            pipeline(pool, 2, 2, 0, gcn_step)
            pool.wait_ge(deg_ready, 1)
            pool.tensor_tensor(dinv[:, :], deg[:, :], neg_half[:, :], ALU.pow).then_inc(dinv_ready, 1)

            def gat_step(st):
                if st.has(0):
                    b = st.b(0)
                    if isinstance(b, int) and b == 1:
                        pool.wait_ge(h_split, SUB[SKIP + 1])
                    if st.from_(0, 1):
                        pool.wait_ge(gat["t1"], b)
                    pool.tensor_tensor(HT, colb(Ch, b).bitcast(F32), colb(Cl, b).bitcast(F32),
                                       ALU.add).then_inc(gat["col"], 1)
                if st.has(1):
                    ln_scale(pool, st, 1, 1)
            pool.wait_ge(h_split, SUB[SKIP] + 2 * SKIP)
            pipeline(pool, 4, 2, 1, gat_step)

            pipeline(pool, 2, 2, 0, lambda st: ln_scale(pool, st, 0, 2))

            pool.wait_ge(bn_var, 1)
            pool.tensor_tensor(brs[:, 0:2], bve[:, 0:2], neg_half[:, 0:2], ALU.pow).then_inc(bn_rs, 1)
            pool.wait_ge(in_adj2, 16)
            for c in range(CH):
                blk = A[:, c, c * P:(c + 1) * P]
                pool.affine_select(out=blk, in_=blk, compare_op=ALU.is_ge, fill=NEG, base=0,
                                   pattern=[[-1, P]], channel_multiplier=1).then_inc(causal_ready, 1)
            pool.wait_ge(bn_var, 2)
            pool.tensor_tensor(brs[:, 2:3], bve[:, 2:3], neg_half[:, 0:1], ALU.pow).then_inc(bn_rs, 1)

            def att_step(st):
                if st.has(0):
                    b = st.b(0)
                    if st.from_(0, 1):
                        pool.wait_ge(att["col"], b)
                    pool.tensor_tensor(OS, colb(Ch, b).bitcast(F32), colb(Cl, b).bitcast(F32),
                                       ALU.add).then_inc(att["bn_in"], 1)
                if st.has(1):
                    ln_scale(pool, st, 1, 3)
            pool.wait_ge(l2_o_split, NB)
            pipeline(pool, 4, 2, 1, att_step)

        @block.tensor
        def _(pe):
            pe.wait_ge(consts, 6)

            def transposes4(bk, srcs):
                for i, s in enumerate(srcs):
                    mm = pe.transpose(bank[bk][:, i * P:(i + 1) * P], s, ident[:, :])
                return mm

            def prepare(groups):
                for g in groups:
                    kind, c = GROUPS[g]
                    bk = bank[BANKS[g]]
                    if g >= 4 and g not in LSTM_WEIGHTS:
                        pe.wait_ge(prep_done, g if BANKS[g - 1] == BANKS[g] else g - c)
                    if kind == "vec":
                        pe.wait_ge(in_vec, 16 * 11)
                        pe.transpose(bk[:, 0:NVEC], vec_rows[0:NVEC, :], ident[0:NVEC, 0:NVEC])
                        mm = pe.transpose(bk[:, BHH_COL:BHH_COL + 16], bhh_rows[0:16, :], ident[0:16, 0:16])
                    elif kind == "adj":
                        if c == 0:
                            pe.wait_ge(in_adj, 16)
                        mm = transposes4(BANKS[g], [A[:, t, c * P:(c + 1) * P] for t in range(CH)])
                    elif kind == "rowsum":
                        for c in range(CH):
                            pe.matmul(bk[:, :], ones_r[:, :], Ath[:, c, :], start=(c == 0), stop=False)
                            mm = pe.matmul(bk[:, :], ones_r[:, :], Atl[:, c, :], start=False, stop=(c == CH - 1))
                    elif kind == "colsum":
                        for c in range(CH):
                            mm = pe.matmul(bk[:, :], ones[:, :], A[:, c, :], start=(c == 0), stop=(c == CH - 1))
                    elif kind == "diag":
                        pe.wait_ge(diag_ready, 1)
                        mm = pe.matmul(bk[:, :], ones[:, :], diag_blocks.rearrange("p a b -> p (a b)"),
                                       start=True, stop=True)
                    elif kind == "bg1":
                        mm = pe.matmul(bk[:, 0:P], ones[0:1, :], bg1_row[:, :], start=True, stop=True)
                    elif kind == "tw":
                        pe.wait_ge(in_small, 16 * 6)
                        mm = transposes4(BANKS[g], [stage_w[:, i, :] for i in range(4)])
                    elif kind == "bnw":
                        mm = transposes4(BANKS[g], [stage_w[:, i, :] for i in range(4, 8)])
                    elif kind == "fold":
                        pe.matmul(bk[:, 0:2], tw[:, 0, :], V[:, COL["a"]:COL["a"] + 2], start=True, stop=True)
                        pe.matmul(bk[:, P:2 * P], tw[:, 1, :], tw[:, 2, :], start=True, stop=True)
                        mm = pe.matmul(bk[:, 2 * P:3 * P], tw[:, 3, :], wo32[:, :], start=True, stop=True)
                    elif kind == "deg":
                        mm = transposes4(BANKS[g], [deg_rows[:, c * P:(c + 1) * P] for c in range(CH)])
                    elif kind == "dinv":
                        pe.wait_ge(dinv_col, 1)
                        mm = transposes4(BANKS[g], [dinv_cols[:, c * P:(c + 1) * P] for c in range(CH)])
                    elif kind == "ahat":
                        pe.wait_ge(diag_ready, 2)
                        mm = transposes4(BANKS[g], [loops[:, c, :] if t == c else A[:, t, c * P:(c + 1) * P]
                                                    for t in range(CH)])
                    elif kind == "wih":
                        mm = transposes4(BANKS[g], [wih_rows[:, 4 * c + k, :] for k in range(4)])
                    else:
                        mm = transposes4(BANKS[g], [whh_rows[:, 4 * c + k, :] for k in range(4)])
                    mm.then_inc(prep_mm, 1)

            prepare(BEFORE_GCN)
            pe.wait_ge(prep_done, CH)

            def gcn_step(st):
                if st.has(2):
                    b, r = st.b(2), st.ring(2, 2)
                    pe.wait_ge(gcn_h, b + 1)
                    if st.from_(2, 2):
                        pe.wait_ge(gcn_agg_split, b - 1)
                    for c in range(CH):
                        mm = product(pe, bank[r][:, :], (Hh[:, r, c, :], Hl[:, r, c, :]), (Ath[:, c, :], Atl[:, c, :]),
                                     c == 0, c == CH - 1)
                    mm.then_inc(gcn_agg, 1)
                if st.has(3):
                    b, r = st.b(3), st.ring(3, 2)
                    pe.wait_ge(gcn_agg_split, b + 1)
                    if st.from_(3, 2):
                        pe.wait_ge(gcn_z_sum, b - 1)
                    product(pe, bank[2 + r][:, :], (gcn_wh[:, 0, :], gcn_wl[:, 0, :]),
                            (Gh[:, r, :], Gl[:, r, :])).then_inc(gcn_z, 1)
                if st.has(4):
                    b, r = st.b(4), st.ring(4, 2)
                    pe.wait_ge(gcn_z_split, b + 1)
                    if st.from_(4, 2):
                        pe.wait_ge(gcn_y_sum, b - 1)
                    for c in range(CH):
                        cs = slice(c * P, (c + 1) * P)
                        mm = product(pe, bank[4 + r][:, cs], (Zh[:, r, cs], Zl[:, r, cs]),
                                     (gcn_wh[:, 1, :], gcn_wl[:, 1, :]))
                    mm.then_inc(gcn_y, 1)
                if st.has(5):
                    b, r = st.b(5), st.ring(5, 2)
                    pe.wait_ge(gcn_y_split, b + 1)
                    if st.from_(5, 1):
                        pe.wait_ge(gcn_o_split, b)
                    for c in range(CH):
                        mm = product(pe, bank[6][:, :], (Yh[:, r, c, :], Yl[:, r, c, :]), (Ath[:, c, :], Atl[:, c, :]),
                                     c == 0, c == CH - 1)
                    mm.then_inc(gcn_o, 1)
            pipeline(pe, 6, 2, 5, gcn_step, lambda j: prepare(WITH_GCN.get(j, ())))

            pe.wait_ge(gcn_o_split, NB)
            pe.wait_ge(in_lstm, 32)
            prepare(LSTM_WEIGHTS)
            pe.wait_ge(prep_done, 21)

            def lstm_pair(p, r, following):
                nb, nw, _ = lstm_units(p)
                if p > 1:
                    per = 2 * (p - 1) * nb // lstm_units(p - 1)[0]
                    pe.wait_ge(h_split, SUB[p - 1] + per * (r + 1))
                for s in range(p):
                    for k in range(2):
                        q = SUB[p] + (r * p + s) * 2 + k
                        if not (p == 1 and isinstance(r, int) and r == 0):
                            pe.wait_ge(all_gates, q - 1)
                        gates = [g for g in GATES if s > 0 or g != 1]
                        xs = (col_view(Ch, p, r, k, s), col_view(Cl, p, r, k, s))
                        for g in gates:
                            o = tile_view(bank[4 * k + g], p)
                            gs = slice(g * P, (g + 1) * P)
                            mm = product(pe, o, (WXh[:, p - 1, gs], WXl[:, p - 1, gs]), xs, True, s == 0)
                            if s == 0:
                                mm.then_inc(gate_mm, 1)
                        if s > 0:
                            pe.wait_ge(h_split, q - 1)
                            hs = (tile_view(STh[:, k, :], p), tile_view(STl[:, k, :], p))
                            for g in gates:
                                o = tile_view(bank[4 * k + g], p)
                                gs = slice(g * P, (g + 1) * P)
                                product(pe, o, (WHh[:, p - 2, gs], WHl[:, p - 2, gs]), hs, False,
                                        True).then_inc(gate_mm, 1)
            lstm_loop(pe, lstm_pair)

            def back_to_rows(st, s):
                b = st.b(0)
                pe.wait_ge(s["col"], b + 1)
                if st.from_(0, 1):
                    pe.wait_ge(s["x_new"], b)
                transposes4(0, [HT[:, c * P:(c + 1) * P] for c in range(CH)]).then_inc(s["t1"], 1)

            def rows_to_col(st, s, nth):
                b, r = st.b(1), st.ring(1, 4)
                pe.wait_ge(ln_normed, nth * NB + b + 1)
                if st.from_(1, 1):
                    pe.wait_ge(s["nt"], b)
                transposes4(1, [N[:, r, c, :] for c in range(CH)]).then_inc(s["t2"], 1)

            def attend(st, s):
                b, r = st.b(4), st.ring(4, 4)
                pe.wait_ge(s["pt_act"], 2 * b + 2)
                pe.wait_ge(s["pt_dve"], 2 * b + 2)
                if st.from_(4, 1):
                    pe.wait_ge(s["final"], b)
                for c in range(CH):
                    t0 = 0 if s is gat else c * P
                    mm = pe.matmul(bank[7][:, t0:T], N[:, r, c, :], PT[:, c, t0:T], start=(c == 0), stop=(c == CH - 1))
                mm.then_inc(s["ag_mm"], 1)

            def project_out(st, s, w):
                pe.wait_ge(s["ag"], st.b(4) + 1)
                for c in range(CH):
                    mm = pe.matmul(bank[7][:, c * P:(c + 1) * P], AG[:, c * P:(c + 1) * P], w, start=True, stop=True)
                mm.then_inc(s["out_mm"], 1)

            def probs_t(st, s, c, bk):
                b = st.b(3)
                pe.wait_ge(s["exp"], 4 * b + c + 1)
                if c >= 2:
                    pe.wait_ge(s["pt_act"] if c % 2 == 0 else s["pt_dve"], 2 * b + 1)
                elif st.from_(3, 1):
                    pe.wait_ge(s["pt_act"] if c % 2 == 0 else s["pt_dve"], 2 * b)
                n = CH if s is gat else c + 1
                transposes4(bk + c % 2, [U[:, st.ring(3, 2), c, i * P:(i + 1) * P] for i in range(n)]
                            ).then_inc(s["pt_mm"], 1)

            def gat_step(st):
                if st.has(0):
                    if st.from_(0, 2):
                        pe.wait_ge(gat["s1"], st.b(0) - 1)
                    back_to_rows(st, gat)
                if st.has(1):
                    rows_to_col(st, gat, 1)
                if st.has(4):
                    attend(st, gat)
                if st.has(3):
                    probs_t(st, gat, 0, 4)
                    probs_t(st, gat, 1, 4)
                if st.has(4):
                    project_out(st, gat, gat_w[:, :])
                if st.has(3):
                    probs_t(st, gat, 2, 4)
                    probs_t(st, gat, 3, 4)
                if st.has(1):
                    b, r = st.b(1), st.ring(1, 2)
                    pe.wait_ge(gat["nt"], b + 1)
                    if st.from_(1, 2):
                        pe.wait_ge(gat["u"], 4 * b - 4)
                    pe.matmul(bank[2 + r][:, :], gat_v2[:, :], NT, start=True, stop=True)
                    if st.has(0):
                        pe.wait_ge(gat["x_new"], b + 2)
                    for c in range(CH):
                        mm = pe.matmul(bank[0][:, c:c + 1], NT[:, c * P:(c + 1) * P], gat_v[:, 0:1],
                                       start=True, stop=True)
                    mm.then_inc(gat["proj"], 1)
            def l2_step(st):
                if st.has(2):
                    b, r = st.b(2), st.ring(2, 2)
                    pe.wait_ge(l2_split, b + 1)
                    if st.from_(2, 2):
                        pe.wait_ge(l2_agg_split, b - 1)
                    for c in range(CH):
                        mm = product(pe, bank[r][:, :], (Nh[:, r, c, :], Nl[:, r, c, :]), (Ath[:, c, :], Atl[:, c, :]),
                                     c == 0, c == CH - 1)
                    mm.then_inc(l2_agg, 1)
                if st.has(3):
                    b, r = st.b(3), st.ring(3, 2)
                    pe.wait_ge(l2_agg_split, b + 1)
                    if st.from_(3, 2):
                        pe.wait_ge(l2_zstats, b - 1)
                    for h in range(HALVES):
                        mm = product(pe, bank[2 + 2 * r + h][:, :], (bn_wh[:, h, :], bn_wl[:, h, :]),
                                     (colb(Ch, b), colb(Cl, b)))
                    mm.then_inc(l2_z, 1)
            def gat_between(j):
                if j == 0:
                    prepare(A_HAT)
                if j == NB + 2:
                    pe.wait_ge(gat["s1"], NB)
                    pe.wait_ge(gat["u"], CH * NB)
                for k in L2_EARLY.get(j, ()):
                    l2_step(Step(k, k))
            pe.wait_ge(all_gates, SUB[SKIP + 1])
            pipeline(pe, 8, 4, 4, gat_step, gat_between)
            pipeline(pe, 6, 2, 3, l2_step, first=6)

            def l2b_step(st):
                if st.has(0):
                    b, r = st.b(0), st.ring(0, 2)
                    if st.from_(0, 2):
                        pe.wait_ge(l2_relu, b - 1)
                    for h in range(HALVES):
                        mm = product(pe, bank[2 * r + h][:, :], (bn_wh[:, h, :], bn_wl[:, h, :]),
                                     (colb(Ch, b), colb(Cl, b)))
                    mm.then_inc(l2_z2, 1)
                if st.has(1):
                    b, r = st.b(1), st.ring(1, 2)
                    pe.wait_ge(l2_r_split, b + 1)
                    if st.from_(1, 2):
                        pe.wait_ge(l2_o_split, b - 1)
                    for h in range(HALVES):
                        mm = product(pe, bank[4 + r][:, :], (bn_wh[:, 2 + h, :], bn_wl[:, 2 + h, :]),
                                     (Rh[:, r, h, :], Rl[:, r, h, :]), h == 0, h == HALVES - 1)
                    mm.then_inc(l2_o, 1)
            pe.wait_ge(l2_zstats, NB)
            pipeline(pe, 4, 2, 1, l2b_step)

            def att_step(st):
                def scores(c):
                    b, r = st.b(2), st.ring(2, 2)
                    w = (c + 1) * P
                    if c >= 2 or st.from_(2, 1):
                        pe.wait_ge(att["u"], 4 * b + c - 1)
                    q = slice(c * P, w)
                    product(pe, bank[3 + c % 2][:, 0:w], (QTh[:, r, q], QTl[:, r, q]),
                            (NTh[:, r, 0:w], NTl[:, r, 0:w])).then_inc(att["sc"], 1)

                if st.has(0):
                    back_to_rows(st, att)
                if st.has(2):
                    pe.wait_ge(att["qt"], st.b(2) + 1)
                    scores(0)
                    scores(1)
                if st.has(4):
                    attend(st, att)
                if st.has(1):
                    rows_to_col(st, att, 3)
                if st.has(3):
                    probs_t(st, att, 0, 5)
                    probs_t(st, att, 1, 5)
                if st.has(2):
                    scores(2)
                    scores(3)
                if st.has(4):
                    project_out(st, att, w_vo[:, :])
                if st.has(1):
                    b, r = st.b(1), st.ring(1, 2)
                    pe.wait_ge(att["nt"], b + 1)
                    if st.from_(1, 1):
                        pe.wait_ge(att["qt"], b)
                    product(pe, bank[2][:, :], (w_qkh, w_qkl), (NTh[:, r, :], NTl[:, r, :])).then_inc(att["proj"], 1)
                if st.has(3):
                    probs_t(st, att, 2, 5)
                    probs_t(st, att, 3, 5)
            pe.wait_ge(att["w_split"], 1)
            pe.wait_ge(l2_o_split, NB)
            pipeline(pe, 8, 4, 4, att_step)

        @block.scalar
        def _(act):
            act.wait_ge(consts, 6)
            act.activation(s1x[:, 0:1], ones[:, 0:1], ACT.Tanh)
            act.activation(ones_r[:, :], ones[:, :], ACT.Copy).then_inc(prep_hi, 1)
            act.wait_ge(in_gcn_w, 32)
            act.activation(gcn_wh[:, :, :], gcn_w32[:, :, :], ACT.Copy).then_inc(prep_hi, 1)

            def prepare(groups):
                for g in groups:
                    kind, c = GROUPS[g]
                    bk = bank[BANKS[g]][:, :]
                    if kind in ("adj", "bnw", "wih", "whh"):
                        act.wait_ge(prep_mm, g + 1)
                    if kind == "adj":
                        i = act.activation(Ath[:, c, :], bk, ACT.Copy)
                    elif kind == "bnw":
                        i = act.activation(bn_wh[:, :, :].rearrange("p a b -> p (a b)"), bk, ACT.Copy)
                    elif kind == "wih":
                        i = act.activation(WXh[:, c, :], bk, ACT.Copy, scale=1.0 if c == 0 else 0.5)
                    elif kind == "whh":
                        i = act.activation(WHh[:, c, :], bk, ACT.Copy, scale=0.5)
                    elif kind == "ahat":
                        act.wait_ge(ahat_tmp, c + 1)
                        i = act.activation(Ath[:, c, :], Th[:, c, :], ACT.Copy)
                    else:
                        continue
                    i.then_inc(prep_hi, 1)

            def gcn_step(st):
                if st.has(1):
                    b = st.b(1)
                    if st.from_(1, 2):
                        act.wait_ge(gcn_h, b - 1)
                    ln_apply(act, st, 1, 0, 2)
                if st.has(2):
                    b, r = st.b(2), st.ring(2, 2)
                    act.wait_ge(gcn_agg, b + 1)
                    if st.from_(2, 2):
                        act.wait_ge(gcn_z, b - 1)
                    act.activation(Gh[:, r, :], bank[r][:, :], ACT.Copy).then_inc(gcn_agg_hi, 1)
                if st.has(3):
                    b, r = st.b(3), st.ring(3, 2)
                    act.wait_ge(gcn_z_sum, b + 1)
                    if st.from_(3, 2):
                        act.wait_ge(gcn_y, b - 1)
                    act.activation(Zh[:, r, :], T1[:, r, :], ACT.Relu).then_inc(gcn_z_hi, 1)
                if st.has(4):
                    b, r = st.b(4), st.ring(4, 2)
                    act.wait_ge(gcn_y_sum, b + 1)
                    if st.from_(4, 2):
                        act.wait_ge(gcn_o, b - 1)
                    act.activation(Yh[:, r, :, :].rearrange("p a b -> p (a b)"), T2[:, r, :],
                                   ACT.Copy).then_inc(gcn_y_hi, 1)
                if st.has(5):
                    b = st.b(5)
                    act.wait_ge(gcn_o, b + 1)
                    act.activation(colb(Ch, b), bank[6][:, :], ACT.Relu).then_inc(gcn_o_hi, 1)
            pipeline(act, 6, 2, 5, gcn_step, lambda j: prepare(BEFORE_GCN if j == 0 else WITH_GCN.get(j, ())))

            act.wait_ge(gcn_o_split, NB)
            prepare(LSTM_WEIGHTS)

            def gates(p, r, s, k):
                q = SUB[p] + (r * p + s) * 2 + k
                order = [g for g in GATES if s > 0 or g != 1]
                base = GAT0[p] + r * 2 * (4 * p - 1) + (k * 3 if s == 0 else 6 + (s - 1) * 8 + k * 4)
                if not (p == 1 and isinstance(r, int) and r == 0):
                    act.wait_ge(h_full, q - 1)
                for n, g in enumerate(order):
                    act.wait_ge(gate_mm, base + n + 1)
                    i = act.activation(tile_view(TG[:, k, g, :], p), tile_view(bank[4 * k + g], p), ACT.Tanh,
                                       bias=lstm_bias[:, p - 1, g:g + 1], scale=1.0 if g == 2 else 0.5)
                    if n == len(order) - 2:
                        i.then_inc(cell_gates, 1)
                i.then_inc(all_gates, 1)

            def tanh_c(p, r, s, k):
                q = SUB[p] + (r * p + s) * 2 + k
                act.wait_ge(cell_new, q + 1)
                act.activation(tile_view(TC[:, k, :], p), tile_view(CC[:, k, :], p), ACT.Tanh,
                               scale=0.5).then_inc(cell_tanh, 1)

            def lstm_pair(p, r, following):
                for s in range(p):
                    for k in range(2):
                        if s + k > 0 or not begun(p, r):
                            gates(p, r, s, k)
                        if following and s == p - 1 and k == 1:
                            gates(*following, 0, 0)
                        if p > 1:
                            tanh_c(p, r, s, k)
                        elif k == 1:
                            tanh_c(p, r, 0, 0)
                            tanh_c(p, r, 0, 1)
            lstm_loop(act, lstm_pair)

            def pt_copy(st, lag, c, s, bk):
                b = st.b(lag)
                act.wait_ge(s["pt_mm"], 4 * b + c + 1)
                if c == 0 and st.from_(lag, 1):
                    act.wait_ge(s["ag_mm"], b)
                n = CH if s is gat else c + 1
                act.activation(PT[:, 0:n, c * P:(c + 1) * P],
                               bank[bk][:, 0:n * P].rearrange("p (a b) -> p a b", b=P), ACT.Copy).then_inc(s["pt_act"], 1)

            def exp_row(st, lag, c, s):
                b, r = st.b(lag), st.ring(lag, 2)
                w = T if s is gat else (c + 1) * P
                if c == 0:
                    act.wait_ge(s["bias"], b + 1)
                    if s is gat:
                        act.wait_ge(s["v"], 4 * b + 4)
                    if st.from_(lag, 2):
                        act.wait_ge(s["rden"], b - 1)
                act.activation(U[:, r, c, 0:w], U[:, r, c, 0:w], ACT.Exp, bias=soft_b[:, r, c:c + 1],
                               accum_out=den[:, r, c:c + 1]).then_inc(s["exp"], 1)

            def attended(st, lag, s):
                b = st.b(lag)
                act.wait_ge(s["ag_mm"], b + 1)
                if st.from_(lag, 1):
                    act.wait_ge(s["out_mm"], b)
                act.activation(AG, bank[7][:, :], ACT.Copy).then_inc(s["ag"], 1)

            def gat_step(st):
                def relu_part(c):
                    b = st.b(2)
                    if c == 0:
                        act.wait_ge(gat["s1_8"], b + 1)
                    act.wait_ge(gat["u"], 4 * b + c + 1)
                    if c >= 1 or st.from_(2, 1):
                        act.wait_ge(gat["v"], 4 * b + c)
                    act.activation(bank[6][:, :], U[:, st.ring(2, 2), c, :], ACT.Relu, bias=s1x[:, c:c + 1],
                                   scale=1.0 - SLOPE).then_inc(gat["relu"], 1)

                for c in range(CH):
                    if st.has(3):
                        exp_row(st, 3, c, gat)
                        if c == 3:
                            pt_copy(st, 3, 2, gat, 4)
                    if st.has(2):
                        relu_part(c)
                    if st.has(4) and c == 2:
                        attended(st, 4, gat)
                    if st.has(3) and c == 2:
                        pt_copy(st, 3, 0, gat, 4)
                    if st.has(1) and c == 0:
                        b = st.b(1)
                        act.wait_ge(gat["t2"], b + 1)
                        if st.from_(1, 1):
                            act.wait_ge(gat["proj"], b)
                        act.activation(NT, bank[1][:, :], ACT.Copy).then_inc(gat["nt"], 1)
                if st.has(0):
                    if st.from_(0, 4):
                        act.wait_ge(gat["ag_mm"], st.b(0) - 3)
                    ln_apply(act, st, 0, 1, 4)
            def l2_step(st):
                if st.has(1):
                    if st.from_(1, 2):
                        act.wait_ge(l2_split, st.b(1) - 1)
                    ln_apply(act, st, 1, 2, 2)
                if st.has(2):
                    b, r = st.b(2), st.ring(2, 2)
                    act.wait_ge(l2_agg, b + 1)
                    act.activation(colb(Ch, b), bank[r][:, :], ACT.Copy).then_inc(l2_agg_hi, 1)
            def gat_between(j):
                if j == 0:
                    prepare(A_HAT)
                for k in L2_EARLY.get(j, ()):
                    if k == 1:
                        act.wait_ge(gat["ag_mm"], NB - 2)
                    l2_step(Step(k, k))
            act.wait_ge(h_split, SUB[SKIP + 1])
            pipeline(act, 8, 4, 4, gat_step, gat_between)
            pipeline(act, 6, 2, 3, l2_step, first=6)

            def l2b_step(st):
                if st.has(0):
                    b, r = st.b(0), st.ring(0, 2)
                    act.wait_ge(l2_z2, b + 1)
                    if st.from_(0, 2):
                        act.wait_ge(l2_r_split, b - 1)
                    for h in range(HALVES):
                        i = act.activation(RZ[:, r, h, :], bank[2 * r + h][:, :], ACT.Relu, bias=bbi[:, h:h + 1],
                                           scale=bsc[:, h:h + 1])
                    i.then_inc(l2_relu, 1)
                if st.has(1):
                    b, r = st.b(1), st.ring(1, 2)
                    act.wait_ge(l2_o, b + 1)
                    act.activation(colb(Ch, b), bank[4 + r][:, :], ACT.Copy).then_inc(l2_o_hi, 1)
            act.wait_ge(bn_ready, 1)
            pipeline(act, 4, 2, 1, l2b_step)

            def att_step(st):
                if st.has(4):
                    for c in range(3):
                        exp_row(st, 4, c, att)
                if st.has(2):
                    b, r = st.b(2), st.ring(2, 2)
                    act.wait_ge(att["t2"], b + 1)
                    if st.from_(2, 2):
                        act.wait_ge(att["sc"], 4 * b - 4)
                    act.activation(NTh[:, r, :], bank[1][:, :], ACT.Copy).then_inc(att["nt_hi"], 1)
                if st.has(5):
                    attended(st, 5, att)
                if st.has(4):
                    pt_copy(st, 4, 0, att, 5)
                    exp_row(st, 4, 3, att)
                if st.has(2):
                    b, r = st.b(2), st.ring(2, 2)
                    act.wait_ge(att["proj"], b + 1)
                    act.activation(QTh[:, r, :], bank[2][:, :], ACT.Copy).then_inc(att["qt_hi"], 1)
                if st.has(0):
                    b = st.b(0)
                    act.wait_ge(att["bn_in"], b + 1)
                    if st.from_(0, 1):
                        act.wait_ge(att["t1"], b)
                    act.activation(HT, OS, ACT.Identity, bias=bbi[:, 2:3], scale=bsc[:, 2:3]).then_inc(att["col"], 1)
                if st.has(4):
                    pt_copy(st, 4, 2, att, 5)
                if st.has(1):
                    if st.from_(1, 4):
                        act.wait_ge(att["ag_mm"], st.b(1) - 3)
                    ln_apply(act, st, 1, 3, 4)
            act.wait_ge(l2_o_split, NB)
            act.activation(w_qkh, w_qk[:, :], ACT.Copy).then_inc(att["w_hi"], 1)
            act.wait_ge(bn_ready, 2)
            pipeline(act, 8, 4, 5, att_step)

        @block.vector
        def _(dve):
            n = [0]

            def then(i):
                n[0] += 1
                i.then_inc(dve_chain, 1)
                dve.wait_ge(dve_chain, n[0])

            hi = [2]

            def split_lo(dst, src, hi_ap, scale=None):
                hi[0] += 1
                dve.wait_ge(prep_hi, hi[0])
                h = hi_ap.bitcast(F32)
                if scale is None:
                    i = dve.tensor_tensor(dst, src, h, ALU.subtract)
                else:
                    i = dve.scalar_tensor_tensor(out=dst, in0=src, scalar=scale, in1=h, op0=ALU.mult, op1=ALU.subtract)
                return i

            def prepare_gcn():
                dve.wait_ge(prep_hi, 2)
                then(dve.tensor_tensor(gcn_wl[:, :, :], gcn_w32[:, :, :], gcn_wh[:, :, :].bitcast(F32), ALU.subtract))
                prepare(BEFORE_GCN)
                for c in range(CH):
                    i = dve.tensor_tensor(diag_blocks[:, c, :], A[:, c, c * P:(c + 1) * P], ident[:, :], ALU.mult)
                i.then_inc(diag_ready, 1)

            def prepare(groups):
                for g in groups:
                    kind, c = GROUPS[g]
                    bk = bank[BANKS[g]][:, :]
                    if kind not in ("adj", "bnw", "wih", "whh"):
                        dve.wait_ge(prep_mm, g + 1)
                    if kind == "vec":
                        then(dve.tensor_copy(V[:, 0:NVEC], bk[:, 0:NVEC]))
                        then(dve.tensor_copy(V[:, BHH_COL:BHH_COL + 16], bk[:, BHH_COL:BHH_COL + 16]))
                        lb = lstm_bias[:, :, :].rearrange("p a b -> p (a b)")
                        then(dve.tensor_tensor(lb, V[:, 0:16], V[:, BHH_COL:BHH_COL + 16], ALU.add))
                        for s in (slice(0, 2), slice(3, 4)):
                            then(dve.tensor_scalar(lstm_bias[:, :, s], lstm_bias[:, :, s], 0.5, None, ALU.mult))
                        i = dve.tensor_copy(s1[:, 0:1], V[:, 0:1])
                    elif kind == "adj":
                        i = split_lo(Atl[:, c, :], bk, Ath[:, c, :])
                    elif kind == "rowsum":
                        then(dve.tensor_copy(deg_rows, bk))
                        i = dve.tensor_scalar(bias_deg, deg_rows, V[:, COL["bg0"]:COL["bg0"] + 1], None, ALU.mult)
                    elif kind == "colsum":
                        i = dve.tensor_tensor(deg_t, bk, deg_rows, ALU.add)
                    elif kind == "diag":
                        dve.wait_ge(prep_done, g)
                        i = dve.scalar_tensor_tensor(out=deg_rows, in0=deg_t, scalar=1.0, in1=bk, op0=ALU.add,
                                                     op1=ALU.subtract)
                    elif kind == "bg1":
                        i = dve.tensor_copy(bg1_all[:, :], bk[:, 0:P])
                    elif kind == "tw":
                        i = dve.tensor_copy(tw.rearrange("p a b -> p (a b)"), bk)
                    elif kind == "bnw":
                        i = split_lo(bn_wl[:, :, :].rearrange("p a b -> p (a b)"), bk,
                                     bn_wh[:, :, :].rearrange("p a b -> p (a b)"))
                    elif kind == "fold":
                        then(dve.tensor_copy(gat_v[:, :], bk[:, 0:2]))
                        then(dve.tensor_scalar(gat_v2[:, :], ones[:, :], gat_v[:, 1:2], None, ALU.mult))
                        then(dve.tensor_scalar(w_qk[:, :], bk[:, P:2 * P], float(D) ** -0.5, None, ALU.mult))
                        i = dve.tensor_copy(w_vo[:, :], bk[:, 2 * P:3 * P])
                    elif kind == "deg":
                        dve.tensor_copy(deg[:, :], bk.rearrange("p (c q) -> p c q", q=P)[:, :, 0]).then_inc(deg_ready, 1)
                        i = dve.tensor_copy(s1[:, 0:1], ones[:, 0:1])
                    elif kind == "dinv":
                        i = dve.tensor_copy(dinv_all, bk)
                    elif kind == "ahat":
                        dve.scalar_tensor_tensor(out=Th[:, c, :], in0=bk, scalar=dinv[:, c:c + 1], in1=dinv_all,
                                                 op0=ALU.mult, op1=ALU.mult).then_inc(ahat_tmp, 1)
                        continue
                    elif kind == "wih":
                        i = split_lo(WXl[:, c, :], bk, WXh[:, c, :], 1.0 if c == 0 else 0.5)
                    else:
                        i = split_lo(WHl[:, c, :], bk, WHh[:, c, :], 0.5)
                    i.then_inc(prep_done, 1)

            def inverse_roots():
                dve.wait_ge(dinv_ready, 1)
                for c in range(CH):
                    i = dve.tensor_scalar(dinv_cols[:, c * P:(c + 1) * P], ones[:, :], dinv[:, c:c + 1], None, ALU.mult)
                i.then_inc(dinv_col, 1)

            def gcn_step(st):
                if st.has(0):
                    b, r = st.b(0), st.ring(0, 2)
                    if isinstance(st.j, int) and st.j == 0:
                        dve.wait_ge(in_x0, 16)
                    elif isinstance(st.j, int):
                        dve.wait_ge(in_x[st.j // 4], 64 if st.j >= 4 else 48)
                    else:
                        for q in range(1, 4):
                            dve.wait_ge(in_x[q], 64)
                    ln_stats(dve, st, 0, 0)
                if st.has(1):
                    b, r = st.b(1), st.ring(1, 2)
                    dve.wait_ge(ln_normed, b + 1)
                    if st.from_(1, 2):
                        dve.wait_ge(gcn_agg, b - 1)
                    dve.tensor_copy(Hh[:, r, :, :], N[:, r, :, :]).then_inc(gcn_hh, 1)
                    dve.wait_ge(gcn_hh, b + 1)
                    dve.tensor_tensor(Hl[:, r, :, :], N[:, r, :, :], Hh[:, r, :, :].bitcast(F32),
                                      ALU.subtract).then_inc(gcn_h, 1)
                if st.has(2):
                    b, r = st.b(2), st.ring(2, 2)
                    dve.wait_ge(gcn_agg_hi, b + 1)
                    dve.tensor_tensor(Gl[:, r, :], bank[r][:, :], Gh[:, r, :].bitcast(F32),
                                      ALU.subtract).then_inc(gcn_agg_split, 1)
                if st.has(3):
                    b, r = st.b(3), st.ring(3, 2)
                    dve.wait_ge(gcn_z, b + 1)
                    dve.tensor_tensor(T1[:, r, :], bank[2 + r][:, :], bias_deg, ALU.add).then_inc(gcn_z_sum, 1)
                if st.has(4):
                    b, r = st.b(4), st.ring(4, 2)
                    dve.wait_ge(gcn_y, b + 1)
                    dve.tensor_tensor(T2[:, r, :].rearrange("p (a b) -> p a b", b=P),
                                      bank[4 + r][:, :].rearrange("p (a b) -> p a b", b=P),
                                      bg1_all[:, None, :].to_broadcast([P, CH, P]), ALU.add).then_inc(gcn_y_sum, 1)
                if st.has(3):
                    b, r = st.b(3), st.ring(3, 2)
                    dve.wait_ge(gcn_z_hi, b + 1)
                    dve.scalar_tensor_tensor(out=Zl[:, r, :], in0=T1[:, r, :], scalar=0.0,
                                             in1=Zh[:, r, :].bitcast(F32), op0=ALU.max,
                                             op1=ALU.subtract).then_inc(gcn_z_split, 1)
                if st.has(4):
                    b, r = st.b(4), st.ring(4, 2)
                    dve.wait_ge(gcn_y_hi, b + 1)
                    dve.tensor_tensor(Yl[:, r, :, :].rearrange("p a b -> p (a b)"), T2[:, r, :],
                                      Yh[:, r, :, :].rearrange("p a b -> p (a b)").bitcast(F32),
                                      ALU.subtract).then_inc(gcn_y_split, 1)
                if st.has(5):
                    b = st.b(5)
                    dve.wait_ge(gcn_o_hi, b + 1)
                    dve.scalar_tensor_tensor(out=colb(Cl, b), in0=bank[6][:, :], scalar=0.0,
                                             in1=colb(Ch, b).bitcast(F32), op0=ALU.max,
                                             op1=ALU.subtract).then_inc(gcn_o_split, 1)
            def gcn_between(j):
                if j == 0:
                    prepare_gcn()
                prepare(WITH_GCN.get(j, ()))
                if j == NB + 2:
                    inverse_roots()
            pipeline(dve, 6, 2, 5, gcn_step, gcn_between)
            prepare(LSTM_WEIGHTS)

            def cell(p, r, s, k):
                q = SUB[p] + (r * p + s) * 2 + k
                ti, tg, tf = (tile_view(TG[:, k, g, :], p) for g in (0, 2, 1))
                cc = tile_view(CC[:, k, :], p)
                dve.wait_ge(cell_gates, q + 1)
                if s == 0:
                    dve.scalar_tensor_tensor(out=cc, in0=ti, scalar=1.0, in1=tg, op0=ALU.add,
                                             op1=ALU.mult).then_inc(cell_new, 1)
                    return
                ta, tb = tile_view(TA, p), tile_view(TB, p)
                dve.scalar_tensor_tensor(out=ta, in0=ti, scalar=1.0, in1=tg, op0=ALU.add, op1=ALU.mult)
                dve.scalar_tensor_tensor(out=tb, in0=tf, scalar=1.0, in1=cc, op0=ALU.add,
                                         op1=ALU.mult).then_inc(cell_parts, 1)
                dve.wait_ge(cell_parts, PARTS[p] + (r * (p - 1) + s - 1) * 2 + k + 1)
                dve.scalar_tensor_tensor(out=cc, in0=tb, scalar=0.5, in1=ta, op0=ALU.mult,
                                         op1=ALU.add).then_inc(cell_new, 1)

            def h_value(p, r, s, k):
                q = SUB[p] + (r * p + s) * 2 + k
                dve.wait_ge(all_gates, q + 1)
                dve.wait_ge(cell_tanh, q + 1)
                dve.scalar_tensor_tensor(out=tile_view(HF[:, k, :], p), in0=tile_view(TG[:, k, 3, :], p), scalar=1.0,
                                         in1=tile_view(TC[:, k, :], p), op0=ALU.add, op1=ALU.mult).then_inc(h_full, 1)

            def h_parts(p, r, s, k):
                if s < p - 1:
                    return tile_view(STh[:, k, :], p), tile_view(STl[:, k, :], p)
                return col_view(Ch, p, r, k, s), col_view(Cl, p, r, k, s)

            def h_high(p, r, s, k):
                dve.wait_ge(h_full, SUB[p] + (r * p + s) * 2 + k + 1)
                dve.tensor_copy(h_parts(p, r, s, k)[0], tile_view(HF[:, k, :], p)).then_inc(h_hi, 1)

            def h_low(p, r, s, k):
                dve.wait_ge(h_hi, SUB[p] + (r * p + s) * 2 + k + 1)
                dh, dl = h_parts(p, r, s, k)
                dve.tensor_tensor(dl, tile_view(HF[:, k, :], p), dh.bitcast(F32), ALU.subtract).then_inc(h_split, 1)

            def lstm_pair(p, r, following):
                for s in range(p):
                    for k in range(2):
                        if s + k > 0 or not begun(p, r):
                            cell(p, r, s, k)
                        if following and s == p - 1 and k == 1:
                            cell(*following, 0, 0)
                        if p > 1:
                            h_value(p, r, s, k)
                            h_high(p, r, s, k)
                            h_low(p, r, s, k)
                        elif k == 1:
                            for part in (h_value, h_high, h_low):
                                part(p, r, 0, 0)
                                part(p, r, 0, 1)
            PARTS = {1: 0}
            for p in range(1, SKIP + 1):
                PARTS[p + 1] = PARTS[p] + lstm_units(p)[2] * 2 * (p - 1)
            lstm_loop(dve, lstm_pair)

            def xb(b):
                return X[:, bass.ds(b, 1), :, :].rearrange("p o c d -> p (o c d)")

            def pt_copy(st, c, s, bk):
                b = st.b(3)
                dve.wait_ge(s["pt_mm"], 4 * b + c + 1)
                if c == 1 and st.from_(3, 1):
                    dve.wait_ge(s["ag_mm"], b)
                m = CH if s is gat else c + 1
                dve.tensor_copy(PT[:, 0:m, c * P:(c + 1) * P],
                                bank[bk + 1][:, 0:m * P].rearrange("p (a b) -> p a b", b=P)).then_inc(s["pt_dve"], 1)

            def inverse_sums(st, s):
                b, r = st.b(4), st.ring(4, 2)
                if st.from_(4, 1):
                    dve.wait_ge(s["final"], b)
                dve.reciprocal(rden[:, :], den[:, r, :]).then_inc(s["rden"], 1)

            def add_out(st, s):
                b = st.b(4)
                dve.wait_ge(s["rden"], b + 1)
                dve.wait_ge(s["out_mm"], b + 1)
                for c in range(CH):
                    xc = X[:, bass.ds(b, 1), c, :].rearrange("p o d -> p (o d)")
                    i = dve.scalar_tensor_tensor(out=xc, in0=bank[7][:, c * P:(c + 1) * P], scalar=rden[:, c:c + 1],
                                                 in1=xc, op0=ALU.mult, op1=ALU.add)
                i.then_inc(s["final"], 1)

            def gat_step(st):
                def u_row(c):
                    b, r = st.b(2), st.ring(2, 2)
                    dve.tensor_tensor_reduce(U[:, r, c, :], bank[2 + r][:, :], A[:, c, :], 1.0, NEG, ALU.add,
                                             ALU.max, top[:, c:c + 1]).then_inc(gat["u"], 1)

                def v_row(c):
                    b, r = st.b(2), st.ring(2, 2)
                    dve.wait_ge(gat["relu"], 4 * b + c + 1)
                    dve.scalar_tensor_tensor(out=U[:, r, c, :], in0=U[:, r, c, :], scalar=SLOPE, in1=bank[6][:, :],
                                             op0=ALU.mult, op1=ALU.add).then_inc(gat["v"], 1)

                if st.has(2):
                    b, r = st.b(2), st.ring(2, 2)
                    dve.wait_ge(gat["proj"], b + 1)
                    if st.from_(2, 2):
                        dve.wait_ge(gat["pt_mm"], 4 * b - 4)
                    if st.from_(2, 1):
                        dve.wait_ge(gat["bias"], b)
                    dve.tensor_copy(s1[:, :], bank[0][:, 0:CH]).then_inc(gat["s1"], 1)
                    u_row(0)
                    dve.wait_ge(gat["s1"], b + 1)
                    dve.tensor_scalar(s1x[:, :], s1[:, :], 1.0 - SLOPE, None, ALU.mult).then_inc(gat["s1_8"], 1)
                    u_row(1)
                    v_row(0)
                if st.has(0):
                    b = st.b(0)
                    dve.wait_ge(gat["t1"], b + 1)
                    dve.scalar_tensor_tensor(out=xb(b), in0=bank[0][:, :], scalar=0.5, in1=xb(b), op0=ALU.mult,
                                             op1=ALU.add).then_inc(gat["x_new"], 1)
                if st.has(2):
                    apart(dve)
                    u_row(2)
                    v_row(1)
                if st.has(4):
                    inverse_sums(st, gat)
                if st.has(0):
                    dve.wait_ge(gat["x_new"], st.b(0) + 1)
                    ln_stats(dve, st, 0, 1)
                if st.has(2):
                    apart(dve)
                    u_row(3)
                    v_row(2)
                    b = st.b(2)
                    dve.wait_ge(gat["u"], 4 * b + 4)
                    dve.tensor_tensor(e_top[:, :], top[:, :], s1[:, :], ALU.add).then_inc(gat["e_top"], 1)
                if st.has(3):
                    pt_copy(st, 1, gat, 4)
                if st.has(2):
                    dve.wait_ge(gat["e_top"], b + 1)
                    dve.scalar_tensor_tensor(out=l_top[:, :], in0=e_top[:, :], scalar=SLOPE, in1=e_top[:, :],
                                             op0=ALU.mult, op1=ALU.max).then_inc(gat["l_top"], 1)
                if st.has(4):
                    add_out(st, gat)
                if st.has(2):
                    b, r = st.b(2), st.ring(2, 2)
                    dve.wait_ge(gat["l_top"], b + 1)
                    dve.scalar_tensor_tensor(out=soft_b[:, r, :], in0=s1[:, :], scalar=SLOPE, in1=l_top[:, :],
                                             op0=ALU.mult, op1=ALU.subtract).then_inc(gat["bias"], 1)
                if st.has(3):
                    pt_copy(st, 3, gat, 4)
                if st.has(2):
                    v_row(3)
            dve.wait_ge(h_split, SUB[SKIP + 1])
            for c in range(CH):
                i = dve.tensor_tensor(loops[:, c, :], A[:, c, c * P:(c + 1) * P], ident[:, :], ALU.add)
            i.then_inc(diag_ready, 1)

            def l2_step(st):
                if st.has(0):
                    if isinstance(st.j, int) and st.j < NB:
                        dve.wait_ge(gat["final"], st.j + 1)
                    ln_stats(dve, st, 0, 2)
                if st.has(1):
                    b, r = st.b(1), st.ring(1, 2)
                    dve.wait_ge(ln_normed, 2 * NB + b + 1)
                    if st.from_(1, 2):
                        dve.wait_ge(l2_agg, b - 1)
                    dve.tensor_copy(Nh[:, r, :, :], N[:, r, :, :]).then_inc(l2_hi, 1)
                    dve.wait_ge(l2_hi, b + 1)
                    dve.tensor_tensor(Nl[:, r, :, :], N[:, r, :, :], Nh[:, r, :, :].bitcast(F32),
                                      ALU.subtract).then_inc(l2_split, 1)
                if st.has(2):
                    b, r = st.b(2), st.ring(2, 2)
                    dve.wait_ge(l2_agg_hi, b + 1)
                    dve.tensor_tensor(colb(Cl, b), bank[r][:, :], colb(Ch, b).bitcast(F32),
                                      ALU.subtract).then_inc(l2_agg_split, 1)
                if st.has(3):
                    b, r = st.b(3), st.ring(3, 2)
                    dve.wait_ge(l2_z, b + 1)
                    apart(dve)
                    for h in range(HALVES):
                        i = dve.bn_stats(bst1[:, h, bass.ds(b, 1), :].rearrange("p o s -> p (o s)"),
                                         bank[2 + 2 * r + h][:, :])
                    i.then_inc(l2_zstats, 1)
            def gat_between(j):
                if j == 0:
                    prepare(A_HAT)
                if j == 1:
                    for g in A_HAT:
                        c = GROUPS[g][1]
                        split_lo(Atl[:, c, :], Th[:, c, :], Ath[:, c, :]).then_inc(prep_done, 1)
                    dve.tensor_scalar(A[:, :, :], A[:, :, :], 0.0, NEG, ALU.is_equal,
                                      ALU.mult).then_inc(mask_ready, 1)
                    dve.wait_ge(mask_ready, 1)
                for k in L2_EARLY.get(j, ()):
                    l2_step(Step(k, k))
            pipeline(dve, 8, 4, 4, gat_step, gat_between)

            dve.wait_ge(gat["final"], NB)
            pipeline(dve, 6, 2, 3, l2_step, first=6)

            def bn_params(lo, hi_, gain, beta, bias, k):
                w = slice(lo, hi_)
                then(dve.tensor_scalar(bve[:, w], bmv[:, w, 1], 1.0, EPS, ALU.mult, ALU.add))
                then(dve.tensor_tensor(bmb[:, w], bmv[:, w, 0], bias, ALU.add))
                dve.tensor_tensor(bsh[:, w], bias, bmb[:, w], ALU.subtract).then_inc(bn_var, 1)
                dve.wait_ge(bn_var, k)
                dve.wait_ge(bn_rs, k)
                then(dve.tensor_tensor(bsc[:, w], brs[:, w], gain, ALU.mult))
                then(dve.tensor_tensor(bms[:, w], bsh[:, w], bsc[:, w], ALU.mult))
                dve.tensor_tensor(bbi[:, w], bms[:, w], beta, ALU.add).then_inc(bn_ready, 1)

            dve.wait_ge(l2_zstats, NB)
            for h in range(HALVES):
                then(dve.bn_aggr(bmv[:, h, :], bst1[:, h, :, :].rearrange("p b s -> p (b s)")))
            bn_params(0, 2, V[:, COL["g1"]:COL["g1"] + 2], V[:, COL["be1"]:COL["be1"] + 2],
                      V[:, COL["b1"]:COL["b1"] + 2], 1)

            def l2b_step(st):
                if st.has(0):
                    b, r = st.b(0), st.ring(0, 2)
                    dve.wait_ge(l2_relu, b + 1)
                    if st.from_(0, 2):
                        dve.wait_ge(l2_o, b - 1)
                    dve.tensor_copy(Rh[:, r, :, :], RZ[:, r, :, :]).then_inc(l2_r_hi, 1)
                    dve.wait_ge(l2_r_hi, b + 1)
                    dve.tensor_tensor(Rl[:, r, :, :], RZ[:, r, :, :], Rh[:, r, :, :].bitcast(F32),
                                      ALU.subtract).then_inc(l2_r_split, 1)
                if st.has(1):
                    b, r = st.b(1), st.ring(1, 2)
                    dve.wait_ge(l2_o_hi, b + 1)
                    apart(dve)
                    dve.bn_stats(bst2[:, bass.ds(b, 1), :].rearrange("p o s -> p (o s)"),
                                 bank[4 + r][:, :]).then_inc(l2_o_stats, 1)
                    dve.tensor_tensor(colb(Cl, b), bank[4 + r][:, :], colb(Ch, b).bitcast(F32),
                                      ALU.subtract).then_inc(l2_o_split, 1)
            pipeline(dve, 4, 2, 1, l2b_step)
            dve.wait_ge(l2_o_stats, NB)
            then(dve.bn_aggr(bmv[:, 2, :], bst2[:, :, :].rearrange("p b s -> p (b s)")))
            bn_params(2, 3, V[:, COL["g2"]:COL["g2"] + 1], V[:, COL["be2"]:COL["be2"] + 1],
                      V[:, COL["b2"]:COL["b2"] + 1], 2)

            def att_step(st):
                def u_row(c):
                    b, r = st.b(2), st.ring(2, 2)
                    w = (c + 1) * P
                    dve.wait_ge(att["sc"], 4 * b + c + 1)
                    if c == 0 and st.from_(2, 2):
                        dve.wait_ge(att["pt_mm"], 4 * b - 4)
                    if c == 0 and st.from_(2, 1):
                        dve.wait_ge(att["bias"], b)
                    apart(dve)
                    dve.tensor_tensor_reduce(U[:, r, c, 0:w], bank[3 + c % 2][:, 0:w], A[:, c, 0:w], 1.0, NEG,
                                             ALU.add, ALU.max, top[:, c:c + 1]).then_inc(att["u"], 1)

                def low(dst, bk, high):
                    return dve.tensor_tensor(dst, bank[bk][:, :], high.bitcast(F32), ALU.subtract)

                if st.has(0):
                    b = st.b(0)
                    dve.wait_ge(att["t1"], b + 1)
                    dve.tensor_tensor(xb(b), bank[0][:, :], xb(b), ALU.add).then_inc(att["x_new"], 1)
                    dve.wait_ge(att["x_new"], b + 1)
                    ln_stats(dve, st, 0, 3)
                if st.has(2):
                    u_row(0)
                    u_row(1)
                if st.has(1):
                    b, r = st.b(1), st.ring(1, 2)
                    dve.wait_ge(att["nt_hi"], b + 1)
                    low(NTl[:, r, :], 1, NTh[:, r, :]).then_inc(att["nt"], 1)
                if st.has(3):
                    pt_copy(st, 1, att, 5)
                if st.has(4):
                    inverse_sums(st, att)
                if st.has(2):
                    u_row(2)
                    u_row(3)
                    b, r = st.b(2), st.ring(2, 2)
                    dve.wait_ge(att["u"], 4 * b + 4)
                    if st.from_(2, 2):
                        dve.wait_ge(att["exp"], 4 * b - 4)
                    dve.tensor_scalar(soft_b[:, r, :], top[:, :], -1.0, None, ALU.mult).then_inc(att["bias"], 1)
                if st.has(4):
                    add_out(st, att)
                if st.has(1):
                    b, r = st.b(1), st.ring(1, 2)
                    dve.wait_ge(att["qt_hi"], b + 1)
                    low(QTl[:, r, :], 2, QTh[:, r, :]).then_inc(att["qt"], 1)
                if st.has(3):
                    pt_copy(st, 3, att, 5)
            dve.wait_ge(att["w_hi"], 1)
            dve.tensor_tensor(w_qkl, w_qk[:, :], w_qkh.bitcast(F32), ALU.subtract).then_inc(att["w_split"], 1)
            dve.wait_ge(causal_ready, CH)
            pipeline(dve, 8, 4, 4, att_step)


INPUTS = ["x", "adj", "L0_gnn_Wg0", "L0_gnn_bg0", "L0_gnn_Wg1", "L0_gnn_bg1", "L0_gnn_Wih", "L0_gnn_Whh",
          "L0_gnn_bih", "L0_gnn_bhh", "L1_gnn_W", "L1_gnn_a", "L2_gnn_W1", "L2_gnn_b1", "L2_gnn_g1", "L2_gnn_be1",
          "L2_gnn_W2", "L2_gnn_b2", "L2_gnn_g2", "L2_gnn_be2", "L3_gnn_Wqkv", "L3_gnn_Wo"]


def kernel(**inputs):
    import numpy as np
    import concourse.bacc as bacc
    from concourse.bass_utils import run_bass_kernel_spmd

    nc = bacc.Bacc("TRN2", target_bir_lowering=False, num_devices=1)
    arrays, args = {}, []
    for name in INPUTS:
        a = np.ascontiguousarray(inputs[name])
        arrays[f"in_{name}"] = a
        args.append(nc.dram_tensor(f"in_{name}", a.shape, mybir.dt.from_np(a.dtype), kind="ExternalInput").ap())
    args.append(nc.dram_tensor("out_x", (NB, T, D), F32, kind="ExternalOutput").ap())
    program(nc, *args)
    r = run_bass_kernel_spmd(nc, [arrays], core_ids=[0])
    return r.results[0]["out_x"]
```
